# Optimizing a Trainium2 kernel written in Bass

```python
import numpy as np
import jax
import jax.numpy as jnp

def _softmax(x, axis=-1):
    return jax.nn.softmax(x, axis=axis)

def _gelu(x):
    return jax.nn.gelu(x, approximate=True)

def _silu(x):
    return jax.nn.silu(x)

def _sigmoid(x):
    return jax.nn.sigmoid(x)

def _layernorm(x, axis=-1, eps=1e-05):
    m = jnp.mean(x, axis=axis, keepdims=True)
    v = jnp.var(x, axis=axis, keepdims=True)
    return (x - m) / jnp.sqrt(v + eps)

def _scatter_add(tgt, idx, src, axis=0):
    return tgt.at[idx].add(src)

def _segment_sum(src, seg, n):
    return jax.ops.segment_sum(src, seg, n)
kernel_name = 'mk_vit_tower_d2_tok_img256_r4_02c3ab'

def setup_inputs(seed: int=0):
    np.random.seed(seed)
    _w = jnp.asarray

    def _rec_inputs():
        import jax
        import jax.numpy as jnp
        _rk = jax.random.key(seed)
        x = -4.65018e-05 + 0.999886 * jax.random.normal(jax.random.fold_in(_rk, 1), (64, 3, 128, 128), jnp.float32)
        return x
    x = _rec_inputs()

    def _L0_tok_setup():
        import jax, jax.numpy as jnp
        import numpy as np
        B, C, H, P, D = (64, 3, 128, 16, 64)
        NP = H // P
        key = jax.random.key(seed)
        ks = jax.random.split(key, 7)
        s = lambda fan_in: 1.0 / np.sqrt(fan_in)
        return {'x': jax.random.normal(ks[0], (B, C, H, H), dtype=jnp.float32), 'Wp': jax.random.normal(ks[1], (P * P * C, D), dtype=jnp.float32) * s(P * P * C), 'bp': jax.random.normal(ks[2], (D,), dtype=jnp.float32) * 0.01, 'W1': jax.random.normal(ks[3], (2, D), dtype=jnp.float32) * s(2), 'b1': jax.random.normal(ks[4], (D,), dtype=jnp.float32) * 0.01, 'W2': jax.random.normal(ks[5], (D, D), dtype=jnp.float32) * s(D), 'b2': jax.random.normal(ks[6], (D,), dtype=jnp.float32) * 0.01}
    _L0_tok_all = _L0_tok_setup()
    _L0_tok_in = {k: v for k, v in _L0_tok_all.items() if k in ('Wp', 'bp', 'W1', 'b1', 'W2', 'b2')}
    del _L0_tok_all

    def _L0_attn_setup():
        import jax, jax.numpy as jnp
        import numpy as np
        HEADS = 8
        EPS = 1e-05

        def _ln(t, w, b, headc):
            m = jnp.mean(t, axis=-1, keepdims=True)
            d = t - m
            std = jnp.sqrt(jnp.sum(d * d, axis=-1, keepdims=True) / (headc - 1))
            return w * (d / (std + EPS)) + b
        key = jax.random.key(seed)
        B, N, C = (32, 1024, 64)
        headc = C // HEADS
        x = jax.random.normal(key, (B, N, C), dtype=jnp.float32)
        return {'x': x, 'kln_weight': jnp.ones((HEADS, 1, headc), dtype=jnp.float32), 'kln_bias': jnp.zeros((HEADS, 1, headc), dtype=jnp.float32), 'vln_weight': jnp.ones((HEADS, 1, headc), dtype=jnp.float32), 'vln_bias': jnp.zeros((HEADS, 1, headc), dtype=jnp.float32)}
    _L0_attn_all = _L0_attn_setup()
    _L0_attn_in = {k: v for k, v in _L0_attn_all.items() if k in ('kln_weight', 'kln_bias', 'vln_weight', 'vln_bias')}
    del _L0_attn_all

    def _L0_ffn_setup():
        import jax, jax.numpy as jnp
        import numpy as np
        B, N, D = (16, 1024, 64)
        NUM_EXPERTS, TOP_K, HEADS = (4, 2, 4)
        N_EDGES = 262144
        LN_EPS = 1e-05

        def _layernorm(x, g, b):
            mu = x.mean(-1, keepdims=True)
            var = ((x - mu) ** 2).mean(-1, keepdims=True)
            return (x - mu) * jax.lax.rsqrt(var + LN_EPS) * g + b

        def _forward(x, edge_index, W_gat, att_src, att_dst, b_gat, ln_gamma, ln_beta, W1, b1, W2, b2):
            Bc, Nc, Dc = x.shape
            M = Bc * Nc
            x_flat = x.reshape(M, Dc)
            h = (x_flat @ W_gat).reshape(M, HEADS, NUM_EXPERTS)
            loops = jnp.arange(M, dtype=edge_index.dtype)
            src = jnp.concatenate([edge_index[0], loops])
            dst = jnp.concatenate([edge_index[1], loops])
            a_src = (h * att_src).sum(-1)
            a_dst = (h * att_dst).sum(-1)
            e = jax.nn.leaky_relu(a_src[src] + a_dst[dst], negative_slope=0.2)
            e_max = jax.ops.segment_max(e, dst, num_segments=M)
            ee = jnp.exp(e - e_max[dst])
            denom = jax.ops.segment_sum(ee, dst, num_segments=M)
            alpha = ee / (denom[dst] + 1e-16)
            msg = h[src] * alpha[:, :, None]
            agg = jax.ops.segment_sum(msg, dst, num_segments=M).reshape(M, HEADS * NUM_EXPERTS) + b_gat
            scores = _layernorm(agg, ln_gamma, ln_beta).reshape(M, HEADS, NUM_EXPERTS).mean(1)
            scores = scores.reshape(Bc, Nc, NUM_EXPERTS)
            topk_s, topk_i = jax.lax.top_k(scores, TOP_K)
            w = jax.nn.softmax(topk_s, axis=-1)
            out = jnp.zeros_like(x)
            for ei in range(NUM_EXPERTS):
                g = jnp.where(topk_i == ei, w, 0.0).sum(-1)
                hh = jax.nn.gelu(x @ W1[ei] + b1[ei], approximate=False)
                out = out + g[..., None] * (hh @ W2[ei] + b2[ei])
            return out
        key = jax.random.key(seed)
        ks = jax.random.split(key, 8)
        s = 0.05
        return {'x': jax.random.normal(ks[0], (B, N, D), jnp.float32), 'W_gat': jax.random.normal(ks[1], (D, HEADS * NUM_EXPERTS), jnp.float32) * s, 'att_src': jax.random.normal(ks[2], (HEADS, NUM_EXPERTS), jnp.float32) * s, 'att_dst': jax.random.normal(ks[3], (HEADS, NUM_EXPERTS), jnp.float32) * s, 'b_gat': jnp.zeros((HEADS * NUM_EXPERTS,), jnp.float32), 'ln_gamma': jnp.ones((HEADS * NUM_EXPERTS,), jnp.float32), 'ln_beta': jnp.zeros((HEADS * NUM_EXPERTS,), jnp.float32), 'W1': jax.random.normal(ks[4], (NUM_EXPERTS, D, 2 * D), jnp.float32) * s, 'b1': jnp.zeros((NUM_EXPERTS, 2 * D), jnp.float32), 'W2': jax.random.normal(ks[5], (NUM_EXPERTS, 2 * D, D), jnp.float32) * s, 'b2': jnp.zeros((NUM_EXPERTS, D), jnp.float32), 'edge_index': jax.random.randint(ks[6], (2, N_EDGES), 0, B * N, jnp.int32)}
    _L0_ffn_all = _L0_ffn_setup()
    _L0_ffn_in = {k: v for k, v in _L0_ffn_all.items() if k in ('W_gat', 'att_src', 'att_dst', 'b_gat', 'ln_gamma', 'ln_beta', 'W1', 'b1', 'W2', 'b2', 'edge_index')}
    del _L0_ffn_all

    def _L1_attn_setup():
        import math
        import jax, jax.numpy as jnp
        import numpy as np
        D_MODEL = 64
        N_HEADS = 4
        HEAD_DIM = D_MODEL // N_HEADS
        MAX_REL = 30

        def _rel_pos_encodings(t, d_model):
            n = 2 * MAX_REL + 1
            positions = jnp.arange(n, dtype=jnp.float32)[:, None]
            div_term = jnp.exp(jnp.arange(0, d_model, 2, dtype=jnp.float32) * (-math.log(10000.0) / d_model))
            ang = positions * div_term
            enc = jnp.stack([jnp.sin(ang), jnp.cos(ang)], axis=-1).reshape(n, d_model)
            rng = jnp.arange(t)
            final_mat = jnp.clip(rng[None, :] - rng[:, None], -MAX_REL, MAX_REL) + MAX_REL
            return enc[final_mat]
        key = jax.random.key(seed)
        ks = jax.random.split(key, 12)
        d = D_MODEL
        s = 1.0 / math.sqrt(d)
        inp = {'inputs': jax.random.normal(ks[0], (16, 128, d), dtype=jnp.float32), 'ln_gamma': jnp.ones((d,), jnp.float32), 'ln_beta': jnp.zeros((d,), jnp.float32), 'Wq': jax.random.normal(ks[1], (d, d), jnp.float32) * s, 'bq': jnp.zeros((d,), jnp.float32), 'Wk': jax.random.normal(ks[2], (d, d), jnp.float32) * s, 'bk': jnp.zeros((d,), jnp.float32), 'Wv': jax.random.normal(ks[3], (d, d), jnp.float32) * s, 'bv': jnp.zeros((d,), jnp.float32), 'Wpos': jax.random.normal(ks[4], (d, d), jnp.float32) * s, 'bpos': jnp.zeros((d,), jnp.float32), 'Wo': jax.random.normal(ks[5], (d, d), jnp.float32) * s, 'bo': jnp.zeros((d,), jnp.float32), 'u_bias': jax.random.normal(ks[6], (1, N_HEADS, 1, HEAD_DIM), jnp.float32) * 0.02, 'v_bias': jax.random.normal(ks[7], (1, N_HEADS, 1, HEAD_DIM), jnp.float32) * 0.02}
        return inp
    _L1_attn_all = _L1_attn_setup()
    _L1_attn_in = {k: v for k, v in _L1_attn_all.items() if k in ('ln_gamma', 'ln_beta', 'Wq', 'bq', 'Wk', 'bk', 'Wv', 'bv', 'Wpos', 'bpos', 'Wo', 'bo', 'u_bias', 'v_bias')}
    del _L1_attn_all

    def _L1_ffn_setup():
        import jax, jax.numpy as jnp
        import numpy as np
        TOP_K = 2
        key = jax.random.key(seed)
        ks = jax.random.split(key, 4)
        B, L, D, H, E = (8, 1024, 64, 256, 8)
        s = 0.02
        return {'x': jax.random.normal(ks[0], (B, L, D), jnp.float32), 'Wg': jax.random.normal(ks[1], (D, E), jnp.float32) * s, 'bg': jnp.zeros((E,), jnp.float32), 'W1': jax.random.normal(ks[2], (E, D, H), jnp.float32) * s, 'b1': jnp.zeros((E, H), jnp.float32), 'W2': jax.random.normal(ks[3], (E, H, D), jnp.float32) * s, 'b2': jnp.zeros((E, D), jnp.float32)}
    _L1_ffn_all = _L1_ffn_setup()
    _L1_ffn_in = {k: v for k, v in _L1_ffn_all.items() if k in ('Wg', 'bg', 'W1', 'b1', 'W2', 'b2')}
    del _L1_ffn_all
    return {'x': x, 'L0_tok_Wp': _L0_tok_in['Wp'], 'L0_tok_bp': _L0_tok_in['bp'], 'L0_tok_W1': _L0_tok_in['W1'], 'L0_tok_b1': _L0_tok_in['b1'], 'L0_tok_W2': _L0_tok_in['W2'], 'L0_tok_b2': _L0_tok_in['b2'], 'L0_attn_kln_weight': _L0_attn_in['kln_weight'], 'L0_attn_kln_bias': _L0_attn_in['kln_bias'], 'L0_attn_vln_weight': _L0_attn_in['vln_weight'], 'L0_attn_vln_bias': _L0_attn_in['vln_bias'], 'L0_ffn_W_gat': _L0_ffn_in['W_gat'], 'L0_ffn_att_src': _L0_ffn_in['att_src'], 'L0_ffn_att_dst': _L0_ffn_in['att_dst'], 'L0_ffn_b_gat': _L0_ffn_in['b_gat'], 'L0_ffn_ln_gamma': _L0_ffn_in['ln_gamma'], 'L0_ffn_ln_beta': _L0_ffn_in['ln_beta'], 'L0_ffn_W1': _L0_ffn_in['W1'], 'L0_ffn_b1': _L0_ffn_in['b1'], 'L0_ffn_W2': _L0_ffn_in['W2'], 'L0_ffn_b2': _L0_ffn_in['b2'], 'L0_ffn_edge_index': _L0_ffn_in['edge_index'], 'L1_attn_ln_gamma': _L1_attn_in['ln_gamma'], 'L1_attn_ln_beta': _L1_attn_in['ln_beta'], 'L1_attn_Wq': _L1_attn_in['Wq'], 'L1_attn_bq': _L1_attn_in['bq'], 'L1_attn_Wk': _L1_attn_in['Wk'], 'L1_attn_bk': _L1_attn_in['bk'], 'L1_attn_Wv': _L1_attn_in['Wv'], 'L1_attn_bv': _L1_attn_in['bv'], 'L1_attn_Wpos': _L1_attn_in['Wpos'], 'L1_attn_bpos': _L1_attn_in['bpos'], 'L1_attn_Wo': _L1_attn_in['Wo'], 'L1_attn_bo': _L1_attn_in['bo'], 'L1_attn_u_bias': _L1_attn_in['u_bias'], 'L1_attn_v_bias': _L1_attn_in['v_bias'], 'L1_ffn_Wg': _L1_ffn_in['Wg'], 'L1_ffn_bg': _L1_ffn_in['bg'], 'L1_ffn_W1': _L1_ffn_in['W1'], 'L1_ffn_b1': _L1_ffn_in['b1'], 'L1_ffn_W2': _L1_ffn_in['W2'], 'L1_ffn_b2': _L1_ffn_in['b2']}

def reference(x, L0_tok_Wp, L0_tok_bp, L0_tok_W1, L0_tok_b1, L0_tok_W2, L0_tok_b2, L0_attn_kln_weight, L0_attn_kln_bias, L0_attn_vln_weight, L0_attn_vln_bias, L0_ffn_W_gat, L0_ffn_att_src, L0_ffn_att_dst, L0_ffn_b_gat, L0_ffn_ln_gamma, L0_ffn_ln_beta, L0_ffn_W1, L0_ffn_b1, L0_ffn_W2, L0_ffn_b2, L0_ffn_edge_index, L1_attn_ln_gamma, L1_attn_ln_beta, L1_attn_Wq, L1_attn_bq, L1_attn_Wk, L1_attn_bk, L1_attn_Wv, L1_attn_bv, L1_attn_Wpos, L1_attn_bpos, L1_attn_Wo, L1_attn_bo, L1_attn_u_bias, L1_attn_v_bias, L1_ffn_Wg, L1_ffn_bg, L1_ffn_W1, L1_ffn_b1, L1_ffn_W2, L1_ffn_b2):
    import jax
    import jax.numpy as jnp

    def _L0_tok_ref(x, Wp, bp, W1, b1, W2, b2):
        import jax, jax.numpy as jnp
        import numpy as np
        B, C, H, P, D = (64, 3, 128, 16, 64)
        NP = H // P
        b = x.shape[0]
        patches = x.reshape(b, C, NP, P, NP, P)
        patches = patches.transpose(0, 2, 4, 1, 3, 5).reshape(b, NP * NP, C * P * P)
        embedded = jnp.einsum('bnk,kd->bnd', patches, Wp) + bp
        gx, gy = jnp.meshgrid(jnp.arange(NP, dtype=jnp.float32), jnp.arange(NP, dtype=jnp.float32), indexing='ij')
        xy = jnp.stack([gx, gy], axis=-1).reshape(1, -1, 2) / (NP - 1)
        pos = jax.nn.relu(xy @ W1 + b1) @ W2 + b2
        return embedded + pos

    def _L0_attn_ref(x, kln_weight, kln_bias, vln_weight, vln_bias):
        import jax, jax.numpy as jnp
        import numpy as np
        HEADS = 8
        EPS = 1e-05

        def _ln(t, w, b, headc):
            m = jnp.mean(t, axis=-1, keepdims=True)
            d = t - m
            std = jnp.sqrt(jnp.sum(d * d, axis=-1, keepdims=True) / (headc - 1))
            return w * (d / (std + EPS)) + b
        B, N, C = x.shape
        headc = C // HEADS
        qkv = x.reshape(B, N, HEADS, headc).transpose(0, 2, 1, 3)
        k = _ln(qkv, kln_weight, kln_bias, headc)
        v = _ln(qkv, vln_weight, vln_bias, headc)
        kv = jnp.einsum('bhnd,bhne->bhde', k, v) / N
        out = jnp.einsum('bhnd,bhde->bhne', qkv, kv)
        out = out.transpose(0, 2, 1, 3).reshape(B, N, C)
        return out + x

    def _L0_ffn_ref(x, W_gat, att_src, att_dst, b_gat, ln_gamma, ln_beta, W1, b1, W2, b2, edge_index):
        import jax, jax.numpy as jnp
        import numpy as np
        B, N, D = (16, 1024, 64)
        NUM_EXPERTS, TOP_K, HEADS = (4, 2, 4)
        N_EDGES = 262144
        LN_EPS = 1e-05

        def _layernorm(x, g, b):
            mu = x.mean(-1, keepdims=True)
            var = ((x - mu) ** 2).mean(-1, keepdims=True)
            return (x - mu) * jax.lax.rsqrt(var + LN_EPS) * g + b

        def _forward(x, edge_index, W_gat, att_src, att_dst, b_gat, ln_gamma, ln_beta, W1, b1, W2, b2):
            Bc, Nc, Dc = x.shape
            M = Bc * Nc
            x_flat = x.reshape(M, Dc)
            h = (x_flat @ W_gat).reshape(M, HEADS, NUM_EXPERTS)
            loops = jnp.arange(M, dtype=edge_index.dtype)
            src = jnp.concatenate([edge_index[0], loops])
            dst = jnp.concatenate([edge_index[1], loops])
            a_src = (h * att_src).sum(-1)
            a_dst = (h * att_dst).sum(-1)
            e = jax.nn.leaky_relu(a_src[src] + a_dst[dst], negative_slope=0.2)
            e_max = jax.ops.segment_max(e, dst, num_segments=M)
            ee = jnp.exp(e - e_max[dst])
            denom = jax.ops.segment_sum(ee, dst, num_segments=M)
            alpha = ee / (denom[dst] + 1e-16)
            msg = h[src] * alpha[:, :, None]
            agg = jax.ops.segment_sum(msg, dst, num_segments=M).reshape(M, HEADS * NUM_EXPERTS) + b_gat
            scores = _layernorm(agg, ln_gamma, ln_beta).reshape(M, HEADS, NUM_EXPERTS).mean(1)
            scores = scores.reshape(Bc, Nc, NUM_EXPERTS)
            topk_s, topk_i = jax.lax.top_k(scores, TOP_K)
            w = jax.nn.softmax(topk_s, axis=-1)
            out = jnp.zeros_like(x)
            for ei in range(NUM_EXPERTS):
                g = jnp.where(topk_i == ei, w, 0.0).sum(-1)
                hh = jax.nn.gelu(x @ W1[ei] + b1[ei], approximate=False)
                out = out + g[..., None] * (hh @ W2[ei] + b2[ei])
            return out
        return _forward(x, edge_index, W_gat, att_src, att_dst, b_gat, ln_gamma, ln_beta, W1, b1, W2, b2)

    def _L1_attn_ref(inputs, ln_gamma, ln_beta, Wq, bq, Wk, bk, Wv, bv, Wpos, bpos, Wo, bo, u_bias, v_bias):
        import math
        import jax, jax.numpy as jnp
        import numpy as np
        D_MODEL = 64
        N_HEADS = 4
        HEAD_DIM = D_MODEL // N_HEADS
        MAX_REL = 30

        def _rel_pos_encodings(t, d_model):
            n = 2 * MAX_REL + 1
            positions = jnp.arange(n, dtype=jnp.float32)[:, None]
            div_term = jnp.exp(jnp.arange(0, d_model, 2, dtype=jnp.float32) * (-math.log(10000.0) / d_model))
            ang = positions * div_term
            enc = jnp.stack([jnp.sin(ang), jnp.cos(ang)], axis=-1).reshape(n, d_model)
            rng = jnp.arange(t)
            final_mat = jnp.clip(rng[None, :] - rng[:, None], -MAX_REL, MAX_REL) + MAX_REL
            return enc[final_mat]
        b, t, d = inputs.shape
        h, hd = (N_HEADS, HEAD_DIM)
        mu = jnp.mean(inputs, axis=-1, keepdims=True)
        var = jnp.mean(jnp.square(inputs - mu), axis=-1, keepdims=True)
        x = (inputs - mu) * jax.lax.rsqrt(var + 1e-05) * ln_gamma + ln_beta

        def split_heads(y):
            return y.reshape(b, t, h, hd).transpose(0, 2, 1, 3)
        q = split_heads(x @ Wq.T + bq)
        k = split_heads(x @ Wk.T + bk)
        v = split_heads(x @ Wv.T + bv)
        rel = jax.lax.stop_gradient(_rel_pos_encodings(t, d))
        pos = (rel @ Wpos.T + bpos).reshape(t, t, h, hd)
        qk_score = jnp.einsum('bhtd,bhsd->bhts', q + u_bias, k)
        pos_score = jnp.einsum('bhtd,tshd->bhts', q + v_bias, pos)
        scores = (qk_score + pos_score) / math.sqrt(hd)
        attn = jax.nn.softmax(scores, axis=-1)
        ctx = jnp.einsum('bhts,bhsd->bhtd', attn, v)
        ctx = ctx.transpose(0, 2, 1, 3).reshape(b, t, d)
        return ctx @ Wo.T + bo

    def _L1_ffn_ref(x, Wg, bg, W1, b1, W2, b2):
        import jax, jax.numpy as jnp
        import numpy as np
        TOP_K = 2
        B, L, D = x.shape
        E = W1.shape[0]
        xf = x.reshape(-1, D)
        gate_logits = xf @ Wg + bg
        top_w, top_i = jax.lax.top_k(gate_logits, TOP_K)
        top_w = jax.nn.softmax(top_w, axis=-1)
        w_dense = jnp.sum(jax.nn.one_hot(top_i, E, dtype=xf.dtype) * top_w[..., None], axis=1)
        out = jnp.zeros_like(xf)
        for e in range(E):
            h = jax.nn.gelu(xf @ W1[e] + b1[e], approximate=False)
            out = out + w_dense[:, e:e + 1] * (h @ W2[e] + b2[e])
        return out.reshape(B, L, D)
    h = _L0_tok_ref(x, L0_tok_Wp, L0_tok_bp, L0_tok_W1, L0_tok_b1, L0_tok_W2, L0_tok_b2)
    h = h + _L0_attn_ref(_layernorm(h, axis=-1), L0_attn_kln_weight, L0_attn_kln_bias, L0_attn_vln_weight, L0_attn_vln_bias)
    h = h + _L0_ffn_ref(_layernorm(h, axis=-1), L0_ffn_W_gat, L0_ffn_att_src, L0_ffn_att_dst, L0_ffn_b_gat, L0_ffn_ln_gamma, L0_ffn_ln_beta, L0_ffn_W1, L0_ffn_b1, L0_ffn_W2, L0_ffn_b2, L0_ffn_edge_index)
    h = h + _L1_attn_ref(_layernorm(h, axis=-1), L1_attn_ln_gamma, L1_attn_ln_beta, L1_attn_Wq, L1_attn_bq, L1_attn_Wk, L1_attn_bk, L1_attn_Wv, L1_attn_bv, L1_attn_Wpos, L1_attn_bpos, L1_attn_Wo, L1_attn_bo, L1_attn_u_bias, L1_attn_v_bias)
    h = h + _L1_ffn_ref(_layernorm(h, axis=-1), L1_ffn_Wg, L1_ffn_bg, L1_ffn_W1, L1_ffn_b1, L1_ffn_W2, L1_ffn_b2)
    return h

_drawn_inputs = setup_inputs


def setup_inputs(seed=0):
    import zlib

    import numpy as np

    out = dict(_drawn_inputs(seed))
    spreads = {'L0_attn_kln_weight': (1.0, 0.2),
     'L0_attn_kln_bias': (0.0, 0.306),
     'L0_attn_vln_weight': (1.0, 0.2),
     'L0_attn_vln_bias': (0.0, 0.1),
     'L0_ffn_b_gat': (0.0, 0.8),
     'L0_ffn_ln_gamma': (1.0, 0.6),
     'L0_ffn_ln_beta': (0.0, 0.8),
     'L0_ffn_b1': (0.0, 0.8),
     'L0_ffn_b2': (0.0, 0.354),
     'L1_attn_ln_gamma': (1.0, 0.2),
     'L1_attn_ln_beta': (0.0, 0.1),
     'L1_attn_bq': (0.0, 0.8),
     'L1_attn_bk': (0.0, 2.0),
     'L1_attn_bv': (0.0, 0.1),
     'L1_attn_bpos': (0.0, 2.0),
     'L1_attn_bo': (0.0, 0.295),
     'L1_ffn_bg': (0.0, 0.417),
     'L1_ffn_b1': (0.0, 0.8),
     'L1_ffn_b2': (0.0, 0.36)}
    factors = {'L0_tok_bp': 5.111,
     'L0_tok_b1': 6.966,
     'L0_tok_b2': 3.976,
     'L0_ffn_att_src': 40.397,
     'L0_ffn_att_dst': 51.6,
     'L1_attn_u_bias': 8.0,
     'L1_attn_v_bias': 8.0,
     'L1_ffn_Wg': 2.85,
     'L1_ffn_W1': 8.0,
     'L1_ffn_W2': 7.977}
    for name, (base, spread) in spreads.items():
        noise = np.random.default_rng([zlib.crc32(name.encode()), seed]).standard_normal(out[name].shape)
        drawn = base * np.exp(spread * noise) if base else spread * noise
        out[name] = jnp.asarray(drawn.astype(out[name].dtype))
    for name, factor in factors.items():
        out[name] = (out[name] * factor).astype(out[name].dtype)
    return out
```

```python
from contextlib import ExitStack

import concourse.bass as bass
from concourse import mybir

F32 = mybir.dt.float32
I32 = mybir.dt.int32
BF16 = mybir.dt.bfloat16
ALU = mybir.AluOpType
ACT = mybir.ActivationFunctionType
AX = mybir.AxisListType

P = 128
D = 64
NIMG = 64
NTOK = 64
M = NIMG * NTOK
NT = M // P
KP = 3 * 16 * 16
KC = KP // P
NE = 262144
EC = NE // P
H0, HC0 = 8, 8
GH, GE = 4, 4
F0 = 128
H1, HD1 = 4, 16
E1, F1 = 8, 256
FC1 = F1 // P
EPS = 1e-5
BIG = 1e30
PAD = float(1 << 24)
ROW = 2 * (GH * GE + GH)
HF = ROW // 2
NREL = 2 * NTOK - 1

PK128 = {"Wp": KC * D, "W2a": GE * D, "b1a": GE, "W2b": E1 * FC1 * D, "b1b": E1 * FC1}
PK65 = {"pos1": D, "pos2": D, "Wgat": GH * GE, "W1a": GE * F0, "Wq": D, "Wk": D, "Wv": D, "Wpos": D,
        "Wo": D, "Wg": E1, "u": 1, "v": 1, "W1b": E1 * F1, "enc": NREL, "grid": P}
PROW = {"kw": D, "kb": D, "vw": D, "vb": D, "asrc": GH * GE, "adst": GH * GE, "bgat": GH * GE,
        "lng": GH * GE, "lnb": GH * GE, "g1": D, "be1": D, "b2a": GE * D, "b2b": E1 * D}
CST = {"ident": P, "sign": 7, "iota": D, "kvmask": P, "hcol": H1, "vmask": D, "lowa": GE * GE,
       "lowb": E1 * E1}


def columns(widths):
    at, out = 0, {}
    for name, w in widths.items():
        out[name] = (at, at + w)
        at += w
    return out, at


C128, N128 = columns(PK128)
C65, N65 = columns(PK65)
CROW, NROW = columns(PROW)
CCST, NCST = columns(CST)


def spread(ap, dim, shape):
    return ap.unsqueeze(dim).to_broadcast(shape)


def wait_reg(eng, sem, value):
    eng.wait_ge(sem, value)
    eng.nop(nofuse=True)


class Chain:

    def __init__(self, eng, sem):
        self.eng, self.sem, self.n = eng, sem, 0

    def link(self, ins):
        self.n += 1
        ins.then_inc(self.sem, 1)
        self.eng.wait_ge(self.sem, self.n)


def vit_tower(nc, x, edges, w128, w65, wrow, cst, out):
    ctx = ExitStack()
    with ctx:
        def sb(name, shape, dt=F32):
            return ctx.enter_context(nc.sbuf_tensor(name, shape, dt))

        def sem(name):
            return ctx.enter_context(nc.semaphore(name))

        Ht = sb("h_run", [P, NT * D])
        Zt = sb("z_norm", [P, NT * D])
        Ct = sb("centred", [P, NT * D])
        St = sb("squares", [P, NT * D])
        ZT = sb("z_T", [D + 1, M])
        R = sb("arena", [P, 20480])
        w128s = sb("w128s", [P, N128])
        w65s = sb("w65s", [D + 1, N65])
        rows = sb("rows_s", [P, NROW])
        consts = sb("consts_s", [P, NCST])
        mean = sb("mean", [P, NT * H0])
        var = sb("var", [P, NT * H0])
        ones = sb("ones", [P, P])
        cnt = sb("cnt", [P, NT])
        as_ = sb("a_src", [P, NT, GH])
        ad_ = sb("a_dst", [P, NT, GH])
        HG = sb("h_gat", [P, NT, GH * GE])
        gates = sb("gates", [P, NT, E1])
        nreal = sb("n_real", [1, 1], I32)
        PS = ctx.enter_context(nc.psum_tensor("psum", [P, 4096], F32))

        h3 = Ht[:, :].rearrange("p (t d) -> p t d", d=D)
        z3 = Zt[:, :].rearrange("p (t d) -> p t d", d=D)
        c3 = Ct[:, :].rearrange("p (t d) -> p t d", d=D)
        s3 = St[:, :].rearrange("p (t d) -> p t d", d=D)

        def bank(b):
            return PS[:, b * 512:(b + 1) * 512]

        def W128(n):
            return w128s[:, C128[n][0]:C128[n][1]]

        def W65(n, k=D + 1):
            return w65s[0:k, C65[n][0]:C65[n][1]]

        def RO(n):
            return rows[:, CROW[n][0]:CROW[n][1]]

        def CS(n, k=P):
            return consts[0:k, CCST[n][0]:CCST[n][1]]

        ident = CS("ident")

        ts_d = nc.dram_tensor("src_rows", [M, ROW], F32).ap()
        td_d = nc.dram_tensor("dst_rows", [M + 1, HF], F32).ap()
        nt_d = nc.dram_tensor("node_rows", [M, ROW], F32).ap()
        neg_d = nc.dram_tensor("restart_rows", [P, EC], F32).ap()
        skew_d = nc.dram_tensor("skew", [M * H1 * NREL], F32).ap()

        keyA = R[:, 0:2048]
        keyB = R[:, 2048:4096]
        s_ln = sem("s_ln")
        s_std = sem("s_std")
        n_ln = [0]

        def layernorm(e, ch, xin, z, groups, width, unbiased=False):
            m, v = mean[:, 0:groups], var[:, 0:groups]
            cg = Ct[:, :].rearrange("p (g d) -> p g d", d=width)
            sg = St[:, :].rearrange("p (g d) -> p g d", d=width)
            ch.link(nc.vector.reduce_sum(m, xin, AX.X))
            ch.link(nc.vector.tensor_scalar(m, m, -1.0 / width, None, ALU.mult))
            ch.link(nc.vector.tensor_tensor(cg, xin, spread(m, 2, [P, groups, width]), ALU.add))
            ch.link(nc.vector.tensor_tensor(sg, cg, cg, ALU.mult))
            ch.link(nc.vector.reduce_sum(v, sg, AX.X))
            n_ln[0] += 1
            if unbiased:
                nc.vector.tensor_scalar(v, v, 1.0 / (width - 1), None, ALU.mult).then_inc(s_ln, 1)
            else:
                nc.vector.tensor_scalar(v, v, 1.0 / width, EPS, ALU.mult, ALU.add).then_inc(s_ln, 1)
            e.wait_ge(s_std, n_ln[0])
            if unbiased:
                ch.link(nc.vector.tensor_scalar(v, v, EPS, None, ALU.add))
            ch.link(nc.vector.reciprocal(v, v))
            ch.link(nc.vector.tensor_tensor(z, cg, spread(v, 2, [P, groups, width]), ALU.mult))

        n_root = [0]

        def root(e, groups):
            n_root[0] += 1
            e.wait_ge(s_ln, n_root[0])
            nc.scalar.sqrt(var[:, 0:groups], var[:, 0:groups]).then_inc(s_std, 1)

        def gating(e, ch, sc, n, low, s_x, s_e, k):
            A = R[:, 0:NT * n * n].rearrange("p (t i j) -> p t i j", i=n, j=n)
            B = R[:, 2048:2048 + NT * n * n].rearrange("p (t i j) -> p t i j", i=n, j=n)
            rank = R[:, 4096:4096 + NT * n].rearrange("p (t i) -> p t i", i=n)
            top = R[:, 4608:4608 + NT]
            full = [P, NT, n, n]
            xj, xi = spread(sc, 2, full), spread(sc, 3, full)
            nc.vector.tensor_tensor(A, xj, xi, ALU.is_gt).then_inc(ch.sem, 1)
            ch.n += 1
            ch.link(nc.vector.tensor_tensor(B, xj, xi, ALU.is_equal))
            lo = spread(low, 1, [P, NT, n * n]).rearrange("p t (i j) -> p t i j", i=n)
            ch.link(nc.vector.tensor_tensor(B, B, lo, ALU.mult))
            ch.link(nc.vector.tensor_tensor(A, A, B, ALU.add))
            ch.link(nc.vector.reduce_sum(rank, A, AX.X))
            ch.link(nc.vector.tensor_scalar(rank, rank, 1.5, None, ALU.is_lt))
            ch.link(nc.vector.reduce_max(top, sc, AX.X))
            nc.vector.tensor_tensor(sc, sc, spread(top, 2, [P, NT, n]), ALU.subtract).then_inc(s_x, 1)
            e.wait_ge(s_e, k)
            ch.link(nc.vector.tensor_tensor(sc, sc, rank, ALU.mult))
            ch.link(nc.vector.reduce_sum(top, sc, AX.X))
            ch.link(nc.vector.reciprocal(top, top))
            ch.link(nc.vector.tensor_tensor(sc, sc, spread(top, 2, [P, NT, n]), ALU.mult))

        def transpose_z(e, s_z, s_bank, s_free, z_count):
            e.wait_ge(s_z, z_count)
            for t in range(NT):
                ins = nc.tensor.transpose(PS[0:D, t * P:(t + 1) * P], z3[:, t, :], ident)
                if t % 4 == 3:
                    ins.then_inc(s_bank, 1)

        def copy_zT(e, s_bank, base, s_zT):
            for b in range(8):
                e.wait_ge(s_bank, base + b + 1)
                nc.scalar.copy(ZT[0:D, b * 512:(b + 1) * 512], PS[0:D, b * 512:(b + 1) * 512]).then_inc(s_zT, 1)

        xbuf = [R[:, 10240 + i * 3072:10240 + (i + 1) * 3072].rearrange("p (c t) -> p c t", c=KC) for i in (0, 1)]
        e_src = R[:, 4096:6144].bitcast(I32)
        e_dst = R[:, 6144:8192].bitcast(I32)
        lo_d = R[:, 8192:9216].bitcast(BF16)
        hi_d = R[:, 9216:10240].bitcast(BF16)
        one_lo = [Zt[:, :].bitcast(BF16).rearrange("p (l k) -> p l k", k=64),
                  Ct[:, :].bitcast(BF16).rearrange("p (l k) -> p l k", k=64)]
        one_hi = [St[:, :].bitcast(BF16).rearrange("p (l k) -> p l k", k=64),
                  R[:, 18432:20480].bitcast(BF16).rearrange("p (l k) -> p l k", k=64)]
        iota_lk = keyB.bitcast(BF16).rearrange("p (l k) -> p l k", k=64)
        pos_l = sb("pos_l", [D + 2, P])
        pos_r = sb("pos_r", [D + 2, D])
        rc = sb("real_count", [P, 1])
        HB = 64
        with ExitStack() as c1, nc.Block() as block:
            def sm(n):
                return c1.enter_context(nc.semaphore(n))
            s_pack, s_edge = sm("s_pack"), sm("s_edge")
            s_x = [sm("s_x0"), sm("s_x1")]
            s_xused, s_hid, s_posl, s_posones, s_ones = sm("s_xused"), sm("s_hid"), sm("s_posl"), sm("s_posones"), sm("s_ones")
            s_tok, s_v, s_hot, s_hotused, s_cnt, s_cntc, s_rc, s_rsum = (sm("s_tok"), sm("s_v1"), sm("s_hot"), sm("s_hotused"),
                                                                  sm("s_cnt"), sm("s_cntc"), sm("s_rc"), sm("s_rsum"))
            s_h = sm("s_h")
            NG = M // 512

            @block.sync
            def _(e):
                e.dma_start(e_src, edges[0, :].rearrange("(p c) -> p c", p=P)).then_inc(s_edge, 16)
                e.dma_start(e_dst, edges[1, :].rearrange("(p c) -> p c", p=P)).then_inc(s_edge, 16)
                for g in range(NG):
                    if g >= 2:
                        e.wait_ge(s_xused, g - 1)
                    e.dma_start(xbuf[g % 2], x[:, :, g * 512:(g + 1) * 512]).then_inc(s_x[g % 2], 16)

            @block.scalar
            def _(e):
                e.dma_start(consts[:, :], cst).then_inc(s_pack, 16)
                e.dma_start(w65s[:, :], w65).then_inc(s_pack, 16)
                e.dma_start(w128s[:, :], w128).then_inc(s_pack, 16)
                e.dma_start(rows[:, :], wrow.to_broadcast([P, NROW])).then_inc(s_pack, 16)
                e.dma_start(pos_r[0:D + 1, :], w65[:, C65["pos2"][0]:C65["pos2"][1]]).then_inc(s_pack, 16)
                e.dma_start(pos_r[D + 1:D + 2, :], w65[D:D + 1, C65["pos1"][0]:C65["pos1"][1]]).then_inc(s_pack, 16)
                e.wait_ge(s_hid, 1)
                nc.scalar.activation(pos_l[0:D, :], PS[0:D, 7 * 512:7 * 512 + P], ACT.Relu).then_inc(s_posl, 1)
                for b in range(4):
                    e.wait_ge(s_tok, b + 1)
                    nc.scalar.copy(Ht[:, b * 512:(b + 1) * 512], bank(b)).then_inc(s_h, 1)

            @block.tensor
            def _(e):
                e.wait_ge(s_pack, 96)
                nc.tensor.matmul(PS[0:D, 7 * 512:7 * 512 + P], W65("pos1", 3), W65("grid", 3),
                                 start=True, stop=True).then_inc(s_hid, 1)
                acc = PS[0:64, 4 * 512:4 * 512 + 64]
                e.wait_ge(s_hot, 1)
                nc.tensor.matmul(acc, one_lo[0][:, :, 0], one_hi[0][:, :, 0], start=True, stop=False)
                for k in range(1, HB):
                    ins = nc.tensor.matmul(acc, one_lo[0][:, :, k], one_hi[0][:, :, k], start=False, stop=False)
                ins.then_inc(s_hotused, 1)
                with e.Fori(0, (EC // HB - 2) // 2) as i:
                    for j, b in ((0, 1), (1, 0)):
                        wait_reg(e, s_hot, i * 2 + 2 + j)
                        for k in range(HB):
                            ins = nc.tensor.matmul(acc, one_lo[b][:, :, k], one_hi[b][:, :, k], start=False, stop=False)
                        ins.then_inc(s_hotused, 1)
                e.wait_ge(s_hot, EC // HB)
                for k in range(HB):
                    ins = nc.tensor.matmul(acc, one_lo[1][:, :, k], one_hi[1][:, :, k], start=False, stop=(k == HB - 1))
                ins.then_inc(s_cnt, 1)
                e.wait_ge(s_posl, 1)
                e.wait_ge(s_posones, 1)
                wp = W128("Wp").rearrange("p (c d) -> p c d", c=KC)
                for g in range(NG):
                    e.wait_ge(s_x[g % 2], 16 * (g // 2 + 1))
                    for j in range(4):
                        t = 4 * g + j
                        o = PS[:, t * D:(t + 1) * D]
                        for c in range(KC):
                            ins = nc.tensor.matmul(o, xbuf[g % 2][:, c, j * P:(j + 1) * P], wp[:, c, :],
                                                   start=(c == 0), stop=False)
                        if j == 3:
                            ins.then_inc(s_xused, 1)
                        ins = nc.tensor.matmul(o, pos_l[:, :], pos_r[:, :], start=False, stop=True)
                        if t % 8 == 7:
                            ins.then_inc(s_tok, 1)
                e.wait_ge(s_rc, 1)
                e.wait_ge(s_ones, 1)
                nc.tensor.matmul(PS[0:1, 6 * 512:6 * 512 + 1], rc[:, :], ones[:, 0:1], start=True, stop=True).then_inc(s_rsum, 1)

            @block.vector
            def _(e):
                ch = Chain(e, s_v)
                nc.vector.memset(pos_l[D:D + 2, :], 1.0).then_inc(s_posones, 1)
                nc.vector.memset(ones[:, :], 1.0).then_inc(s_ones, 1)
                nc.vector.memset(ZT[D:D + 1, :], 1.0)
                e.wait_ge(s_edge, 32)
                srcf, dstf = Zt[:, :], Ct[:, :]
                ch.link(nc.vector.tensor_copy(srcf, e_src))
                ch.link(nc.vector.tensor_copy(dstf, e_dst))
                ch.link(nc.vector.scalar_tensor_tensor(keyA, dstf, float(M), srcf, ALU.mult, ALU.add))
                ch.link(nc.vector.tensor_scalar(keyB, srcf, float(M - 1), PAD, ALU.is_ge, ALU.mult))
                ch.link(nc.vector.tensor_tensor(keyA, keyA, keyB, ALU.add))
                ch.link(nc.vector.tensor_scalar(keyA, keyA, PAD, None, ALU.min))
                ch.link(nc.vector.tensor_scalar(keyB, keyA, PAD, None, ALU.is_lt))
                nc.vector.reduce_sum(rc[:, :], keyB, AX.X).then_inc(s_rc, 1)
                lo_i, hi_i = St[:, :].bitcast(I32), R[:, 18432:20480].bitcast(I32)
                ch.link(nc.vector.tensor_scalar(lo_i, e_dst, 63, None, ALU.bitwise_and))
                ch.link(nc.vector.tensor_copy(lo_d, lo_i))
                ch.link(nc.vector.tensor_scalar(hi_i, e_dst, 6, None, ALU.arith_shift_right))
                ch.link(nc.vector.tensor_scalar(dstf, hi_i, 64.0, None, ALU.min))
                ch.link(nc.vector.tensor_scalar(srcf, srcf, float(M - 1), 64.0, ALU.is_lt, ALU.mult))
                ch.link(nc.vector.tensor_tensor(hi_d, dstf, srcf, ALU.add))
                e.wait_ge(s_pack, 96)
                ch.link(nc.vector.tensor_copy(iota_lk, spread(CS("iota"), 2, [P, 64, 64])))

                def hots(b, cols):
                    nc.vector.tensor_tensor(one_lo[b], spread(lo_d[:, cols], 1, [P, 64, HB]), iota_lk, ALU.is_equal)
                    nc.vector.tensor_tensor(one_hi[b], spread(hi_d[:, cols], 1, [P, 64, HB]), iota_lk,
                                            ALU.is_equal).then_inc(s_hot, 1)
                hots(0, slice(0, HB))
                hots(1, slice(HB, 2 * HB))
                with e.Fori(0, (EC // HB - 2) // 2) as i:
                    for j in (0, 1):
                        wait_reg(e, s_hotused, i * 2 + 1 + j)
                        hots(j, bass.ds((i * 2 + 2 + j) * HB, HB))
                e.wait_ge(s_cnt, 1)
                acc = PS[0:64, 4 * 512:4 * 512 + 64].rearrange("l (t b) -> l t b", b=2)
                nc.vector.tensor_copy(cnt[0:64, :], acc[:, :, 0])
                nc.vector.tensor_copy(cnt[64:128, :], acc[:, :, 1])
                e.wait_ge(s_rsum, 1)
                nc.vector.tensor_copy(nreal[:, :], PS[0:1, 6 * 512:6 * 512 + 1])

        kt = R[:, 10240:12288].rearrange("p (t d) -> p t d", d=D)
        vblk = R[:, 12288:16384].rearrange("p (t i d) -> p t i d", i=2, d=D)
        KV = R[0:D, 4096:8192].rearrange("p (t n) -> p t n", n=P)
        TS = R[:, 10240:10240 + NT * ROW].rearrange("p (t r) -> p t r", r=ROW)
        TD = R[:, 11520:11520 + NT * HF].rearrange("p (t r) -> p t r", r=HF)
        NI = R[:, 12288:12288 + NT * ROW].rearrange("p (t r) -> p t r", r=ROW)
        PT = [P, NT, D]
        with ExitStack() as c2, nc.Block() as block:
            def sm(n):
                return c2.enter_context(nc.semaphore(n))
            s_v, s_z, s_bank, s_zT, s_kv, s_kvp, s_kvc, s_o, s_hg, s_tab, s_out, s_zTf = (
                sm("s_v2"), sm("s_z"), sm("s_bank"), sm("s_zT"), sm("s_kv"), sm("s_kvp"), sm("s_kvc"), sm("s_o"),
                sm("s_hg"), sm("s_tab"), sm("s_tabout"), sm("s_zTf"))

            @block.vector
            def _(e):
                ch = Chain(e, s_v)
                nc.vector.memset(R[:, 12288:16384], 0.0).then_inc(s_v, 1)
                ch.n += 1
                layernorm(e, ch, h3, z3, NT, D)
                nc.vector.tensor_tensor(Ht[:, :], Ht[:, :], Zt[:, :], ALU.add).then_inc(s_z, 1)
                zg = Zt[:, :].rearrange("p (g d) -> p g d", d=HC0)
                layernorm(e, ch, zg, Ct[:, :].rearrange("p (g d) -> p g d", d=HC0), NT * H0, HC0, unbiased=True)
                ch.link(nc.vector.tensor_tensor(kt, c3, spread(RO("kw"), 1, PT), ALU.mult))
                ch.link(nc.vector.tensor_tensor(kt, kt, spread(RO("kb"), 1, PT), ALU.add))
                ch.link(nc.vector.tensor_tensor(s3, c3, spread(RO("vw"), 1, PT), ALU.mult))
                for i in (0, 1):
                    r = slice(64 * i, 64 * i + 64)
                    ins = nc.vector.tensor_tensor(vblk[r, :, i, :], s3[r, :, :],
                                                  spread(rows[r, CROW["vb"][0]:CROW["vb"][1]], 1, [64, NT, D]), ALU.add)
                ins.then_inc(s_kv, 1)
                for b in range(8):
                    e.wait_ge(s_kvp, b + 1)
                    nc.vector.tensor_tensor(KV[:, 4 * b:4 * b + 4, :], PS[0:D, b * 512:(b + 1) * 512].rearrange("p (t n) -> p t n", n=P),
                                            spread(CS("kvmask", D), 1, [D, 4, P]), ALU.mult).then_inc(s_kvc, 1)
                for b in range(8):
                    e.wait_ge(s_o, b + 1)
                    for i in (0, 1):
                        r = slice(64 * i, 64 * i + 64)
                        o = PS[r, b * 512:(b + 1) * 512].rearrange("p (t i d) -> p t i d", i=2, d=D)[:, :, i, :]
                        ins = nc.vector.tensor_tensor(h3[r, 4 * b:4 * b + 4, :], h3[r, 4 * b:4 * b + 4, :], o, ALU.add)
                        if (b, i) != (7, 1):
                            ins.then_inc(s_v, 1)
                            ch.n += 1
                ch.link(ins)
                layernorm(e, ch, h3, z3, NT, D)
                nc.vector.memset(NI[:, :, 0:HF], 0.0).then_inc(s_z, 1)
                nc.vector.memset(NI[:, :, HF:ROW], -BIG).then_inc(s_tab, 1)
                e.wait_ge(s_hg, 1)
                ch.link(nc.vector.tensor_copy(HG[:, :, :], bank(0).rearrange("p (t f) -> p t f", f=GH * GE)))
                G4 = [P, NT, GH, GE]
                for name, a, scratch in (("asrc", as_, s3), ("adst", ad_, c3)):
                    pr = scratch[:, :, 0:GH * GE]
                    ch.link(nc.vector.tensor_tensor(pr, HG[:, :, :], spread(RO(name), 1, [P, NT, GH * GE]), ALU.mult))
                    ch.link(nc.vector.reduce_sum(a[:, :, :], pr.rearrange("p t (h e) -> p t h e", h=GH), AX.X))
                for T, a in ((TS, as_), (TD, ad_)):
                    nc.vector.tensor_copy(T[:, :, 0:16].rearrange("p t (h e) -> p t h e", h=GH), spread(a[:, :, :], 3, G4))
                    nc.vector.tensor_copy(T[:, :, 16:20], a[:, :, :])
                nc.vector.tensor_copy(TS[:, :, 20:36], HG[:, :, :])
                nc.vector.memset(TS[:, :, 36:40], 1.0).then_inc(s_tab, 1)

            @block.scalar
            def _(e):
                root(e, NT)
                root(e, NT * H0)
                copy_zT(e, s_bank, 0, s_zT)
                root(e, NT)
                copy_zT(e, s_bank, 8, s_zT)

            @block.tensor
            def _(e):
                transpose_z(e, s_z, s_bank, None, 1)
                e.wait_ge(s_kv, 1)
                for t in range(NT):
                    if t % 4 == 0:
                        e.wait_ge(s_zT, t // 4 + 1)
                    ins = nc.tensor.matmul(PS[0:D, t * P:(t + 1) * P], kt[:, t, :],
                                           vblk[:, t, :, :].rearrange("p i d -> p (i d)"), start=True, stop=True)
                    if t % 4 == 3:
                        ins.then_inc(s_kvp, 1)
                for t in range(NT):
                    if t % 4 == 0:
                        e.wait_ge(s_kvc, t // 4 + 1)
                    ins = nc.tensor.matmul(PS[:, t * P:(t + 1) * P], ZT[0:D, t * P:(t + 1) * P], KV[:, t, :], start=True, stop=True)
                    if t % 4 == 3:
                        ins.then_inc(s_o, 1)
                transpose_z(e, s_z, s_bank, None, 2)
                e.wait_ge(s_zT, 16)
                for t in range(NT):
                    ins = nc.tensor.matmul(PS[:, t * 16:(t + 1) * 16], ZT[0:D, t * P:(t + 1) * P], W65("Wgat", D), start=True, stop=True)
                ins.then_inc(s_hg, 1)

            @block.sync
            def _(e):
                e.wait_ge(s_tab, 1)
                e.dma_start(nt_d.rearrange("(t p) r -> p t r", p=P), NI).then_inc(s_out, 16)
                e.wait_ge(s_tab, 2)
                e.dma_start(ts_d.rearrange("(t p) r -> p t r", p=P), TS).then_inc(s_out, 16)
                e.dma_start(td_d[0:M, :].rearrange("(t p) r -> p t r", p=P), TD).then_inc(s_out, 16)
                e.dma_start(td_d[M:M + 1, :], NI[0:1, 0, 0:HF]).then_inc(s_out, 16)
                e.wait_ge(s_out, 64)

        Y = [R[:, 10240 + i * 2048:10240 + (i + 1) * 2048].rearrange("p (t d) -> p t d", d=D) for i in range(GE)]
        hid = [sb(f"hid{i}", [P, 512]) for i in range(2)]
        keys = [keyA, keyB]
        plan = []
        for k in range(1, 11):
            plan += [("swap", j, k) for j in range(k - 1, -1, -1)]
        plan += [("sign", 0)] + [("swap", j, None) for j in range(10, -1, -1)] + [("sign", 0)]
        for k in range(12, 19):
            b = k - 11 if k < 18 else None
            plan += [("turn", None)] + [("swap", j, b) for j in range(k - 12, -1, -1)] + [("turn", b)]
            plan += [("swap", j, None) for j in range(10, -1, -1)]
            if b is not None:
                plan += [("sign", b)]
        final = sum(it[0] != "sign" for it in plan) % 2
        with ExitStack() as c3_, nc.Block() as block:
            def sm(n):
                return c3_.enter_context(nc.semaphore(n))
            s_swap, s_turn, s_back, s_sign = sm("s_swap"), sm("s_turn"), sm("s_back"), sm("s_sign")
            s_hp, s_hs, s_yp, s_y = sm("s_hp"), sm("s_hs"), sm("s_yp"), sm("s_y")

            @block.vector
            def _(e):
                cur = n = turned = signed = 0
                for it in plan:
                    if it[0] == "swap":
                        _, j, k = it
                        src, dst = keys[cur], keys[cur ^ 1]
                        if n:
                            e.wait_ge(s_swap, n)
                        if k is None:
                            pat, kw = "p (g two s) -> p g two s", dict(two=2, s=1 << j)
                            jobs = [(src.rearrange(pat, **kw), dst.rearrange(pat, **kw), ALU.min, ALU.max)]
                        else:
                            pat = "p (n up g two s) -> p n up g two s"
                            kw = dict(up=2, g=1 << (k - 1 - j), two=2, s=1 << j)
                            a, d = src.rearrange(pat, **kw), dst.rearrange(pat, **kw)
                            jobs = [(a[:, :, 0], d[:, :, 0], ALU.min, ALU.max), (a[:, :, 1], d[:, :, 1], ALU.max, ALU.min)]
                        for a, d, first, second in jobs:
                            ix = (slice(None),) * (len(a.shape) - 2)
                            lo, hi = a[ix + (0,)], a[ix + (1,)]
                            nc.vector.tensor_tensor(d[ix + (0,)], lo, hi, first).then_inc(s_swap, 1)
                            nc.vector.tensor_tensor(d[ix + (1,)], lo, hi, second).then_inc(s_swap, 1)
                            n += 2
                        cur ^= 1
                    elif it[0] == "sign":
                        signed += 1
                        e.wait_ge(s_sign, signed)
                    else:
                        turned += 4
                        e.wait_ge(s_back, turned)
                        cur ^= 1

            @block.scalar
            def _(e):
                for g in range(8):
                    for x_ in range(GE):
                        i = g * GE + x_
                        e.wait_ge(s_hp, i + 1)
                        if i >= 2:
                            e.wait_ge(s_yp, i - 1)
                        nc.scalar.activation(hid[i % 2][:, :], bank(4 + i % 2), ACT.Gelu,
                                             bias=w128s[:, C128["b1a"][0] + x_:C128["b1a"][0] + x_ + 1]).then_inc(s_hs, 1)
                        e.wait_ge(s_yp, i + 1)
                        nc.scalar.copy(Y[x_][:, 4 * g:4 * g + 4, :],
                                       PS[:, (6 + i % 2) * 512:(6 + i % 2) * 512 + 256].rearrange("p (t d) -> p t d", d=D)).then_inc(s_y, 1)
                cur = n = turned = signed = 0
                for it in plan:
                    if it[0] == "swap":
                        cur ^= 1
                        n += 4 if it[2] else 2
                    elif it[0] == "sign":
                        e.wait_ge(s_swap, n)
                        s = consts[:, CCST["sign"][0] + it[1]:CCST["sign"][0] + it[1] + 1]
                        nc.scalar.mul(keys[cur], keys[cur], s).then_inc(s_sign, 1)
                        signed += 1
                    else:
                        for c in range(4):
                            turned += 1
                            e.wait_ge(s_turn, turned)
                            o, i_ = keys[cur ^ 1][:, c * 512:(c + 1) * 512], bank(c)
                            if it[1] is None:
                                nc.scalar.copy(o, i_).then_inc(s_back, 1)
                            else:
                                nc.scalar.mul(o, i_, consts[:, CCST["sign"][0] + it[1]:CCST["sign"][0] + it[1] + 1]).then_inc(s_back, 1)
                        cur ^= 1

            @block.tensor
            def _(e):
                w1 = W65("W1a", D).rearrange("p (e f) -> p e f", e=GE)
                w2 = W128("W2a").rearrange("p (e d) -> p e d", e=GE)
                for g in range(8):
                    for x_ in range(GE):
                        i = g * GE + x_
                        if i >= 2:
                            e.wait_ge(s_hs, i - 1)
                        nc.tensor.matmul(bank(4 + i % 2), w1[:, x_, :], ZT[0:D, g * 512:(g + 1) * 512], start=True, stop=True).then_inc(s_hp, 1)
                        e.wait_ge(s_hs, i + 1)
                        if i >= 2:
                            e.wait_ge(s_y, i - 1)
                        b2 = rows[0:1, CROW["b2a"][0] + x_ * D:CROW["b2a"][0] + (x_ + 1) * D]
                        for j in range(4):
                            o = PS[:, (6 + i % 2) * 512 + j * D:(6 + i % 2) * 512 + (j + 1) * D]
                            nc.tensor.matmul(o, hid[i % 2][:, j * P:(j + 1) * P], w2[:, x_, :], start=True, stop=False)
                            ins = nc.tensor.matmul(o, ones[0:1, :], b2, start=False, stop=True)
                        ins.then_inc(s_yp, 1)
                cur = n = turned = signed = 0
                for it in plan:
                    if it[0] == "swap":
                        cur ^= 1
                        n += 4 if it[2] else 2
                    elif it[0] == "sign":
                        signed += 1
                    else:
                        e.wait_ge(s_swap, n)
                        if signed:
                            e.wait_ge(s_sign, signed)
                        if turned:
                            e.wait_ge(s_back, turned)
                        for c in range(16):
                            ins = nc.tensor.transpose(PS[:, c * P:(c + 1) * P], keys[cur][:, c * P:(c + 1) * P], ident)
                            if c % 4 == 3:
                                ins.then_inc(s_turn, 1)
                        turned += 4
                        cur ^= 1

        K = keys[final]
        other = keys[final ^ 1]
        idx = [R[:, 4096 + i * 2048:4096 + (i + 1) * 2048].bitcast(I32) for i in range(3)]
        DF, SF, XF, SAME = Zt[:, :], Ct[:, :], St[:, :], R[:, 18432:20480]
        prevc, nextc, edgec = sb("prev_col", [P, 1]), sb("next_col", [P, 1]), sb("edge_col", [P, 1])
        with ExitStack() as c4, nc.Block() as block:
            def sm(n):
                return c4.enter_context(nc.semaphore(n))
            s_v, s_d, s_shift, s_neg, s_negout, s_three, s_t, s_i = (sm("s_v4"), sm("s_d"), sm("s_shift"), sm("s_neg"), sm("s_negout"),
                                                           sm("s_three"), sm("s_t"), sm("s_i"))

            @block.vector
            def _(e):
                ch = Chain(e, s_v)
                ki, di = other.bitcast(I32), idx[0]
                ch.link(nc.vector.tensor_copy(ki, K))
                ch.link(nc.vector.tensor_scalar(di, ki, 12, None, ALU.arith_shift_right))
                nc.vector.memset(prevc[:, :], -1.0)
                nc.vector.memset(nextc[:, :], -1.0)
                nc.vector.tensor_copy(DF, di).then_inc(s_d, 1)
                ch.link(nc.vector.tensor_scalar(idx[1], ki, M - 1, None, ALU.bitwise_and))
                nc.vector.tensor_copy(SF, idx[1]).then_inc(s_three, 1)
                e.wait_ge(s_d, 1)
                ch.link(nc.vector.tensor_tensor(SAME[:, 1:], DF[:, 1:], DF[:, :-1], ALU.is_equal))
                e.wait_ge(s_shift, 32)
                ch.link(nc.vector.tensor_tensor(SAME[:, 0:1], DF[:, 0:1], prevc[:, :], ALU.is_equal))
                ch.link(nc.vector.tensor_tensor(edgec[:, :], DF[:, EC - 1:EC], nextc[:, :], ALU.is_equal))
                nc.vector.scalar_tensor_tensor(XF[:, :-1], SAME[:, 1:], 8192.0, DF[:, :-1], ALU.mult, ALU.add).then_inc(s_three, 1)
                nc.vector.scalar_tensor_tensor(XF[:, EC - 1:EC], edgec[:, :], 8192.0, DF[:, EC - 1:EC], ALU.mult, ALU.add).then_inc(s_three, 1)
                nc.vector.tensor_scalar(other, SAME, 1.0, BIG, ALU.subtract, ALU.mult).then_inc(s_neg, 1)

            @block.sync
            def _(e):
                e.wait_ge(s_d, 1)
                with nc.allow_non_contiguous_dma(reason="one column, moved by a partition"):
                    e.dma_start(prevc[1:P, :], DF[0:P - 1, EC - 1:EC]).then_inc(s_shift, 16)
                    e.dma_start(nextc[0:P - 1, :], DF[1:P, 0:1]).then_inc(s_shift, 16)
                e.wait_ge(s_neg, 1)
                e.dma_start(neg_d, other).then_inc(s_negout, 16)
                e.wait_ge(s_negout, 16)

            @block.tensor
            def _(e):
                e.wait_ge(s_three, 3)
                e.wait_ge(s_neg, 1)
                for i, a in enumerate((SF, DF, XF)):
                    for c in range(16):
                        b = (4 * i + c // 4) % 8
                        if c % 4 == 0 and 4 * i + c // 4 >= 8:
                            e.wait_ge(s_i, 4 * i + c // 4 - 7)
                        ins = nc.tensor.transpose(PS[:, b * 512 + (c % 4) * P:b * 512 + (c % 4 + 1) * P], a[:, c * P:(c + 1) * P], ident)
                        if c % 4 == 3:
                            ins.then_inc(s_t, 1)

            @block.scalar
            def _(e):
                for i in range(3):
                    o = idx[i].rearrange("q (p c) -> q c p", c=16)
                    for c in range(4):
                        n = 4 * i + c
                        e.wait_ge(s_t, n + 1)
                        nc.scalar.copy(o[:, 4 * c:4 * c + 4, :], bank(n % 8).rearrange("q (c p) -> q c p", c=4)).then_inc(s_i, 1)

        cur = sb("cur_idx", [P, 3, 16], I32)
        negr = R[0:HF, 18432:20480]
        Gs = R[:, 0:320].rearrange("p (b c r) -> p b c r", b=2, c=4)
        Gd = R[:, 320:480].rearrange("p (b c r) -> p b c r", b=2, c=4)
        ends = R[:, 480:800].rearrange("p (b c r) -> p b c r", b=2, c=4)

        def two(t, at, n=512):
            return t[0:HF, at:at + 2 * n].rearrange("p (b n) -> p b n", b=2)
        leak, ev, acc, dec, wt, run = two(Zt, 0), two(Zt, 1024), two(Ct, 0), two(Ct, 1024), two(St, 0), two(R, 1024, 513)
        with ExitStack() as c5, nc.Block() as block:
            def sm(n):
                return c5.enter_context(nc.semaphore(n))
            s_idx, s_neg, s_row, s_leak, s_ch, s_sub, s_exp, s_acc, s_tr, s_ends, s_done, s_init = (
                sm("s_idx"), sm("s_neg5"), sm("s_row"), sm("s_leak"), sm("s_ch5"), sm("s_sub"), sm("s_exp"), sm("s_acc"),
                sm("s_tr"), sm("s_ends"), sm("s_done"), sm("s_init"))
            s_gat, s_sc = [sm("s_gat0"), sm("s_gat1")], [sm("s_sc0"), sm("s_sc1")]

            def groups(e, body):
                n = e.value_load(nreal[0:1, 0:1], min_val=0, max_val=NE)
                with e.Fori(0, P) as g:
                    with e.If(n > g * EC):
                        body(g)

            @block.sync
            def _(e):
                def body(g):
                    wait_reg(e, s_done, g + 1)
                    e.dma_start(negr[:, :], neg_d[bass.ds(g, 1), :].to_broadcast([HF, EC])).then_inc(s_neg, 16)
                groups(e, body)

            @block.gpsimd
            def _(e):
                def body(g):
                    wait_reg(e, s_idx, 3 * (g + 1))

                    def gather(k):
                        b = k % 2
                        if k >= 2:
                            wait_reg(e, s_row, 4 * g + k - 1)
                        for c in range(4):
                            e.indirect_dma_start(Gs[:, b, c, :], None, ts_d,
                                                 bass.IndirectOffsetOnAxis(cur[:, 0, 4 * k + c:4 * k + c + 1], axis=0)).then_inc(s_gat[b], 16)
                            e.indirect_dma_start(Gd[:, b, c, :], None, td_d,
                                                 bass.IndirectOffsetOnAxis(cur[:, 1, 4 * k + c:4 * k + c + 1], axis=0)).then_inc(s_gat[b], 16)

                    def scatter(k):
                        wait_reg(e, s_ends, 4 * g + k + 1)
                        for c in range(4):
                            e.indirect_dma_start(nt_d, bass.IndirectOffsetOnAxis(cur[:, 2, 4 * k + c:4 * k + c + 1], axis=0),
                                                 ends[:, k % 2, c, :], None, bounds_check=M - 1, oob_is_err=False).then_inc(s_sc[k % 2], 16)
                    gather(0)
                    gather(1)
                    for k in range(4):
                        scatter(k)
                        if k + 2 < 4:
                            gather(k + 2)
                    wait_reg(e, s_sc[0], g * 128 + 128)
                    wait_reg(e, s_sc[1], g * 128 + 128)
                    e.sem_inc(s_done, 1)
                e.sem_inc(s_done, 1)
                groups(e, body)

            @block.tensor
            def _(e):
                def body(g):
                    def turn_in(k):
                        b = k % 2
                        wait_reg(e, s_gat[b], g * 256 + 128 * (k // 2 + 1))
                        if k >= 2:
                            wait_reg(e, s_acc, 4 * g + k - 1)
                        for c in range(4):
                            o = PS[0:HF, b * 512 + c * P:b * 512 + (c + 1) * P]
                            nc.tensor.matmul(o, Gs[:, b, c, 0:HF], ident, start=True, stop=False)
                            nc.tensor.matmul(o, Gd[:, b, c, :], ident, start=False, stop=True)
                            ins = nc.tensor.transpose(PS[0:HF, (2 + b) * 512 + c * P:(2 + b) * 512 + (c + 1) * P], Gs[:, b, c, HF:ROW], ident)
                        ins.then_inc(s_row, 1)

                    def turn_out(k):
                        b = k % 2
                        wait_reg(e, s_acc, 4 * g + k + 1)
                        if k >= 2:
                            wait_reg(e, s_ends, 4 * g + k - 1)
                        for c in range(4):
                            o = (4 + b) * 512 + c * ROW
                            nc.tensor.transpose(PS[:, o:o + HF], acc[:, b, c * P:(c + 1) * P], CS("ident", HF)[:, 0:HF])
                            ins = nc.tensor.transpose(PS[:, o + HF:o + ROW], run[:, b, 1 + c * P:1 + (c + 1) * P], CS("ident", HF)[:, 0:HF])
                        ins.then_inc(s_tr, 1)
                    turn_in(0)
                    for k in range(4):
                        if k < 3:
                            turn_in(k + 1)
                        turn_out(k)
                groups(e, body)

            @block.scalar
            def _(e):
                def body(g):
                    for k in range(4):
                        b = k % 2
                        wait_reg(e, s_row, 4 * g + k + 1)
                        nc.scalar.mul(leak[:, b, :], PS[0:HF, b * 512:(b + 1) * 512], 0.2).then_inc(s_leak, 1)
                        wait_reg(e, s_sub, 8 * g + 2 * k + 1)
                        nc.scalar.activation(wt[:, b, :], wt[:, b, :], ACT.Exp).then_inc(s_exp, 1)
                        wait_reg(e, s_sub, 8 * g + 2 * k + 2)
                        nc.scalar.activation(dec[:, b, :], dec[:, b, :], ACT.Exp).then_inc(s_exp, 1)
                        wait_reg(e, s_tr, 4 * g + k + 1)
                        if k >= 2:
                            wait_reg(e, s_sc[b], g * 128 + 64)
                        nc.scalar.copy(ends[:, b, :, :], PS[:, (4 + b) * 512:(4 + b) * 512 + 4 * ROW].rearrange("p (c f) -> p c f", c=4)).then_inc(s_ends, 1)
                groups(e, body)

            @block.vector
            def _(e):
                nc.vector.memset(run[:, 1, 512:513], 0.0).then_inc(s_init, 1)
                nc.vector.memset(acc[:, 1, 511:512], 0.0).then_inc(s_init, 1)
                e.wait_ge(s_init, 2)
                LINKS = 5 * 4

                def body(g):
                    wait_reg(e, s_done, g + 1)
                    for i in range(3):
                        nc.vector.tensor_copy(cur[:, i, :], idx[i][:, bass.ds(g * 16, 16)]).then_inc(s_idx, 1)
                    wait_reg(e, s_neg, g * 16 + 16)
                    n = [0]

                    def link(ins):
                        n[0] += 1
                        ins.then_inc(s_ch, 1)
                        wait_reg(e, s_ch, g * LINKS + n[0])
                    for k in range(4):
                        b, sl = k % 2, slice(k * 512, (k + 1) * 512)
                        wait_reg(e, s_leak, 4 * g + k + 1)
                        if k >= 2:
                            wait_reg(e, s_tr, 4 * g + k - 1)
                        link(nc.vector.tensor_tensor(ev[:, b, :], PS[0:HF, b * 512:(b + 1) * 512], leak[:, b, :], ALU.max))
                        link(nc.vector.tensor_copy(run[:, b, 0:1], run[:, b ^ 1, 512:513]))
                        link(nc.vector.tensor_tensor_scan(run[:, b, 1:513], negr[:, sl], ev[:, b, :], run[:, b, 0:1], ALU.add, ALU.max))
                        nc.vector.tensor_tensor(wt[:, b, :], ev[:, b, :], run[:, b, 1:513], ALU.subtract).then_inc(s_sub, 1)
                        link(nc.vector.tensor_tensor(dec[:, b, :], negr[:, sl], run[:, b, 0:512], ALU.add))
                        nc.vector.tensor_tensor(dec[:, b, :], dec[:, b, :], run[:, b, 1:513], ALU.subtract).then_inc(s_sub, 1)
                        wait_reg(e, s_exp, 8 * g + 2 * k + 2)
                        link(nc.vector.tensor_tensor(wt[:, b, :], wt[:, b, :], PS[0:HF, (2 + b) * 512:(3 + b) * 512], ALU.mult))
                        nc.vector.tensor_tensor_scan(acc[:, b, :], dec[:, b, :], wt[:, b, :], acc[:, b ^ 1, 511:512], ALU.mult, ALU.add).then_inc(s_acc, 1)
                        wait_reg(e, s_acc, 4 * g + k + 1)
                    assert n[0] == LINKS
                groups(e, body)

        NR = R[:, 6144:6144 + NT * ROW].rearrange("p (t r) -> p t r", r=ROW)
        c4r = sb("row_4095", [P, ROW])
        sm4 = [R[:, 7424 + i * 128:7424 + (i + 1) * 128].rearrange("p (t h) -> p t h", h=GH) for i in range(6)]
        AG = R[:, 8192:8704].rearrange("p (t f) -> p t f", f=GH * GE)
        A2 = R[:, 8704:9216].rearrange("p (t f) -> p t f", f=GH * GE)
        PB = sb("pos_blk", [D, H1, NREL])
        with ExitStack() as c6, nc.Block() as block:
            def sm(n):
                return c6.enter_context(nc.semaphore(n))
            s_ld, s_v, s_x, s_e, s_z, s_bank, s_zT, s_pp, s_pb = (sm("s_ld"), sm("s_v6"), sm("s_x6"), sm("s_e6"), sm("s_z6"), sm("s_bank6"),
                                                             sm("s_zT6"), sm("s_pp"), sm("s_pb"))
            es, ec, er, ss, cn, tm = sm4
            G4 = [P, NT, GH]
            G16 = [P, NT, GH, GE]

            @block.sync
            def _(e):
                e.dma_start(NR[:, :, :], nt_d.rearrange("(t p) r -> p t r", p=P)).then_inc(s_ld, 16)
                e.dma_start(c4r[:, :], ts_d[M - 1:M, :].to_broadcast([P, ROW])).then_inc(s_ld, 16)

            @block.scalar
            def _(e):
                for i in (0, 1, 2):
                    e.wait_ge(s_x, i + 1)
                    t = (es, ec, er)[i]
                    nc.scalar.activation(t[:, :, :], t[:, :, :], ACT.Exp).then_inc(s_e, 1)
                root(e, NT)
                e.wait_ge(s_x, 4)
                nc.scalar.activation(sm4[3][:, :, :], sm4[3][:, :, :], ACT.Exp).then_inc(s_e, 1)
                e.wait_ge(s_pp, 1)
                for h in range(H1):
                    hc = consts[0:D, CCST["hcol"][0] + h:CCST["hcol"][0] + h + 1]
                    nc.scalar.mul(PB[:, h, :], PS[0:D, 0:NREL], hc).then_inc(s_pb, 1)
                root(e, NT)
                root(e, NT)
                copy_zT(e, s_bank, 0, s_zT)

            @block.tensor
            def _(e):
                nc.tensor.matmul(PS[0:D, 0:NREL], W65("Wpos"), W65("enc"), start=True, stop=True).then_inc(s_pp, 1)
                e.wait_ge(s_pb, H1)
                transpose_z(e, s_z, s_bank, None, 1)

            @block.vector
            def _(e):
                ch = Chain(e, s_v)
                V = nc.vector
                e.wait_ge(s_ld, 32)
                ch.link(V.tensor_tensor(es[:, :, :], as_[:, :, :], ad_[:, :, :], ALU.add))
                ch.link(V.tensor_tensor(ec[:, :, :], ad_[:, :, :], spread(c4r[:, 16:20], 1, G4), ALU.add))
                for t in (es, ec):
                    ch.link(V.tensor_scalar(tm[:, :, :], t[:, :, :], 0.2, None, ALU.mult))
                    ch.link(V.tensor_tensor(t[:, :, :], t[:, :, :], tm[:, :, :], ALU.max))
                ch.link(V.tensor_scalar(cn[:, :, 0], cnt[:, :], 0.5, 1.0, ALU.is_ge, ALU.subtract))
                ch.link(V.tensor_scalar(cn[:, :, 0], cn[:, :, 0], BIG, None, ALU.mult))
                ch.link(V.tensor_tensor(ec[:, :, :], ec[:, :, :], cn[:, :, 0:1].to_broadcast(G4), ALU.add))
                RM = NR[:, :, HF + 16:HF + 20]
                ch.link(V.tensor_tensor(tm[:, :, :], es[:, :, :], ec[:, :, :], ALU.max))
                ch.link(V.tensor_tensor(tm[:, :, :], tm[:, :, :], RM, ALU.max))
                V.tensor_tensor(es[:, :, :], es[:, :, :], tm[:, :, :], ALU.subtract).then_inc(s_x, 1)
                V.tensor_tensor(ec[:, :, :], ec[:, :, :], tm[:, :, :], ALU.subtract).then_inc(s_x, 1)
                V.tensor_tensor(er[:, :, :], RM, tm[:, :, :], ALU.subtract).then_inc(s_x, 1)
                e.wait_ge(s_e, 3)
                ch.link(V.tensor_tensor(ec[:, :, :], ec[:, :, :], spread(cnt[:, :], 2, G4), ALU.mult))
                ch.link(V.tensor_tensor(ss[:, :, :], es[:, :, :], ec[:, :, :], ALU.add))
                ch.link(V.tensor_tensor(tm[:, :, :], er[:, :, :], NR[:, :, 16:20], ALU.mult))
                ch.link(V.tensor_tensor(ss[:, :, :], ss[:, :, :], tm[:, :, :], ALU.add))
                ch.link(V.tensor_scalar(ss[:, :, :], ss[:, :, :], 1e-16, None, ALU.add))
                ch.link(V.reciprocal(ss[:, :, :], ss[:, :, :]))
                ag = AG[:, :, :].rearrange("p t (h e) -> p t h e", h=GH)
                a2 = A2[:, :, :].rearrange("p t (h e) -> p t h e", h=GH)
                ch.link(V.tensor_tensor(ag, HG[:, :, :].rearrange("p t (h e) -> p t h e", h=GH), spread(es[:, :, :], 3, G16), ALU.mult))
                c16 = spread(c4r[:, HF:HF + 16], 1, [P, NT, 16]).rearrange("p t (h e) -> p t h e", h=GH)
                ch.link(V.tensor_tensor(a2, c16, spread(ec[:, :, :], 3, G16), ALU.mult))
                ch.link(V.tensor_tensor(AG[:, :, :], AG[:, :, :], A2[:, :, :], ALU.add))
                ch.link(V.tensor_tensor(a2, NR[:, :, 0:16].rearrange("p t (h e) -> p t h e", h=GH), spread(er[:, :, :], 3, G16), ALU.mult))
                ch.link(V.tensor_tensor(AG[:, :, :], AG[:, :, :], A2[:, :, :], ALU.add))
                ch.link(V.tensor_tensor(ag, ag, spread(ss[:, :, :], 3, G16), ALU.mult))
                ch.link(V.tensor_tensor(AG[:, :, :], AG[:, :, :], spread(RO("bgat"), 1, [P, NT, 16]), ALU.add))
                m, v = mean[:, 0:NT], var[:, 0:NT]
                ch.link(V.reduce_sum(m, AG[:, :, :], AX.X))
                ch.link(V.tensor_scalar(m, m, -1.0 / 16, None, ALU.mult))
                ch.link(V.tensor_tensor(AG[:, :, :], AG[:, :, :], spread(m, 2, [P, NT, 16]), ALU.add))
                ch.link(V.tensor_tensor(A2[:, :, :], AG[:, :, :], AG[:, :, :], ALU.mult))
                ch.link(V.reduce_sum(v, A2[:, :, :], AX.X))
                n_ln[0] += 1
                V.tensor_scalar(v, v, 1.0 / 16, EPS, ALU.mult, ALU.add).then_inc(s_ln, 1)
                e.wait_ge(s_std, n_ln[0])
                ch.link(V.reciprocal(v, v))
                ch.link(V.tensor_tensor(AG[:, :, :], AG[:, :, :], spread(v, 2, [P, NT, 16]), ALU.mult))
                ch.link(V.tensor_tensor(AG[:, :, :], AG[:, :, :], spread(RO("lng"), 1, [P, NT, 16]), ALU.mult))
                ch.link(V.tensor_tensor(AG[:, :, :], AG[:, :, :], spread(RO("lnb"), 1, [P, NT, 16]), ALU.add))
                sc = sm4[3][:, :, :]
                ch.link(V.reduce_sum(sc, AG[:, :, :].rearrange("p t (h e) -> p t e h", h=GH), AX.X))
                ch.link(V.tensor_scalar(sc, sc, 1.0 / GH, None, ALU.mult))
                gating(e, ch, sc, GE, CS("lowa"), s_x, s_e, 4)
                for i in range(GE):
                    ch.link(V.tensor_tensor(s3, Y[i], sc[:, :, i:i + 1].to_broadcast(PT), ALU.mult))
                    ch.link(V.tensor_tensor(Ht[:, :], Ht[:, :], St[:, :], ALU.add))
                layernorm(e, ch, h3, z3, NT, D)
                layernorm(e, ch, z3, z3, NT, D)
                ch.link(V.tensor_tensor(z3, z3, spread(RO("g1"), 1, PT), ALU.mult))
                V.tensor_tensor(z3, z3, spread(RO("be1"), 1, PT), ALU.add).then_inc(s_z, 1)

        base = 0

        def take(n):
            nonlocal base
            base += n
            return R[:, base - n:base]
        QU = [take(512)[0:D, :] for _ in (0, 1)]
        QV = [take(512)[0:D, :] for _ in (0, 1)]
        KB = [take(2048)[0:D, :].rearrange("p (i h s) -> p i h s", i=8, h=H1) for _ in (0, 1)]
        VB = [take(512).rearrange("p (i d) -> p i d", i=8) for _ in (0, 1)]
        RB = [take(4 * H1 * NREL).rearrange("p (t x) -> p t x", t=4) for _ in (0, 1)]
        PO = [take(1024) for _ in (0, 1)]
        SC = [take(1024) for _ in (0, 1)]
        AT = [take(1024) for _ in (0, 1)]
        CT = [take(512)[0:D + 1, :] for _ in (0, 1)]
        mx, sm_ = sb("row_max", [P, 16]), sb("row_sum", [P, 16])
        assert base <= 20480
        with ExitStack() as c7, nc.Block() as block:
            def sm(n):
                return c7.enter_context(nc.semaphore(n))
            names = ["s_q", "s_k", "s_vp", "s_rp", "s_proj", "s_kb", "s_vb", "s_rb", "s_skew", "s_scp", "s_sx", "s_se", "s_at", "s_atp",
                     "s_atc", "s_cp", "s_ct", "s_op", "s_h7", "s_v7", "s_one"]
            S = {n: sm(n) for n in names}
            s_pos = [sm("s_pos0"), sm("s_pos1")]
            s_rbo = [sm("s_rbo0"), sm("s_rbo1")]

            @block.tensor
            def _(e):
                T = nc.tensor

                def project(g):
                    cols = slice(g * 512, (g + 1) * 512)
                    if g:
                        e.wait_ge(S["s_proj"], 2 * g)
                        e.wait_ge(S["s_kb"], H1 * g)
                        e.wait_ge(S["s_vb"], g)
                    T.matmul(PS[0:D, 0:512], W65("Wq"), ZT[:, cols], start=True, stop=True).then_inc(S["s_q"], 1)
                    T.matmul(PS[0:D, 512:1024], W65("Wk"), ZT[:, cols], start=True, stop=True).then_inc(S["s_k"], 1)
                    for i in range(8):
                        for r in (0, 64):
                            ins = T.matmul(PS[r:r + 64, 1024 + i * D:1024 + (i + 1) * D],
                                           ZT[:, g * 512 + i * 64:g * 512 + (i + 1) * 64], W65("Wv"), start=True, stop=True)
                    ins.then_inc(S["s_vp"], 1)
                    e.wait_ge(S["s_proj"], 2 * g + 2)
                    for j in range(4):
                        n = 4 * g + j
                        if n:
                            e.wait_ge(S["s_rb"], n)
                        T.matmul(PS[:, 1536:1536 + H1 * NREL], QV[g % 2][:, j * P:(j + 1) * P],
                                 PB[:, :, :].rearrange("p h r -> p (h r)"), start=True, stop=True).then_inc(S["s_rp"], 1)

                def attend(g):
                    b = g % 2
                    e.wait_ge(S["s_kb"], H1 * (g + 1))
                    if g:
                        e.wait_ge(S["s_sx"], 4 * g)
                    for i in range(8):
                        o = PS[64 * (i % 2):64 * (i % 2) + 64, 2048 + (i // 2) * 256:2048 + (i // 2 + 1) * 256]
                        ins = T.matmul(o, QU[b][:, i * 64:(i + 1) * 64], KB[b][:, i, :, :].rearrange("p h s -> p (h s)"), start=True, stop=True)
                        if i % 4 == 3:
                            ins.then_inc(S["s_scp"], 1)
                    e.wait_ge(S["s_at"], g + 1)
                    if g:
                        e.wait_ge(S["s_op"], g)
                        e.wait_ge(S["s_h7"], g)
                    for t in range(8):
                        o = PS[:, 3072 + t * P:3072 + (t + 1) * P]
                        ins = T.transpose(o, SC[b][:, t * P:(t + 1) * P], ident)
                        if t % 4 == 3:
                            ins.then_inc(S["s_atp"], 1)
                    e.wait_ge(S["s_atc"], 2 * g + 2)
                    e.wait_ge(S["s_vb"], g + 1)
                    for i in range(8):
                        for hp in range(2):
                            at = AT[b][:, ((i // 2) * 2 + hp) * P + (i % 2) * 64:((i // 2) * 2 + hp) * P + (i % 2) * 64 + 64]
                            ins = T.matmul(PS[hp * 32:(hp + 1) * 32, 3072 + i * 64:3072 + (i + 1) * 64], VB[b][:, i, hp * 32:(hp + 1) * 32], at,
                                           start=True, stop=True)
                    ins.then_inc(S["s_cp"], 1)
                    e.wait_ge(S["s_ct"], g + 1)
                    for j in range(4):
                        ins = T.matmul(PS[:, 3584 + j * D:3584 + (j + 1) * D], CT[b][:, j * P:(j + 1) * P], W65("Wo"), start=True, stop=True)
                    ins.then_inc(S["s_op"], 1)
                e.wait_ge(S["s_one"], 2)
                project(0)
                for g in range(8):
                    if g < 7:
                        project(g + 1)
                    attend(g)

            @block.scalar
            def _(e):
                A = nc.scalar

                def project(g):
                    b = g % 2
                    if g >= 2:
                        e.wait_ge(S["s_scp"], 2 * (g - 1))
                    e.wait_ge(S["s_q"], g + 1)
                    if g >= 2:
                        e.wait_ge(S["s_rp"], 4 * (g - 1))
                    u = w65s[0:D, C65["u"][0]:C65["u"][1]]
                    v = w65s[0:D, C65["v"][0]:C65["v"][1]]
                    A.activation(QU[b], PS[0:D, 0:512], ACT.Identity, bias=u).then_inc(S["s_proj"], 1)
                    A.activation(QV[b], PS[0:D, 0:512], ACT.Identity, bias=v).then_inc(S["s_proj"], 1)
                    e.wait_ge(S["s_k"], g + 1)
                    for h in range(H1):
                        hc = consts[0:D, CCST["hcol"][0] + h:CCST["hcol"][0] + h + 1]
                        A.mul(KB[b][:, :, h, :], PS[0:D, 512:1024].rearrange("p (i s) -> p i s", i=8), hc).then_inc(S["s_kb"], 1)
                    for j in range(4):
                        n = 4 * g + j
                        e.wait_ge(S["s_rp"], n + 1)
                        if g >= 2:
                            e.wait_ge(s_rbo[b], 64 * (g // 2))
                        A.copy(RB[b][:, j, :], PS[:, 1536:1536 + H1 * NREL]).then_inc(S["s_rb"], 1)

                def attend(g):
                    b = g % 2
                    e.wait_ge(S["s_se"], g + 1)
                    A.activation(SC[b], SC[b], ACT.Exp, scale=HD1 ** -0.5).then_inc(S["s_skew"], 1)
                    for i in (0, 1):
                        e.wait_ge(S["s_atp"], 2 * g + i + 1)
                        if g >= 2:
                            e.wait_ge(S["s_cp"], g - 1)
                        A.copy(AT[b][:, i * 512:(i + 1) * 512], PS[:, 3072 + i * 512:3072 + (i + 1) * 512]).then_inc(S["s_atc"], 1)
                    e.wait_ge(S["s_cp"], g + 1)
                    if g >= 2:
                        e.wait_ge(S["s_op"], g - 1)
                    A.copy(CT[b][0:D, :], PS[0:D, 3072:3584]).then_inc(S["s_ct"], 1)
                project(0)
                for g in range(8):
                    if g < 7:
                        project(g + 1)
                    attend(g)

            @block.sync
            def _(e):
                for g in range(8):
                    b = g % 2
                    for j in range(4):
                        n = 4 * g + j
                        e.wait_ge(S["s_rb"], n + 1)
                        e.dma_start(skew_d[n * P * H1 * NREL:(n + 1) * P * H1 * NREL].rearrange("(p x) -> p x", p=P), RB[b][:, j, :]).then_inc(s_rbo[b], 16)
                    e.wait_ge(s_rbo[b], 64 * (g // 2 + 1))
                    if g >= 2:
                        e.wait_ge(S["s_sx"], 4 * (g - 1))
                    for i in range(8):
                        tok0 = g * 512 + i * 64
                        src = bass.AP(tensor=skew_d.tensor, offset=tok0 * H1 * NREL + NTOK - 1,
                                      ap=[[H1 * NREL - 1, 64], [NREL, H1], [1, 64]])
                        dst = PO[b][64 * (i % 2):64 * (i % 2) + 64, (i // 2) * 256:(i // 2 + 1) * 256].rearrange("p (h s) -> p h s", h=H1)
                        e.dma_start(dst, src).then_inc(s_pos[b], 16)

            @block.vector
            def _(e):
                ch = Chain(e, S["s_v7"])
                V = nc.vector
                for b in (0, 1):
                    V.memset(CT[b][D:D + 1, :], 1.0).then_inc(S["s_one"], 1)

                def values(g):
                    e.wait_ge(S["s_vp"], g + 1)
                    if g >= 2:
                        e.wait_ge(S["s_cp"], g - 1)
                    V.tensor_tensor(VB[g % 2], PS[:, 1024:1536].rearrange("p (i d) -> p i d", i=8),
                                    spread(CS("vmask"), 1, [P, 8, D]), ALU.mult).then_inc(S["s_vb"], 1)

                def attend(g):
                    b = g % 2
                    sc3 = SC[b].rearrange("p (r s) -> p r s", s=64)
                    R3 = [P, 16, 64]
                    e.wait_ge(s_pos[b], 128 * (g // 2 + 1))
                    e.wait_ge(S["s_scp"], 2 * g + 2)
                    if g >= 2:
                        e.wait_ge(S["s_atp"], 2 * (g - 1))
                    for i in (0, 1):
                        V.tensor_tensor(SC[b][:, i * 512:(i + 1) * 512], PS[:, 2048 + i * 512:2048 + (i + 1) * 512],
                                        PO[b][:, i * 512:(i + 1) * 512], ALU.add).then_inc(S["s_sx"], 2)
                    e.wait_ge(S["s_sx"], 4 * g + 4)
                    ch.link(V.reduce_max(mx[:, :], sc3, AX.X))
                    V.tensor_tensor(sc3, sc3, spread(mx[:, :], 2, R3), ALU.subtract).then_inc(S["s_se"], 1)
                    e.wait_ge(S["s_skew"], g + 1)
                    ch.link(V.reduce_sum(sm_[:, :], sc3, AX.X))
                    ch.link(V.reciprocal(sm_[:, :], sm_[:, :]))
                    V.tensor_tensor(sc3, sc3, spread(sm_[:, :], 2, R3), ALU.mult).then_inc(S["s_at"], 1)
                    e.wait_ge(S["s_op"], g + 1)
                    V.tensor_tensor(h3[:, 4 * g:4 * g + 4, :], h3[:, 4 * g:4 * g + 4, :],
                                    PS[:, 3584:3584 + 256].rearrange("p (t d) -> p t d", d=D), ALU.add).then_inc(S["s_h7"], 1)
                values(0)
                for g in range(8):
                    if g < 7:
                        values(g + 1)
                    attend(g)

        hb = [R[:, 8192 + i * 512:8192 + (i + 1) * 512] for i in range(4)]
        tmp = R[:, 10240:10240 + 512]
        oa = Ct[:, :].rearrange("p (t d) -> p t d", d=D)
        with ExitStack() as c8, nc.Block() as block:
            def sm(n):
                return c8.enter_context(nc.semaphore(n))
            s_v, s_z, s_bank, s_zT, s_x, s_e, s_lg, s_hp, s_hs, s_yp, s_yc, s_fin, s_out = (
                sm("s_v8"), sm("s_z8"), sm("s_bank8"), sm("s_zT8"), sm("s_x8"), sm("s_e8"), sm("s_lg"), sm("s_hp8"), sm("s_hs8"),
                sm("s_yp8"), sm("s_yc"), sm("s_fin"), sm("s_out"))
            seq = [(g, x_) for g in range(8) for x_ in range(E1)]

            @block.tensor
            def _(e):
                T = nc.tensor
                transpose_z(e, s_z, s_bank, None, 1)
                e.wait_ge(s_zT, 8)
                for t in range(NT):
                    ins = T.matmul(PS[:, t * E1:(t + 1) * E1], ZT[:, t * P:(t + 1) * P], W65("Wg"), start=True, stop=True)
                ins.then_inc(s_lg, 1)
                w1 = W65("W1b", D).rearrange("p (e f) -> p e f", e=E1)
                w2 = W128("W2b").rearrange("p (e c d) -> p e c d", e=E1, c=FC1)

                def up(n):
                    g, x_ = seq[n]
                    for c in range(FC1):
                        q = 2 * n + c
                        if q >= 4:
                            e.wait_ge(s_hs, q - 3)
                        T.matmul(bank(1 + q % 4), w1[:, x_, c * P:(c + 1) * P], ZT[0:D, g * 512:(g + 1) * 512], start=True, stop=True).then_inc(s_hp, 1)

                def down(n):
                    g, x_ = seq[n]
                    e.wait_ge(s_hs, 2 * n + 2)
                    if n >= 2:
                        e.wait_ge(s_yc, n - 1)
                    b2 = rows[0:1, CROW["b2b"][0] + x_ * D:CROW["b2b"][0] + (x_ + 1) * D]
                    for j in range(4):
                        o = PS[:, (5 + n % 2) * 512 + j * D:(5 + n % 2) * 512 + (j + 1) * D]
                        for c in range(FC1):
                            T.matmul(o, hb[(2 * n + c) % 4][:, j * P:(j + 1) * P], w2[:, x_, c, :], start=(c == 0), stop=False)
                        ins = T.matmul(o, ones[0:1, :], b2, start=False, stop=True)
                    ins.then_inc(s_yp, 1)
                up(0)
                for n in range(len(seq)):
                    if n + 1 < len(seq):
                        up(n + 1)
                    down(n)

            @block.scalar
            def _(e):
                root(e, NT)
                copy_zT(e, s_bank, 0, s_zT)
                e.wait_ge(s_x, 1)
                nc.scalar.activation(gates[:, :, :], gates[:, :, :], ACT.Exp).then_inc(s_e, 1)
                for n, (g, x_) in enumerate(seq):
                    for c in range(FC1):
                        q = 2 * n + c
                        e.wait_ge(s_hp, q + 1)
                        if q >= 4:
                            e.wait_ge(s_yp, n - 1)
                        nc.scalar.activation(hb[q % 4], bank(1 + q % 4), ACT.Gelu,
                                             bias=w128s[:, C128["b1b"][0] + x_ * FC1 + c:C128["b1b"][0] + x_ * FC1 + c + 1]).then_inc(s_hs, 1)

            @block.vector
            def _(e):
                ch = Chain(e, s_v)
                V = nc.vector
                layernorm(e, ch, h3, z3, NT, D)
                V.tensor_copy(oa, h3).then_inc(s_z, 1)
                e.wait_ge(s_lg, 1)
                ch.link(V.tensor_copy(gates[:, :, :], PS[:, 0:NT * E1].rearrange("p (t e) -> p t e", e=E1)))
                gating(e, ch, gates[:, :, :], E1, CS("lowb"), s_x, s_e, 1)
                for n, (g, x_) in enumerate(seq):
                    e.wait_ge(s_yp, n + 1)
                    t = tmp[:, (n % 2) * 256:(n % 2) * 256 + 256].rearrange("p (t d) -> p t d", d=D)
                    V.tensor_tensor(t, PS[:, (5 + n % 2) * 512:(5 + n % 2) * 512 + 256].rearrange("p (t d) -> p t d", d=D),
                                    gates[:, 4 * g:4 * g + 4, x_:x_ + 1].to_broadcast([P, 4, D]), ALU.mult).then_inc(s_yc, 1)
                    e.wait_ge(s_yc, n + 1)
                    ch.link(V.tensor_tensor(oa[:, 4 * g:4 * g + 4, :], oa[:, 4 * g:4 * g + 4, :], t, ALU.add))
                    if x_ == E1 - 1:
                        V.tensor_copy(t[:, 0:1, 0:1], t[:, 0:1, 0:1]).then_inc(s_fin, 1)

            @block.sync
            def _(e):
                for g in range(8):
                    e.wait_ge(s_fin, g + 1)
                    e.dma_start(out[g * 512:(g + 1) * 512, :].rearrange("(t p) d -> p t d", p=P), oa[:, 4 * g:4 * g + 4, :]).then_inc(s_out, 16)
                e.wait_ge(s_out, 128)


def kernel(**inputs):
    import numpy as np
    import concourse.bacc as bacc
    from concourse.bass_utils import run_bass_kernel_spmd

    a = {k: np.asarray(v) for k, v in inputs.items()}
    f = np.float32

    x = a["x"].reshape(NIMG, 3, 8, 16, 8, 16).transpose(1, 3, 5, 0, 2, 4).reshape(KC, P, M).transpose(1, 0, 2)

    def pad(m, n=D + 1):
        return np.concatenate([m, np.zeros((n - m.shape[0], m.shape[1]), f)], 0)

    def with_bias(w, b):
        return np.concatenate([w, b.reshape(1, -1)], 0)

    n = np.arange(NTOK)
    grid = np.stack([n // 8, n % 8]).astype(f) / f(7)
    grid = np.concatenate([np.concatenate([grid, np.ones((1, NTOK), f)], 0)] * 2, 1)
    rel = np.arange(61, dtype=f)[:, None] * np.exp(np.arange(0, D, 2, dtype=f) * f(-np.log(10000.0) / D))
    enc = np.stack([np.sin(rel), np.cos(rel)], -1).reshape(61, D).astype(f)
    enc = enc[np.clip(np.arange(-NTOK + 1, NTOK), -30, 30) + 30].T
    enc = np.concatenate([enc, np.ones((1, NREL), f)], 0)
    p = np.arange(P)
    heads = np.arange(D) // HD1
    c = {
        "ident": np.eye(P, dtype=f),
        "sign": np.stack([1 - 2 * ((p >> b) & 1) for b in range(7)], 1).astype(f),
        "iota": np.tile(np.arange(D, dtype=f), (P, 1)),
        "kvmask": pad(np.tile((np.arange(D)[:, None] // HC0 == np.arange(D) // HC0).astype(f) / f(NTOK), (1, 2)), P),
        "hcol": pad((heads[:, None] == np.arange(H1)).astype(f), P),
        "vmask": (heads[None, :] % 2 == (p[:, None] // 64)).astype(f),
        "lowa": np.tile(np.tril(np.ones((GE, GE), f), -1).reshape(1, -1), (P, 1)),
        "lowb": np.tile(np.tril(np.ones((E1, E1), f), -1).reshape(1, -1), (P, 1)),
    }
    g = a
    w65 = {
        "pos1": pad(np.concatenate([g["L0_tok_W1"], g["L0_tok_b1"][None], np.zeros((D - 3, D), f), g["L0_tok_bp"][None]], 0)),
        "pos2": with_bias(g["L0_tok_W2"], g["L0_tok_b2"]),
        "Wgat": pad(g["L0_ffn_W_gat"]),
        "W1a": pad(g["L0_ffn_W1"].transpose(1, 0, 2).reshape(D, -1)),
        "Wq": with_bias(g["L1_attn_Wq"].T, g["L1_attn_bq"]),
        "Wk": with_bias(g["L1_attn_Wk"].T, g["L1_attn_bk"]),
        "Wv": with_bias(g["L1_attn_Wv"].T, g["L1_attn_bv"]),
        "Wpos": with_bias(g["L1_attn_Wpos"].T, g["L1_attn_bpos"]),
        "Wo": with_bias(g["L1_attn_Wo"].T, g["L1_attn_bo"]),
        "Wg": with_bias(g["L1_ffn_Wg"], g["L1_ffn_bg"]),
        "u": pad(g["L1_attn_u_bias"].reshape(D, 1)),
        "v": pad(g["L1_attn_v_bias"].reshape(D, 1)),
        "W1b": pad(g["L1_ffn_W1"].transpose(1, 0, 2).reshape(D, -1)),
        "enc": enc,
        "grid": pad(grid),
    }
    w128 = {
        "Wp": g["L0_tok_Wp"].reshape(KC, P, D).transpose(1, 0, 2).reshape(P, -1),
        "W2a": g["L0_ffn_W2"].transpose(1, 0, 2).reshape(P, -1),
        "b1a": g["L0_ffn_b1"].T,
        "W2b": g["L1_ffn_W2"].reshape(E1, FC1, P, D).transpose(2, 0, 1, 3).reshape(P, -1),
        "b1b": g["L1_ffn_b1"].reshape(E1 * FC1, P).T,
    }
    wrow = {
        "kw": g["L0_attn_kln_weight"], "kb": g["L0_attn_kln_bias"],
        "vw": g["L0_attn_vln_weight"], "vb": g["L0_attn_vln_bias"],
        "asrc": g["L0_ffn_att_src"], "adst": g["L0_ffn_att_dst"], "bgat": g["L0_ffn_b_gat"],
        "lng": g["L0_ffn_ln_gamma"], "lnb": g["L0_ffn_ln_beta"], "g1": g["L1_attn_ln_gamma"], "be1": g["L1_attn_ln_beta"],
        "b2a": g["L0_ffn_b2"], "b2b": g["L1_ffn_b2"],
    }

    def packed(parts, widths):
        for k, w in widths.items():
            assert parts[k].shape[1] == w, (k, parts[k].shape, w)
        return np.ascontiguousarray(np.concatenate([parts[k] for k in widths], 1))
    arrays = {
        "pixels": np.ascontiguousarray(x),
        "edge_list": np.ascontiguousarray(a["L0_ffn_edge_index"]),
        "w128": packed(w128, PK128), "w65": packed(w65, PK65),
        "wrow": packed({k: v.reshape(1, -1) for k, v in wrow.items()}, PROW),
        "consts": packed(c, CST),
    }
    nc = bacc.Bacc("TRN2", target_bir_lowering=False, num_devices=1)
    args = [nc.dram_tensor(k, v.shape, mybir.dt.from_np(v.dtype), kind="ExternalInput").ap() for k, v in arrays.items()]
    out = nc.dram_tensor("out", (M, D), F32, kind="ExternalOutput").ap()
    vit_tower(nc, *args, out)
    r = run_bass_kernel_spmd(nc, [arrays], core_ids=[0])
    return r.results[0]["out"].reshape(NIMG, NTOK, D)
```

```python
from contextlib import ExitStack

import concourse.bass as bass
from concourse import mybir

F32 = mybir.dt.float32
I32 = mybir.dt.int32
BF16 = mybir.dt.bfloat16
ALU = mybir.AluOpType
ACT = mybir.ActivationFunctionType
AX = mybir.AxisListType

P = 128
D = 64
NIMG = 64
NTOK = 64
M = NIMG * NTOK
NT = M // P
KP = 3 * 16 * 16
KC = KP // P
NE = 262144
EC = NE // P
H0, HC0 = 8, 8
GH, GE = 4, 4
F0 = 128
H1, HD1 = 4, 16
E1, F1 = 8, 256
FC1 = F1 // P
EPS = 1e-5
BIG = 1e30
PAD = float(1 << 24)
ROW = 2 * (GH * GE + GH)
HF = ROW // 2
NUP = E1 + E1 * F1
NREL = 2 * NTOK - 1
CUTS = ((32, 16), (128, 32), (EC, 256))
STEP = 512

PK128 = {"Wp": KC * D, "W2a": GE * D, "W2b": E1 * FC1 * D, "b1b": E1 * FC1}
PK65 = {"pos1": D, "pos2": D, "Wgat": GH * GE, "W1a": GE * F0, "Wq": D, "Wk": D, "Wv": D, "Wpos": D,
        "Wo": D, "u": 1, "v": 1, "enc": NREL, "grid": P, "b2b": D}
PROW = {"kw": D, "kb": D, "vw": D, "vb": D, "asrc": GH * GE, "adst": GH * GE, "bgat": GH * GE,
        "lng": GH * GE, "lnb": GH * GE, "g1": D, "be1": D, "b2a": GE * D, "bg": E1}
CST = {"ident": P, "sign": 7, "iota": D, "kvmask": P, "hcol": H1, "vmask": D, "lowa": GE * GE,
       "lowb": E1 * E1, "pick": E1, "fold": D, "lane": 1, "hi4": 1, "head": HF}


def columns(widths):
    at, out = 0, {}
    for name, w in widths.items():
        out[name] = (at, at + w)
        at += w
    return out, at


C128, N128 = columns(PK128)
C65, N65 = columns(PK65)
CROW, NROW = columns(PROW)
CCST, NCST = columns(CST)


def spread(ap, dim, shape):
    return ap.unsqueeze(dim).to_broadcast(shape)


def wait_reg(eng, sem, value):
    eng.wait_ge(sem, value)
    eng.nop(nofuse=True)


class Chain:

    def __init__(self, eng, sem):
        self.eng, self.sem, self.n = eng, sem, 0

    def link(self, ins):
        self.n += 1
        ins.then_inc(self.sem, 1)
        self.eng.wait_ge(self.sem, self.n)


def vit_tower(nc, x, edges, w128, w65, wrow, w1b, cst, out):
    ctx = ExitStack()
    with ctx:
        def sb(name, shape, dt=F32):
            return ctx.enter_context(nc.sbuf_tensor(name, shape, dt))

        def sem(name):
            return ctx.enter_context(nc.semaphore(name))

        Ht = sb("h_run", [P, NT * D])
        Zt = sb("z_norm", [P, NT * D])
        Ct = sb("centred", [P, NT * D])
        St = sb("squares", [P, NT * D])
        zt_mem = sb("z_T", [P, M])
        ZT = zt_mem[0:D + 1, :]
        R = sb("arena", [P, 20480])
        w128s = sb("w128s", [P, N128])
        w65s = sb("w65s", [D + 1, N65])
        wup = sb("w_up", [P, NUP])
        wup3 = sb("w_up3", [P, 3, NUP], BF16)
        rows = sb("rows_s", [P, NROW])
        consts = sb("consts_s", [P, NCST])
        mean = sb("mean", [P, NT * H0])
        var = sb("var", [P, NT * H0])
        ones = sb("ones", [P, P])
        cnt = sb("cnt", [P, NT])
        as_ = sb("a_src", [P, NT, GH])
        ad_ = sb("a_dst", [P, NT, GH])
        HG = sb("h_gat", [P, NT, GH * GE])
        ad3 = sb("a_dst3", [P, 3, NT, GH], BF16)
        gates = sb("gates", [P, NT, E1])
        nreal = sb("n_real", [1, 2], I32)
        PS = ctx.enter_context(nc.psum_tensor("psum", [P, 4096], F32))

        h3 = Ht[:, :].rearrange("p (t d) -> p t d", d=D)
        z3 = Zt[:, :].rearrange("p (t d) -> p t d", d=D)
        c3 = Ct[:, :].rearrange("p (t d) -> p t d", d=D)
        s3 = St[:, :].rearrange("p (t d) -> p t d", d=D)

        def bank(b):
            return PS[:, b * 512:(b + 1) * 512]

        def W128(n):
            return w128s[:, C128[n][0]:C128[n][1]]

        def W65(n, k=D + 1):
            return w65s[0:k, C65[n][0]:C65[n][1]]

        def RO(n):
            return rows[:, CROW[n][0]:CROW[n][1]]

        def CS(n, k=P):
            return consts[0:k, CCST[n][0]:CCST[n][1]]

        ident = CS("ident")

        ts_d = nc.dram_tensor("src_rows", [M, ROW], F32).ap()
        nt_d = nc.dram_tensor("node_rows", [M, ROW], F32).ap()
        neg_d = nc.dram_tensor("restart_row", [NE + STEP], F32).ap()
        lo_row = nc.dram_tensor("dst_low_row", [NE + STEP], BF16).ap()
        hi_row = nc.dram_tensor("dst_high_row", [NE + STEP], BF16).ap()
        skew_d = nc.dram_tensor("skew", [M * H1 * NREL], F32).ap()

        keyA = R[:, 0:2048]
        keyB = R[:, 2048:4096]
        s_ln = sem("s_ln")
        s_std = sem("s_std")
        n_ln = [0]

        def layernorm(e, ch, xin, z, groups, width, unbiased=False):
            m, v = mean[:, 0:groups], var[:, 0:groups]
            cg = Ct[:, :].rearrange("p (g d) -> p g d", d=width)
            sg = St[:, :].rearrange("p (g d) -> p g d", d=width)
            ch.link(nc.vector.reduce_sum(m, xin, AX.X))
            ch.link(nc.vector.tensor_scalar(m, m, -1.0 / width, None, ALU.mult))
            ch.link(nc.vector.tensor_tensor(cg, xin, spread(m, 2, [P, groups, width]), ALU.add))
            ch.link(nc.vector.tensor_tensor(sg, cg, cg, ALU.mult))
            ch.link(nc.vector.reduce_sum(v, sg, AX.X))
            n_ln[0] += 1
            if unbiased:
                nc.vector.tensor_scalar(v, v, 1.0 / (width - 1), None, ALU.mult).then_inc(s_ln, 1)
            else:
                nc.vector.tensor_scalar(v, v, 1.0 / width, EPS, ALU.mult, ALU.add).then_inc(s_ln, 1)
            e.wait_ge(s_std, n_ln[0])
            if unbiased:
                ch.link(nc.vector.tensor_scalar(v, v, EPS, None, ALU.add))
            ch.link(nc.vector.reciprocal(v, v))
            ch.link(nc.vector.tensor_tensor(z, cg, spread(v, 2, [P, groups, width]), ALU.mult))

        n_root = [0]

        def root(e, groups):
            n_root[0] += 1
            e.wait_ge(s_ln, n_root[0])
            nc.scalar.sqrt(var[:, 0:groups], var[:, 0:groups]).then_inc(s_std, 1)

        def gating(e, ch, sc, n, low, s_x, s_e, k):
            A = R[:, 0:NT * n * n].rearrange("p (t i j) -> p t i j", i=n, j=n)
            B = R[:, 2048:2048 + NT * n * n].rearrange("p (t i j) -> p t i j", i=n, j=n)
            rank = R[:, 4096:4096 + NT * n].rearrange("p (t i) -> p t i", i=n)
            top = R[:, 4608:4608 + NT]
            full = [P, NT, n, n]
            xj, xi = spread(sc, 2, full), spread(sc, 3, full)
            nc.vector.tensor_tensor(A, xj, xi, ALU.is_gt).then_inc(ch.sem, 1)
            ch.n += 1
            ch.link(nc.vector.tensor_tensor(B, xj, xi, ALU.is_equal))
            lo = spread(low, 1, [P, NT, n * n]).rearrange("p t (i j) -> p t i j", i=n)
            ch.link(nc.vector.tensor_tensor(B, B, lo, ALU.mult))
            ch.link(nc.vector.tensor_tensor(A, A, B, ALU.add))
            ch.link(nc.vector.reduce_sum(rank, A, AX.X))
            ch.link(nc.vector.tensor_scalar(rank, rank, 1.5, None, ALU.is_lt))
            ch.link(nc.vector.reduce_max(top, sc, AX.X))
            nc.vector.tensor_tensor(sc, sc, spread(top, 2, [P, NT, n]), ALU.subtract).then_inc(s_x, 1)
            e.wait_ge(s_e, k)
            ch.link(nc.vector.tensor_tensor(sc, sc, rank, ALU.mult))
            ch.link(nc.vector.reduce_sum(top, sc, AX.X))
            ch.link(nc.vector.reciprocal(top, top))
            ch.link(nc.vector.tensor_tensor(sc, sc, spread(top, 2, [P, NT, n]), ALU.mult))

        def transpose_z(e, s_z, s_bank, s_free, z_count):
            e.wait_ge(s_z, z_count)
            for t in range(NT):
                ins = nc.tensor.transpose(PS[0:D, t * P:(t + 1) * P], z3[:, t, :], ident)
                if t % 4 == 3:
                    ins.then_inc(s_bank, 1)

        def copy_zT(e, s_bank, base, s_zT):
            for b in range(8):
                e.wait_ge(s_bank, base + b + 1)
                nc.scalar.copy(ZT[0:D, b * 512:(b + 1) * 512], PS[0:D, b * 512:(b + 1) * 512]).then_inc(s_zT, 1)

        xbuf = [R[:, 10240 + i * 3072:10240 + (i + 1) * 3072].rearrange("p (c t) -> p c t", c=KC) for i in (0, 1)]
        e_src = R[:, 4096:6144].bitcast(I32)
        e_dst = R[:, 6144:8192].bitcast(I32)
        lo_d = R[:, 8192:9216].bitcast(BF16)
        hi_d = R[:, 9216:10240].bitcast(BF16)
        one_lo = [Zt[:, :].bitcast(BF16).rearrange("p (l k) -> p l k", k=64),
                  Ct[:, :].bitcast(BF16).rearrange("p (l k) -> p l k", k=64)]
        one_hi = [St[:, :].bitcast(BF16).rearrange("p (l k) -> p l k", k=64),
                  R[:, 18432:20480].bitcast(BF16).rearrange("p (l k) -> p l k", k=64)]
        iota_lk = keyB.bitcast(BF16).rearrange("p (l k) -> p l k", k=64)
        pos_l = sb("pos_l", [D + 2, P])
        pos_r = sb("pos_r", [D + 2, D])
        rc = sb("real_count", [P, 2])
        blocks = sb("block_counts", [P, EC // CUTS[0][0]])
        dense = sb("dense", [P, 3])
        zeros = sb("zeros", [P, D], BF16)
        HB = EC // NT
        with ExitStack() as c1, nc.Block() as block:
            def sm(n):
                return c1.enter_context(nc.semaphore(n))
            s_pack, s_edge = sm("s_pack"), sm("s_edge")
            s_x = [sm("s_x0"), sm("s_x1")]
            s_xused, s_hid, s_posl, s_posones, s_ones = sm("s_xused"), sm("s_hid"), sm("s_posl"), sm("s_posones"), sm("s_ones")
            s_tok, s_v, s_hot, s_hotused, s_cnt, s_cntc, s_rc, s_rsum = (sm("s_tok"), sm("s_v1"), sm("s_hot"), sm("s_hotused"),
                                                                  sm("s_cnt"), sm("s_cntc"), sm("s_rc"), sm("s_rsum"))
            s_h = sm("s_h")
            NG = M // 512

            @block.sync
            def _(e):
                e.dma_start(e_src, edges[0, :].rearrange("(p c) -> p c", p=P)).then_inc(s_edge, 16)
                e.dma_start(e_dst, edges[1, :].rearrange("(p c) -> p c", p=P)).then_inc(s_edge, 16)
                for g in range(NG):
                    if g >= 2:
                        e.wait_ge(s_xused, g - 1)
                    e.dma_start(xbuf[g % 2], x[:, :, g * 512:(g + 1) * 512]).then_inc(s_x[g % 2], 16)

            @block.scalar
            def _(e):
                e.dma_start(consts[:, :], cst).then_inc(s_pack, 16)
                e.dma_start(w65s[:, :], w65).then_inc(s_pack, 16)
                e.dma_start(w128s[:, :], w128).then_inc(s_pack, 16)
                e.dma_start(rows[:, :], wrow.to_broadcast([P, NROW])).then_inc(s_pack, 16)
                e.dma_start(pos_r[0:D + 1, :], w65[:, C65["pos2"][0]:C65["pos2"][1]]).then_inc(s_pack, 16)
                e.dma_start(pos_r[D + 1:D + 2, :], w65[D:D + 1, C65["pos1"][0]:C65["pos1"][1]]).then_inc(s_pack, 16)
                for half in (0, 1):
                    e.dma_start(wup[half * D:(half + 1) * D, :], w1b).then_inc(s_pack, 16)
                e.wait_ge(s_hid, 1)
                nc.scalar.activation(pos_l[0:D, :], PS[0:D, 7 * 512:7 * 512 + P], ACT.Relu).then_inc(s_posl, 1)
                for b in range(4):
                    e.wait_ge(s_tok, b + 1)
                    nc.scalar.copy(Ht[:, b * 512:(b + 1) * 512], bank(b)).then_inc(s_h, 1)

            @block.tensor
            def _(e):
                e.wait_ge(s_pack, 128)
                nc.tensor.matmul(PS[0:D, 7 * 512:7 * 512 + P], W65("pos1", 3), W65("grid", 3),
                                 start=True, stop=True).then_inc(s_hid, 1)
                acc = PS[0:64, 4 * 512:4 * 512 + 64]
                wp = W128("Wp").rearrange("p (c d) -> p c d", c=KC)
                e.wait_ge(s_posl, 1)
                e.wait_ge(s_posones, 1)
                nc.tensor.matmul(acc, zeros[:, :], zeros[:, :], start=True, stop=False)
                with e.Fori(0, NG // 2) as i:
                    for j in range(8):
                        if j % 4 == 0:
                            wait_reg(e, s_x[j // 4], i * 16 + 16)
                        o = PS[:, bass.ds(i * 512 + j * D, D)]
                        for c in range(KC):
                            ins = nc.tensor.matmul(o, xbuf[j // 4][:, c, (j % 4) * P:(j % 4 + 1) * P], wp[:, c, :],
                                                   start=(c == 0), stop=False)
                        if j % 4 == 3:
                            ins.then_inc(s_xused, 1)
                        ins = nc.tensor.matmul(o, pos_l[:, :], pos_r[:, :], start=False, stop=True)
                        if j == 7:
                            ins.then_inc(s_tok, 1)
                        wait_reg(e, s_hot, i * 8 + (j + 1))
                        for k in range(HB):
                            ins = nc.tensor.matmul(acc, one_lo[j % 2][:, :, k], one_hi[j % 2][:, :, k], start=False, stop=False)
                        ins.then_inc(s_hotused, 1)
                nc.tensor.matmul(acc, zeros[:, :], zeros[:, :], start=False, stop=True).then_inc(s_cnt, 1)
                e.wait_ge(s_rc, 1)
                e.wait_ge(s_ones, 1)
                nc.tensor.matmul(PS[0:1, 6 * 512:6 * 512 + 2], ones[:, 0:1], rc[:, :], start=True, stop=True).then_inc(s_rsum, 1)

            @block.vector
            def _(e):
                ch = Chain(e, s_v)
                nc.vector.memset(zeros[:, :], 0.0)
                nc.vector.memset(pos_l[D:D + 2, :], 1.0).then_inc(s_posones, 1)
                nc.vector.memset(ones[:, :], 1.0).then_inc(s_ones, 1)
                nc.vector.memset(ZT[D:D + 1, :], 1.0)
                e.wait_ge(s_edge, 32)
                srcf, dstf = Zt[:, :], Ct[:, :]
                ch.link(nc.vector.tensor_copy(srcf, e_src))
                ch.link(nc.vector.tensor_copy(dstf, e_dst))
                ch.link(nc.vector.scalar_tensor_tensor(keyA, dstf, float(M), srcf, ALU.mult, ALU.add))
                ch.link(nc.vector.tensor_scalar(keyB, srcf, float(M - 1), PAD, ALU.is_ge, ALU.mult))
                ch.link(nc.vector.tensor_tensor(keyA, keyA, keyB, ALU.add))
                ch.link(nc.vector.tensor_scalar(keyA, keyA, PAD, None, ALU.min))
                ch.link(nc.vector.tensor_scalar(keyB, keyA, PAD, None, ALU.is_lt))
                ch.link(nc.vector.reduce_sum(rc[:, 0:1], keyB, AX.X))
                for i, (blk, keep) in enumerate(CUTS):
                    nb = EC // blk
                    ch.link(nc.vector.reduce_sum(blocks[:, 0:nb], keyB.rearrange("p (n b) -> p n b", b=blk), AX.X))
                    ch.link(nc.vector.reduce_max(dense[:, i:i + 1], blocks[:, 0:nb], AX.X))
                    ch.link(nc.vector.tensor_scalar(dense[:, i:i + 1], dense[:, i:i + 1], float(keep), None, ALU.is_gt))
                nc.vector.reduce_max(rc[:, 1:2], dense[:, :], AX.X).then_inc(s_rc, 1)
                lo_i, hi_i = St[:, :].bitcast(I32), R[:, 18432:20480].bitcast(I32)
                ch.link(nc.vector.tensor_scalar(lo_i, e_dst, 63, None, ALU.bitwise_and))
                ch.link(nc.vector.tensor_copy(lo_d, lo_i))
                ch.link(nc.vector.tensor_scalar(hi_i, e_dst, 6, None, ALU.arith_shift_right))
                ch.link(nc.vector.tensor_scalar(dstf, hi_i, 64.0, None, ALU.min))
                ch.link(nc.vector.tensor_scalar(srcf, srcf, float(M - 1), 64.0, ALU.is_lt, ALU.mult))
                ch.link(nc.vector.tensor_tensor(hi_d, dstf, srcf, ALU.add))
                e.wait_ge(s_pack, 128)
                ch.link(nc.vector.tensor_copy(iota_lk, spread(CS("iota"), 2, [P, 64, 64])))

                def hots(b, cols):
                    nc.vector.tensor_tensor(one_lo[b], spread(lo_d[:, cols], 1, [P, 64, HB]), iota_lk, ALU.is_equal)
                    nc.vector.tensor_tensor(one_hi[b], spread(hi_d[:, cols], 1, [P, 64, HB]), iota_lk,
                                            ALU.is_equal).then_inc(s_hot, 1)
                hots(0, slice(0, HB))
                hots(1, slice(HB, 2 * HB))
                with e.Fori(0, (EC // HB - 2) // 2) as i:
                    for j in (0, 1):
                        wait_reg(e, s_hotused, i * 2 + 1 + j)
                        hots(j, bass.ds((i * 2 + 2 + j) * HB, HB))
                e.wait_ge(s_cnt, 1)
                acc = PS[0:64, 4 * 512:4 * 512 + 64].rearrange("l (t b) -> l t b", b=2)
                nc.vector.tensor_copy(cnt[0:64, :], acc[:, :, 0])
                nc.vector.tensor_copy(cnt[64:128, :], acc[:, :, 1])
                e.wait_ge(s_rsum, 1)
                nc.vector.tensor_copy(nreal[:, :], PS[0:1, 6 * 512:6 * 512 + 2])

        kt = R[:, 10240:12288].rearrange("p (t d) -> p t d", d=D)
        vblk = R[:, 12288:16384].rearrange("p (t i d) -> p t i d", i=2, d=D)
        KV = R[0:D, 4096:8192].rearrange("p (t n) -> p t n", n=P)
        TS = R[:, 10240:10240 + NT * ROW].rearrange("p (t r) -> p t r", r=ROW)
        NI = R[:, 12288:12288 + NT * ROW].rearrange("p (t r) -> p t r", r=ROW)
        PT = [P, NT, D]
        with ExitStack() as c2, nc.Block() as block:
            def sm(n):
                return c2.enter_context(nc.semaphore(n))
            s_v, s_z, s_bank, s_zT, s_kv, s_kvp, s_kvc, s_o, s_hg, s_tab, s_out, s_zTf = (
                sm("s_v2"), sm("s_z"), sm("s_bank"), sm("s_zT"), sm("s_kv"), sm("s_kvp"), sm("s_kvc"), sm("s_o"),
                sm("s_hg"), sm("s_tab"), sm("s_tabout"), sm("s_zTf"))

            @block.vector
            def _(e):
                ch = Chain(e, s_v)
                nc.vector.memset(R[:, 12288:16384], 0.0).then_inc(s_v, 1)
                ch.n += 1
                layernorm(e, ch, h3, z3, NT, D)
                nc.vector.tensor_tensor(Ht[:, :], Ht[:, :], Zt[:, :], ALU.add).then_inc(s_z, 1)
                zg = Zt[:, :].rearrange("p (g d) -> p g d", d=HC0)
                layernorm(e, ch, zg, Ct[:, :].rearrange("p (g d) -> p g d", d=HC0), NT * H0, HC0, unbiased=True)
                ch.link(nc.vector.tensor_tensor(kt, c3, spread(RO("kw"), 1, PT), ALU.mult))
                ch.link(nc.vector.tensor_tensor(kt, kt, spread(RO("kb"), 1, PT), ALU.add))
                ch.link(nc.vector.tensor_tensor(s3, c3, spread(RO("vw"), 1, PT), ALU.mult))
                for i in (0, 1):
                    r = slice(64 * i, 64 * i + 64)
                    ins = nc.vector.tensor_tensor(vblk[r, :, i, :], s3[r, :, :],
                                                  spread(rows[r, CROW["vb"][0]:CROW["vb"][1]], 1, [64, NT, D]), ALU.add)
                ins.then_inc(s_kv, 1)
                for b in range(8):
                    e.wait_ge(s_kvp, b + 1)
                    nc.vector.tensor_tensor(KV[:, 4 * b:4 * b + 4, :], PS[0:D, b * 512:(b + 1) * 512].rearrange("p (t n) -> p t n", n=P),
                                            spread(CS("kvmask", D), 1, [D, 4, P]), ALU.mult).then_inc(s_kvc, 1)
                for b in range(8):
                    e.wait_ge(s_o, b + 1)
                    for i in (0, 1):
                        r = slice(64 * i, 64 * i + 64)
                        o = PS[r, b * 512:(b + 1) * 512].rearrange("p (t i d) -> p t i d", i=2, d=D)[:, :, i, :]
                        ins = nc.vector.tensor_tensor(h3[r, 4 * b:4 * b + 4, :], h3[r, 4 * b:4 * b + 4, :], o, ALU.add)
                        if (b, i) != (7, 1):
                            ins.then_inc(s_v, 1)
                            ch.n += 1
                ch.link(ins)
                layernorm(e, ch, h3, z3, NT, D)
                nc.vector.memset(NI[:, :, 0:HF], 0.0).then_inc(s_z, 1)
                nc.vector.memset(NI[:, :, HF:ROW], -BIG).then_inc(s_tab, 1)
                e.wait_ge(s_hg, 1)
                ch.link(nc.vector.tensor_copy(HG[:, :, :], bank(0).rearrange("p (t f) -> p t f", f=GH * GE)))
                G4 = [P, NT, GH, GE]
                for name, a, scratch in (("asrc", as_, s3), ("adst", ad_, c3)):
                    pr = scratch[:, :, 0:GH * GE]
                    ch.link(nc.vector.tensor_tensor(pr, HG[:, :, :], spread(RO(name), 1, [P, NT, GH * GE]), ALU.mult))
                    ch.link(nc.vector.reduce_sum(a[:, :, :], pr.rearrange("p t (h e) -> p t h e", h=GH), AX.X))
                nc.vector.tensor_copy(TS[:, :, 0:16].rearrange("p t (h e) -> p t h e", h=GH), spread(as_[:, :, :], 3, G4))
                nc.vector.tensor_copy(TS[:, :, 16:20], as_[:, :, :])
                low = s3[:, :, 0:GH]
                ch.link(nc.vector.tensor_copy(ad3[:, 0, :, :], ad_[:, :, :]))
                ch.link(nc.vector.tensor_tensor(low, ad_[:, :, :], ad3[:, 0, :, :], ALU.subtract))
                ch.link(nc.vector.tensor_copy(ad3[:, 1, :, :], low))
                ch.link(nc.vector.tensor_tensor(low, low, ad3[:, 1, :, :], ALU.subtract))
                ch.link(nc.vector.tensor_copy(ad3[:, 2, :, :], low))
                nc.vector.tensor_copy(TS[:, :, 20:36], HG[:, :, :])
                nc.vector.memset(TS[:, :, 36:40], 1.0).then_inc(s_tab, 1)

            @block.scalar
            def _(e):
                root(e, NT)
                root(e, NT * H0)
                copy_zT(e, s_bank, 0, s_zT)
                root(e, NT)
                copy_zT(e, s_bank, 8, s_zT)

            @block.tensor
            def _(e):
                transpose_z(e, s_z, s_bank, None, 1)
                e.wait_ge(s_kv, 1)
                for t in range(NT):
                    if t % 4 == 0:
                        e.wait_ge(s_zT, t // 4 + 1)
                    ins = nc.tensor.matmul(PS[0:D, t * P:(t + 1) * P], kt[:, t, :],
                                           vblk[:, t, :, :].rearrange("p i d -> p (i d)"), start=True, stop=True)
                    if t % 4 == 3:
                        ins.then_inc(s_kvp, 1)
                for t in range(NT):
                    if t % 4 == 0:
                        e.wait_ge(s_kvc, t // 4 + 1)
                    ins = nc.tensor.matmul(PS[:, t * P:(t + 1) * P], ZT[0:D, t * P:(t + 1) * P], KV[:, t, :], start=True, stop=True)
                    if t % 4 == 3:
                        ins.then_inc(s_o, 1)
                transpose_z(e, s_z, s_bank, None, 2)
                e.wait_ge(s_zT, 16)
                for t in range(NT):
                    ins = nc.tensor.matmul(PS[:, t * 16:(t + 1) * 16], ZT[0:D, t * P:(t + 1) * P], W65("Wgat", D), start=True, stop=True)
                ins.then_inc(s_hg, 1)

            @block.sync
            def _(e):
                e.wait_ge(s_tab, 1)
                e.dma_start(nt_d.rearrange("(t p) r -> p t r", p=P), NI).then_inc(s_out, 16)
                e.wait_ge(s_tab, 2)
                e.dma_start(ts_d.rearrange("(t p) r -> p t r", p=P), TS).then_inc(s_out, 16)
                e.wait_ge(s_out, 32)

        Y = [R[:, 10240 + i * 2048:10240 + (i + 1) * 2048].rearrange("p (t d) -> p t d", d=D) for i in range(GE)]
        hid = [sb(f"hid{i}", [P, 512]) for i in range(2)]
        keys = [keyA, keyB]

        def merges(bits, first, last, w):
            return [("swap", j, k if k < bits else None, w) for k in range(first, last + 1) for j in range(k - 1, -1, -1)]

        def across(bits, w):
            plan = [("sign", 0, w)] + [("swap", j, None, w) for j in range(bits - 1, -1, -1)] + [("sign", 0, w)]
            for k in range(bits + 1, bits + 8):
                b = k - bits if k < bits + 7 else None
                plan += [("turn", None, w)] + [("swap", j, b, w) for j in range(k - bits - 1, -1, -1)] + [("turn", b, w)]
                plan += [("swap", j, None, w) for j in range(bits - 1, -1, -1)]
                if b is not None:
                    plan += [("sign", b, w)]
            return plan
        full_plan = merges(11, 1, 10, EC) + across(11, EC)
        short_plan = (merges(11, 1, 5, 2048) + [("pack", 32, 16, 2048)]
                      + merges(11, 5, 6, 1024) + [("pack", 64, 32, 1024)]
                      + merges(9, 6, 9, 512) + across(8, 256))

        def walk(plan):
            cur = n = turned = signed = 0
            for it in plan:
                yield it, cur, n, turned, signed
                if it[0] == "swap":
                    n += 4 if it[2] is not None else 2
                    cur ^= 1
                elif it[0] == "pack":
                    n += 2
                    cur ^= 1
                elif it[0] == "sign":
                    signed += 1
                else:
                    turned += max(1, it[2] // 512)
                    cur ^= 1
            yield None, cur, n, turned, signed

        idxS = R[:, 4096:4096 + 2056].bitcast(I32)
        idxX = R[:, 6152:6152 + 2052].bitcast(I32)
        DF, SF, XF = Zt, Ct, St
        prevc, nextc, edgec = sb("prev_col", [P, 1]), sb("next_col", [P, 1]), sb("edge_col", [P, 1])
        tail_b = sb("tail_b", [1, STEP], BF16)
        tail_f = sb("tail_f", [1, STEP])
        same_t = R[:, 18432:20480]
        with ExitStack() as c3_, nc.Block() as block:
            def sm(n):
                return c3_.enter_context(nc.semaphore(n))
            s_swap, s_turn, s_back, s_sign = sm("s_swap"), sm("s_turn"), sm("s_back"), sm("s_sign")
            s_hp, s_hs, s_yp, s_y = sm("s_hp"), sm("s_hs"), sm("s_yp"), sm("s_y")
            s_v, s_d, s_shift, s_neg, s_rows, s_three, s_t, s_i, s_tail = (sm("s_v4"), sm("s_d"), sm("s_shift"), sm("s_neg"), sm("s_rows"),
                                                                   sm("s_three"), sm("s_t"), sm("s_i"), sm("s_tail"))

            def either(e, short, full):
                dense_ = e.value_load(nreal[0:1, 1:2], min_val=0, max_val=P)
                with e.If(dense_ < 1):
                    short()
                with e.If(dense_ > 0):
                    full()

            def sort_vector(e, plan):
                for it, cur, n, turned, signed in walk(plan):
                    if it is None:
                        e.wait_ge(s_swap, n)
                        return cur, n
                    src, dst = keys[cur][:, 0:it[-1]], keys[cur ^ 1][:, 0:it[-1]]
                    if it[0] == "swap":
                        _, j, k, w = it
                        if n:
                            e.wait_ge(s_swap, n)
                        if k is None:
                            pat, kw = "p (g two s) -> p g two s", dict(two=2, s=1 << j)
                            jobs = [(src.rearrange(pat, **kw), dst.rearrange(pat, **kw), ALU.min, ALU.max)]
                        else:
                            pat = "p (n up g two s) -> p n up g two s"
                            kw = dict(up=2, g=1 << (k - 1 - j), two=2, s=1 << j)
                            a, d = src.rearrange(pat, **kw), dst.rearrange(pat, **kw)
                            jobs = [(a[:, :, 0], d[:, :, 0], ALU.min, ALU.max), (a[:, :, 1], d[:, :, 1], ALU.max, ALU.min)]
                        for a, d, first, second in jobs:
                            ix = (slice(None),) * (len(a.shape) - 2)
                            lo, hi = a[ix + (0,)], a[ix + (1,)]
                            nc.vector.tensor_tensor(d[ix + (0,)], lo, hi, first).then_inc(s_swap, 1)
                            nc.vector.tensor_tensor(d[ix + (1,)], lo, hi, second).then_inc(s_swap, 1)
                    elif it[0] == "pack":
                        _, blk, keep, w = it
                        e.wait_ge(s_swap, n)
                        a = src.rearrange("p (n up b) -> p n up b", up=2, b=blk)
                        d = dst[:, 0:w * keep // blk].rearrange("p (n up b) -> p n up b", up=2, b=keep)
                        nc.vector.tensor_copy(d[:, :, 0], a[:, :, 0, 0:keep]).then_inc(s_swap, 1)
                        nc.vector.tensor_copy(d[:, :, 1], a[:, :, 1, blk - keep:]).then_inc(s_swap, 1)
                    elif it[0] == "sign":
                        e.wait_ge(s_sign, signed + 1)
                    else:
                        e.wait_ge(s_back, turned + max(1, it[2] // 512))

            NR3, TURNS = 8 * GE, 14
            AHEAD = NR3 - TURNS

            def between(step):
                def after(k):
                    step(AHEAD + k)
                    if k == TURNS - 1:
                        step(NR3)
                return after

            def expert_scalar(e):
                def step(i):
                    if i < NR3:
                        e.wait_ge(s_hp, i + 1)
                        if i >= 2:
                            e.wait_ge(s_yp, i - 1)
                        nc.scalar.activation(hid[i % 2][:, :], bank(4 + i % 2), ACT.Gelu).then_inc(s_hs, 1)
                    if i:
                        g, x_ = divmod(i - 1, GE)
                        e.wait_ge(s_yp, i)
                        nc.scalar.copy(Y[x_][:, 4 * g:4 * g + 4, :],
                                       PS[:, (6 + (i - 1) % 2) * 512:(6 + (i - 1) % 2) * 512 + 256].rearrange("p (t d) -> p t d", d=D)).then_inc(s_y, 1)
                return step

            def expert_tensor(e):
                w1 = W65("W1a").rearrange("p (e f) -> p e f", e=GE)
                w2 = W128("W2a").rearrange("p (e d) -> p e d", e=GE)

                def step(i):
                    if i < NR3:
                        g, x_ = divmod(i, GE)
                        if i >= 2:
                            e.wait_ge(s_hs, i - 1)
                        nc.tensor.matmul(bank(4 + i % 2), w1[:, x_, :], ZT[:, g * 512:(g + 1) * 512], start=True, stop=True).then_inc(s_hp, 1)
                    if i:
                        r = i - 1
                        x_ = r % GE
                        e.wait_ge(s_hs, i)
                        if r >= 2:
                            e.wait_ge(s_y, r - 1)
                        b2 = rows[0:1, CROW["b2a"][0] + x_ * D:CROW["b2a"][0] + (x_ + 1) * D]
                        o = PS[:, (6 + r % 2) * 512:(6 + r % 2) * 512 + 4 * D].rearrange("p (t d) -> p t d", d=D)
                        nc.tensor.matmul(o, ones[0:1, :], spread(b2, 1, [1, 4, D]), start=True, stop=False)
                        for j in range(4):
                            ins = nc.tensor.matmul(o[:, j, :], hid[r % 2][:, j * P:(j + 1) * P], w2[:, x_, :], start=False, stop=(j == 3))
                        ins.then_inc(s_yp, 1)
                return step

            def sort_scalar(e, plan, after):
                k = 0
                for it, cur, n, turned, signed in walk(plan):
                    if it is None:
                        return
                    if it[0] in ("sign", "turn") and it[1] is not None:
                        s = consts[:, CCST["sign"][0] + it[1]:CCST["sign"][0] + it[1] + 1]
                    if it[0] == "sign":
                        w = it[2]
                        e.wait_ge(s_swap, n)
                        nc.scalar.mul(keys[cur][:, 0:w], keys[cur][:, 0:w], s).then_inc(s_sign, 1)
                    elif it[0] == "turn":
                        w = min(it[2], 512)
                        for c in range(it[2] // w):
                            e.wait_ge(s_turn, turned + c + 1)
                            o, i_ = keys[cur ^ 1][:, c * w:(c + 1) * w], PS[:, c * w:(c + 1) * w]
                            if it[1] is None:
                                nc.scalar.copy(o, i_).then_inc(s_back, 1)
                            else:
                                nc.scalar.mul(o, i_, s).then_inc(s_back, 1)
                        after(k)
                        k += 1

            def sort_tensor(e, plan, after):
                k = 0
                for it, cur, n, turned, signed in walk(plan):
                    if it is None:
                        return
                    if it[0] == "turn":
                        w = it[2]
                        e.wait_ge(s_swap, n)
                        if signed:
                            e.wait_ge(s_sign, signed)
                        if turned:
                            e.wait_ge(s_back, turned)
                        per = min(w, 512) // P
                        for c in range(w // P):
                            ins = nc.tensor.transpose(PS[:, c * P:(c + 1) * P], keys[cur][:, c * P:(c + 1) * P], ident)
                            if c % per == per - 1:
                                ins.then_inc(s_turn, 1)
                        after(k)
                        k += 1

            def columns_vector(e, w, cur, n):
                ch = Chain(e, s_v)
                K, other = keys[cur][:, 0:w], keys[cur ^ 1][:, 0:w]
                ki, di, si = other.bitcast(I32), idxS[:, 0:w], idxX[:, 0:w]
                d, sf, xf, same = DF[:, 0:w], SF[:, 0:w], XF[:, 0:w], same_t[:, 0:w]
                nc.vector.memset(tail_b[:, :], 0.0)
                nc.vector.memset(tail_f[:, :], 0.0).then_inc(s_tail, 1)
                ch.link(nc.vector.tensor_copy(ki, K))
                ch.link(nc.vector.tensor_scalar(di, ki, 12, None, ALU.arith_shift_right))
                nc.vector.memset(prevc[:, :], -1.0)
                nc.vector.memset(nextc[:, :], -1.0)
                nc.vector.tensor_copy(d, di).then_inc(s_d, 1)
                ch.link(nc.vector.tensor_scalar(si, ki, M - 1, None, ALU.bitwise_and))
                nc.vector.tensor_copy(sf, si).then_inc(s_three, 1)
                e.wait_ge(s_d, 1)
                ch.link(nc.vector.tensor_tensor(same[:, 1:], d[:, 1:], d[:, :-1], ALU.is_equal))
                e.wait_ge(s_shift, 32)
                ch.link(nc.vector.tensor_tensor(same[:, 0:1], d[:, 0:1], prevc[:, :], ALU.is_equal))
                ch.link(nc.vector.tensor_tensor(edgec[:, :], d[:, w - 1:w], nextc[:, :], ALU.is_equal))
                nc.vector.scalar_tensor_tensor(xf[:, :-1], same[:, 1:], 8192.0, d[:, :-1], ALU.mult, ALU.add).then_inc(s_three, 1)
                nc.vector.scalar_tensor_tensor(xf[:, w - 1:w], edgec[:, :], 8192.0, d[:, w - 1:w], ALU.mult, ALU.add).then_inc(s_three, 1)
                lo_b, hi_b = K.bitcast(BF16)[:, 0:w], K.bitcast(BF16)[:, w:2 * w]
                ch.link(nc.vector.tensor_scalar(ki, di, P - 1, None, ALU.bitwise_and))
                ch.link(nc.vector.tensor_copy(lo_b, ki))
                ch.link(nc.vector.tensor_scalar(ki, di, 7, None, ALU.arith_shift_right))
                nc.vector.tensor_copy(hi_b, ki).then_inc(s_neg, 1)
                nc.vector.tensor_scalar(same, same, 1.0, BIG, ALU.subtract, ALU.mult).then_inc(s_neg, 1)
                e.wait_ge(s_three, 3)
                e.wait_ge(s_t, 3 * max(1, w // 512))
                nc.vector.memset(idxS[:, w:w + 8], 0)
                nc.vector.memset(idxX[:, 0:4], 8191)

            def columns_sync(e, w, cur):
                e.wait_ge(s_d, 1)
                with nc.allow_non_contiguous_dma(reason="one column, moved by a partition"):
                    e.dma_start(prevc[1:P, :], DF[0:P - 1, w - 1:w]).then_inc(s_shift, 16)
                    e.dma_start(nextc[0:P - 1, :], DF[1:P, 0:1]).then_inc(s_shift, 16)
                e.wait_ge(s_neg, 2)
                e.wait_ge(s_tail, 1)
                K = keys[cur][:, 0:w].bitcast(BF16)
                for row, a, tail in ((lo_row, K[:, 0:w], tail_b), (hi_row, K[:, w:2 * w], tail_b), (neg_d, same_t[:, 0:w], tail_f)):
                    e.dma_start(row[0:P * w].rearrange("(p c) -> p c", p=P), a).then_inc(s_rows, 16)
                    e.dma_start(row[P * w:P * w + STEP].unsqueeze(0), tail[:, :]).then_inc(s_rows, 16)
                e.wait_ge(s_rows, 96)

            def columns_tensor(e, w):
                nb = max(1, w // 512)
                e.wait_ge(s_three, 3)
                for i, a in enumerate((SF, XF)):
                    for c in range(w // P):
                        ins = nc.tensor.transpose(PS[:, i * 2048 + c * P:i * 2048 + (c + 1) * P], a[:, c * P:(c + 1) * P], ident)
                    ins.then_inc(s_t, nb + nb * i)

            def columns_scalar(e, w):
                nb = max(1, w // 512)
                e.wait_ge(s_t, 3 * nb)
                e.wait_ge(s_neg, 2)
                for i, ix in enumerate((idxS[:, 0:w], idxX[:, 4:4 + w])):
                    o = ix.rearrange("q (p c) -> q c p", c=w // P)
                    for c in range(nb):
                        k = (w // P) // nb
                        nc.scalar.copy(o[:, c * k:(c + 1) * k, :],
                                       PS[:, i * 2048 + c * 512:i * 2048 + c * 512 + k * P].rearrange("q (c p) -> q c p", c=k)).then_inc(s_i, 1)

            @block.vector
            def _(e):
                def path(plan, w):
                    cur, n = sort_vector(e, plan)
                    columns_vector(e, w, cur, n)
                either(e, lambda: path(short_plan, 256), lambda: path(full_plan, EC))

            @block.sync
            def _(e):
                def path(plan, w):
                    for it, cur, n, turned, signed in walk(plan):
                        pass
                    columns_sync(e, w, cur)
                either(e, lambda: path(short_plan, 256), lambda: path(full_plan, EC))

            @block.scalar
            def _(e):
                step = expert_scalar(e)
                for i in range(AHEAD):
                    step(i)

                def path(plan, w):
                    sort_scalar(e, plan, between(step))
                    columns_scalar(e, w)
                either(e, lambda: path(short_plan, 256), lambda: path(full_plan, EC))

            @block.tensor
            def _(e):
                step = expert_tensor(e)
                for i in range(AHEAD):
                    step(i)

                def path(plan, w):
                    sort_tensor(e, plan, between(step))
                    e.wait_ge(s_y, NR3)
                    columns_tensor(e, w)
                either(e, lambda: path(short_plan, 256), lambda: path(full_plan, EC))

        curS = sb("cur_src", [P, 2, 4], I32)
        curX = sb("cur_row", [P, 2, 4], I32)

        def two(t, at, n=512, k=HF):
            return t[0:k, at:at + 2 * n].rearrange("p (b n) -> p b n", b=2)
        Gs = R[:, 0:320].rearrange("p (b c r) -> p b c r", b=2, c=4)
        ends = R[:, 480:800].rearrange("p (b c r) -> p b c r", b=2, c=4)
        leak, ev, acc, dec, wt = two(Zt, 0), two(Zt, 1024), two(Ct, 0), two(Ct, 1024), two(St, 0)
        run = two(R, 1024, 513)
        negr = two(St, 1024)
        mk = two(R, 2052, 512, P)
        lo_s = two(R[:, 3076:3588].bitcast(BF16), 0, 512, P)
        hi_s = two(R[:, 18432:18944].bitcast(BF16), 0, 512, P)
        oh = two(R[:, 18944:19456].bitcast(BF16), 0, 512, P)
        OUTER, INNER = 16, NE // STEP // 2 // 16
        with ExitStack() as c5, nc.Block() as block:
            def sm(n):
                return c5.enter_context(nc.semaphore(n))
            s_row, s_leak, s_ch, s_sub, s_exp, s_acc, s_tr, s_ends, s_oh, s_t1, s_msk, s_cp, s_ini = (
                sm("s_row"), sm("s_leak"), sm("s_ch5"), sm("s_sub"), sm("s_exp"), sm("s_acc"), sm("s_tr"), sm("s_ends"),
                sm("s_oh"), sm("s_t1"), sm("s_msk"), sm("s_cp"), sm("s_ini"))
            s_mul = sm("s_mul")
            s_gat, s_sc = [sm("s_gat0"), sm("s_gat1")], [sm("s_sc0"), sm("s_sc1")]
            s_lh, s_ng = [sm("s_lh0"), sm("s_lh1")], [sm("s_ng0"), sm("s_ng1")]

            def rounds(e, n, body):
                with e.Fori(0, OUTER) as o:
                    with e.If(n > o * (INNER * 2 * STEP)):
                        with e.Fori(0, INNER) as k:
                            g = o * INNER + k
                            with e.If(n > g * (2 * STEP)):
                                body(g)

            def streamed(e):
                return e.value_load(nreal[0:1, 0:1], min_val=0, max_val=NE)

            @block.sync
            def _(e):
                def digits(i, b):
                    for row, t in ((lo_row, lo_s), (hi_row, hi_s)):
                        e.dma_start(t[:, b, :], row[bass.ds(i * STEP, STEP)].unsqueeze(0).to_broadcast([P, STEP])).then_inc(s_lh[b], 16)
                n = streamed(e)
                digits(0, 0)

                def body(g):
                    for b in (0, 1):
                        i = 2 * g + b
                        wait_reg(e, s_msk, i + 1)
                        digits(i + 1, b ^ 1)
                        wait_reg(e, s_acc, i + 1)
                        e.dma_start(negr[:, b, :], neg_d[bass.ds(i * STEP, STEP)].unsqueeze(0).to_broadcast([HF, STEP])).then_inc(s_ng[b], 16)
                rounds(e, n, body)

            @block.gpsimd
            def _(e):
                n = streamed(e)
                e.wait_ge(s_ini, 1)

                def gather(i, b, made):
                    e.tensor_copy(curS[:, b, :], idxS[:, bass.ds(i * 4, 4)] if not isinstance(i, int) else idxS[:, i * 4:i * 4 + 4]).then_inc(s_cp, 1)
                    if isinstance(made, int):
                        e.wait_ge(s_cp, made)
                    else:
                        wait_reg(e, s_cp, made)
                    for c in range(4):
                        e.indirect_dma_start(Gs[:, b, c, :], None, ts_d,
                                             bass.IndirectOffsetOnAxis(curS[:, b, c:c + 1], axis=0)).then_inc(s_gat[b], 16)

                def scatter(i, b, made, before):
                    wait_reg(e, s_sc[b], before)
                    e.tensor_copy(curX[:, b, :], idxX[:, bass.ds(i * 4, 4)]).then_inc(s_cp, 1)
                    wait_reg(e, s_cp, made)
                    wait_reg(e, s_ends, i + 2)
                    for c in range(4):
                        e.indirect_dma_start(nt_d, bass.IndirectOffsetOnAxis(curX[:, b, c:c + 1], axis=0),
                                             ends[:, b, c, :], None, bounds_check=M - 1, oob_is_err=False).then_inc(s_sc[b], 16)
                gather(0, 0, 1)
                gather(1, 1, 2)
                e.tensor_copy(curX[:, 0, :], idxX[:, 0:4]).then_inc(s_cp, 1)
                e.tensor_copy(curX[:, 1, :], idxX[:, 0:4]).then_inc(s_cp, 1)
                e.wait_ge(s_cp, 4)
                for b in (0, 1):
                    for c in range(4):
                        e.indirect_dma_start(nt_d, bass.IndirectOffsetOnAxis(curX[:, b, c:c + 1], axis=0),
                                             ends[:, b, c, :], None, bounds_check=M - 1, oob_is_err=False).then_inc(s_sc[b], 16)

                def body(g):
                    for b in (0, 1):
                        i = 2 * g + b
                        scatter(i, b ^ 1, 4 * g + 2 * b + 5, 64 * g + 64)
                        wait_reg(e, s_row, i + 1)
                        gather(i + 2, b, 4 * g + 2 * b + 6)
                rounds(e, n, body)
                last = (n + (2 * STEP - 1)) // (2 * STEP)
                scatter(2 * last, 1, 4 * last + 5, 64 * last + 64)
                wait_reg(e, s_sc[0], 64 * last + 64)
                wait_reg(e, s_sc[1], 64 * last + 128)
                wait_reg(e, s_gat[0], 64 * last + 64)
                wait_reg(e, s_gat[1], 64 * last + 64)

            @block.tensor
            def _(e):
                T = nc.tensor

                def lookup(b):
                    for k in range(3):
                        ins = T.matmul(bank(b), ad3[:, k, :, :].rearrange("p t h -> p (t h)"), oh[:, b, :], start=(k == 0), stop=(k == 2))
                    ins.then_inc(s_t1, 1)

                def turn_in(b):
                    o = PS[0:HF, (2 + b) * 512:(3 + b) * 512]
                    T.matmul(o, CS("head"), mk[:, b, :], start=True, stop=False)
                    for c in range(4):
                        T.matmul(o[:, c * P:(c + 1) * P], Gs[:, b, c, 0:HF], ident, start=False, stop=(c == 3))
                    for c in range(4):
                        ins = T.transpose(PS[0:HF, (4 + b) * 512 + c * P:(4 + b) * 512 + (c + 1) * P], Gs[:, b, c, HF:ROW], ident)
                    ins.then_inc(s_row, 1)

                def turn_out(b):
                    for c in range(4):
                        o = (6 + b) * 512 + c * ROW
                        T.transpose(PS[:, o:o + HF], acc[:, b, c * P:(c + 1) * P], CS("ident", HF)[:, 0:HF])
                        ins = T.transpose(PS[:, o + HF:o + ROW], run[:, b, 1 + c * P:1 + (c + 1) * P], CS("ident", HF)[:, 0:HF])
                    ins.then_inc(s_tr, 1)
                n = streamed(e)
                e.wait_ge(s_oh, 1)
                lookup(0)
                e.wait_ge(s_msk, 2)
                e.wait_ge(s_gat[0], 64)
                turn_in(0)

                def body(g):
                    for b in (0, 1):
                        i = 2 * g + b
                        wait_reg(e, s_oh, i + 2)
                        lookup(b ^ 1)
                        wait_reg(e, s_msk, i + 3)
                        wait_reg(e, s_gat[b ^ 1], 64 * (g + 1 + b))
                        turn_in(b ^ 1)
                        wait_reg(e, s_acc, i + 3)
                        wait_reg(e, s_ends, i + 1)
                        turn_out(b)
                rounds(e, n, body)

            @block.scalar
            def _(e):
                n = streamed(e)
                e.wait_ge(s_row, 1)
                nc.scalar.mul(leak[:, 0, :], PS[0:HF, 1024:1536], 0.2).then_inc(s_leak, 1)

                def body(g):
                    for b in (0, 1):
                        i = 2 * g + b
                        wait_reg(e, s_sub, 4 * g + 2 * b + 1)
                        nc.scalar.activation(wt[:, b, :], wt[:, b, :], ACT.Exp).then_inc(s_exp, 1)
                        wait_reg(e, s_sub, 4 * g + 2 * b + 2)
                        nc.scalar.activation(dec[:, b, :], dec[:, b, :], ACT.Exp).then_inc(s_exp, 1)
                        wait_reg(e, s_row, i + 2)
                        nc.scalar.mul(leak[:, b ^ 1, :], PS[0:HF, (2 + (b ^ 1)) * 512:(3 + (b ^ 1)) * 512], 0.2).then_inc(s_leak, 1)
                        wait_reg(e, s_tr, i + 3)
                        wait_reg(e, s_sc[b], 64 * (g + 1 + b))
                        nc.scalar.copy(ends[:, b, :, :], PS[:, (6 + b) * 512:(6 + b) * 512 + 4 * ROW].rearrange("p (c f) -> p c f", c=4)).then_inc(s_ends, 1)
                rounds(e, n, body)

            @block.vector
            def _(e):
                V = nc.vector
                LINKS = 4
                n = streamed(e)
                V.memset(ends[:, :, :, :], 0.0).then_inc(s_ini, 1)
                for s_, k in ((s_acc, 2), (s_tr, 2), (s_ends, 2), (s_msk, 1)):
                    e.sem_inc(s_, k)
                V.memset(run[:, 1, 512:513], 0.0).then_inc(s_ch, 1)
                V.memset(acc[:, 1, 511:512], 0.0).then_inc(s_ch, 1)
                e.wait_ge(s_ch, 2)

                def onehot(b):
                    V.tensor_scalar(oh[:, b, :], lo_s[:, b, :], CS("lane"), None, ALU.is_equal).then_inc(s_oh, 1)

                def mask(b):
                    V.scalar_tensor_tensor(mk[:, b, :], hi_s[:, b, :], CS("hi4"), bank(b), ALU.is_equal, ALU.mult).then_inc(s_msk, 1)
                e.wait_ge(s_lh[0], 32)
                onehot(0)
                e.wait_ge(s_t1, 1)
                mask(0)

                def body(g):
                    for b in (0, 1):
                        i = 2 * g + b
                        made = [2 * LINKS * g + LINKS * b + 2]

                        def link(ins):
                            made[0] = made[0] + 1
                            ins.then_inc(s_ch, 1)
                            wait_reg(e, s_ch, made[0])
                        wait_reg(e, s_leak, i + 1)
                        wait_reg(e, s_tr, i + 1)
                        V.tensor_copy(run[:, b, 0:1], run[:, b ^ 1, 512:513]).then_inc(s_ch, 1)
                        made[0] = made[0] + 1
                        link(V.tensor_tensor(ev[:, b, :], PS[0:HF, (2 + b) * 512:(3 + b) * 512], leak[:, b, :], ALU.max))
                        wait_reg(e, s_ng[b], 16 * g + 16)
                        link(V.tensor_tensor_scan(run[:, b, 1:513], negr[:, b, :], ev[:, b, :], run[:, b, 0:1], ALU.add, ALU.max))
                        V.tensor_tensor(wt[:, b, :], ev[:, b, :], run[:, b, 1:513], ALU.subtract).then_inc(s_sub, 1)
                        link(V.tensor_tensor(dec[:, b, :], negr[:, b, :], run[:, b, 0:512], ALU.add))
                        V.tensor_tensor(dec[:, b, :], dec[:, b, :], run[:, b, 1:513], ALU.subtract).then_inc(s_sub, 1)
                        wait_reg(e, s_lh[b ^ 1], 32 * (g + 1 + b))
                        onehot(b ^ 1)
                        wait_reg(e, s_exp, 4 * g + 2 * b + 2)
                        V.tensor_tensor(wt[:, b, :], wt[:, b, :], PS[0:HF, (4 + b) * 512:(5 + b) * 512], ALU.mult).then_inc(s_mul, 1)
                        wait_reg(e, s_t1, i + 2)
                        mask(b ^ 1)
                        wait_reg(e, s_mul, i + 1)
                        V.tensor_tensor_scan(acc[:, b, :], dec[:, b, :], wt[:, b, :], acc[:, b ^ 1, 511:512], ALU.mult, ALU.add).then_inc(s_acc, 1)
                        wait_reg(e, s_acc, i + 3)
                rounds(e, n, body)

        NR = R[:, 6144:6144 + NT * ROW].rearrange("p (t r) -> p t r", r=ROW)
        c4r = sb("row_4095", [P, ROW])
        sm4 = [R[:, 7424 + i * 128:7424 + (i + 1) * 128].rearrange("p (t h) -> p t h", h=GH) for i in range(6)]
        AG = R[:, 8192:8704].rearrange("p (t f) -> p t f", f=GH * GE)
        A2 = R[:, 8704:9216].rearrange("p (t f) -> p t f", f=GH * GE)
        PB = sb("pos_blk", [D, H1, NREL])
        with ExitStack() as c6, nc.Block() as block:
            def sm(n):
                return c6.enter_context(nc.semaphore(n))
            s_ld, s_v, s_x, s_e, s_z, s_bank, s_zT, s_pp, s_pb = (sm("s_ld"), sm("s_v6"), sm("s_x6"), sm("s_e6"), sm("s_z6"), sm("s_bank6"),
                                                             sm("s_zT6"), sm("s_pp"), sm("s_pb"))
            es, ec, er, ss, cn, tm = sm4
            G4 = [P, NT, GH]
            G16 = [P, NT, GH, GE]

            @block.sync
            def _(e):
                e.dma_start(NR[:, :, :], nt_d.rearrange("(t p) r -> p t r", p=P)).then_inc(s_ld, 16)
                e.dma_start(c4r[:, :], ts_d[M - 1:M, :].to_broadcast([P, ROW])).then_inc(s_ld, 16)

            @block.scalar
            def _(e):
                for i in (0, 1, 2):
                    e.wait_ge(s_x, i + 1)
                    t = (es, ec, er)[i]
                    nc.scalar.activation(t[:, :, :], t[:, :, :], ACT.Exp).then_inc(s_e, 1)
                root(e, NT)
                e.wait_ge(s_x, 4)
                nc.scalar.activation(sm4[3][:, :, :], sm4[3][:, :, :], ACT.Exp).then_inc(s_e, 1)
                e.wait_ge(s_pp, 1)
                for h in range(H1):
                    hc = consts[0:D, CCST["hcol"][0] + h:CCST["hcol"][0] + h + 1]
                    nc.scalar.mul(PB[:, h, :], PS[0:D, 0:NREL], hc).then_inc(s_pb, 1)
                root(e, NT)
                root(e, NT)
                copy_zT(e, s_bank, 0, s_zT)

            @block.tensor
            def _(e):
                nc.tensor.matmul(PS[0:D, 0:NREL], W65("Wpos"), W65("enc"), start=True, stop=True).then_inc(s_pp, 1)
                e.wait_ge(s_pb, H1)
                transpose_z(e, s_z, s_bank, None, 1)

            @block.vector
            def _(e):
                ch = Chain(e, s_v)
                V = nc.vector
                e.wait_ge(s_ld, 32)
                ch.link(V.tensor_tensor(es[:, :, :], as_[:, :, :], ad_[:, :, :], ALU.add))
                ch.link(V.tensor_tensor(ec[:, :, :], ad_[:, :, :], spread(c4r[:, 16:20], 1, G4), ALU.add))
                for t in (es, ec):
                    ch.link(V.tensor_scalar(tm[:, :, :], t[:, :, :], 0.2, None, ALU.mult))
                    ch.link(V.tensor_tensor(t[:, :, :], t[:, :, :], tm[:, :, :], ALU.max))
                ch.link(V.tensor_scalar(cn[:, :, 0], cnt[:, :], 0.5, 1.0, ALU.is_ge, ALU.subtract))
                ch.link(V.tensor_scalar(cn[:, :, 0], cn[:, :, 0], BIG, None, ALU.mult))
                ch.link(V.tensor_tensor(ec[:, :, :], ec[:, :, :], cn[:, :, 0:1].to_broadcast(G4), ALU.add))
                RM = NR[:, :, HF + 16:HF + 20]
                ch.link(V.tensor_tensor(tm[:, :, :], es[:, :, :], ec[:, :, :], ALU.max))
                ch.link(V.tensor_tensor(tm[:, :, :], tm[:, :, :], RM, ALU.max))
                V.tensor_tensor(es[:, :, :], es[:, :, :], tm[:, :, :], ALU.subtract).then_inc(s_x, 1)
                V.tensor_tensor(ec[:, :, :], ec[:, :, :], tm[:, :, :], ALU.subtract).then_inc(s_x, 1)
                V.tensor_tensor(er[:, :, :], RM, tm[:, :, :], ALU.subtract).then_inc(s_x, 1)
                e.wait_ge(s_e, 3)
                ch.link(V.tensor_tensor(ec[:, :, :], ec[:, :, :], spread(cnt[:, :], 2, G4), ALU.mult))
                ch.link(V.tensor_tensor(ss[:, :, :], es[:, :, :], ec[:, :, :], ALU.add))
                ch.link(V.tensor_tensor(tm[:, :, :], er[:, :, :], NR[:, :, 16:20], ALU.mult))
                ch.link(V.tensor_tensor(ss[:, :, :], ss[:, :, :], tm[:, :, :], ALU.add))
                ch.link(V.tensor_scalar(ss[:, :, :], ss[:, :, :], 1e-16, None, ALU.add))
                ch.link(V.reciprocal(ss[:, :, :], ss[:, :, :]))
                ag = AG[:, :, :].rearrange("p t (h e) -> p t h e", h=GH)
                a2 = A2[:, :, :].rearrange("p t (h e) -> p t h e", h=GH)
                ch.link(V.tensor_tensor(ag, HG[:, :, :].rearrange("p t (h e) -> p t h e", h=GH), spread(es[:, :, :], 3, G16), ALU.mult))
                c16 = spread(c4r[:, HF:HF + 16], 1, [P, NT, 16]).rearrange("p t (h e) -> p t h e", h=GH)
                ch.link(V.tensor_tensor(a2, c16, spread(ec[:, :, :], 3, G16), ALU.mult))
                ch.link(V.tensor_tensor(AG[:, :, :], AG[:, :, :], A2[:, :, :], ALU.add))
                ch.link(V.tensor_tensor(a2, NR[:, :, 0:16].rearrange("p t (h e) -> p t h e", h=GH), spread(er[:, :, :], 3, G16), ALU.mult))
                ch.link(V.tensor_tensor(AG[:, :, :], AG[:, :, :], A2[:, :, :], ALU.add))
                ch.link(V.tensor_tensor(ag, ag, spread(ss[:, :, :], 3, G16), ALU.mult))
                ch.link(V.tensor_tensor(AG[:, :, :], AG[:, :, :], spread(RO("bgat"), 1, [P, NT, 16]), ALU.add))
                m, v = mean[:, 0:NT], var[:, 0:NT]
                ch.link(V.reduce_sum(m, AG[:, :, :], AX.X))
                ch.link(V.tensor_scalar(m, m, -1.0 / 16, None, ALU.mult))
                ch.link(V.tensor_tensor(AG[:, :, :], AG[:, :, :], spread(m, 2, [P, NT, 16]), ALU.add))
                ch.link(V.tensor_tensor(A2[:, :, :], AG[:, :, :], AG[:, :, :], ALU.mult))
                ch.link(V.reduce_sum(v, A2[:, :, :], AX.X))
                n_ln[0] += 1
                V.tensor_scalar(v, v, 1.0 / 16, EPS, ALU.mult, ALU.add).then_inc(s_ln, 1)
                e.wait_ge(s_std, n_ln[0])
                ch.link(V.reciprocal(v, v))
                ch.link(V.tensor_tensor(AG[:, :, :], AG[:, :, :], spread(v, 2, [P, NT, 16]), ALU.mult))
                ch.link(V.tensor_tensor(AG[:, :, :], AG[:, :, :], spread(RO("lng"), 1, [P, NT, 16]), ALU.mult))
                ch.link(V.tensor_tensor(AG[:, :, :], AG[:, :, :], spread(RO("lnb"), 1, [P, NT, 16]), ALU.add))
                sc = sm4[3][:, :, :]
                ch.link(V.reduce_sum(sc, AG[:, :, :].rearrange("p t (h e) -> p t e h", h=GH), AX.X))
                ch.link(V.tensor_scalar(sc, sc, 1.0 / GH, None, ALU.mult))
                gating(e, ch, sc, GE, CS("lowa"), s_x, s_e, 4)
                for i in range(GE):
                    ch.link(V.tensor_tensor(s3, Y[i], sc[:, :, i:i + 1].to_broadcast(PT), ALU.mult))
                    ch.link(V.tensor_tensor(Ht[:, :], Ht[:, :], St[:, :], ALU.add))
                layernorm(e, ch, h3, z3, NT, D)
                layernorm(e, ch, z3, z3, NT, D)
                ch.link(V.tensor_tensor(z3, z3, spread(RO("g1"), 1, PT), ALU.mult))
                V.tensor_tensor(z3, z3, spread(RO("be1"), 1, PT), ALU.add).then_inc(s_z, 1)

        base = 0

        def take(n):
            nonlocal base
            base += n
            return R[:, base - n:base]
        QU = [take(512)[0:D, :] for _ in (0, 1)]
        QV = [take(512)[0:D, :] for _ in (0, 1)]
        KB = [take(2048)[0:D, :].rearrange("p (i h s) -> p i h s", i=8, h=H1) for _ in (0, 1)]
        VB = [take(512).rearrange("p (i d) -> p i d", i=8) for _ in (0, 1)]
        RB = [take(4 * H1 * NREL).rearrange("p (t x) -> p t x", t=4) for _ in (0, 1)]
        PO = [take(1024) for _ in (0, 1)]
        SC = [take(1024) for _ in (0, 1)]
        AT = [take(1024) for _ in (0, 1)]
        CT = [take(512)[0:D + 1, :] for _ in (0, 1)]
        mx, sm_ = sb("row_max", [P, 16]), sb("row_sum", [P, 16])
        assert base <= 20480
        with ExitStack() as c7, nc.Block() as block:
            def sm(n):
                return c7.enter_context(nc.semaphore(n))
            names = ["s_q", "s_k", "s_vp", "s_rp", "s_proj", "s_kb", "s_vb", "s_rb", "s_skew", "s_scp", "s_sx", "s_se", "s_at", "s_atp",
                     "s_atc", "s_cp", "s_ct", "s_op", "s_h7", "s_v7", "s_one", "s_split"]
            S = {n: sm(n) for n in names}
            s_pos = [sm("s_pos0"), sm("s_pos1")]
            s_rbo = [sm("s_rbo0"), sm("s_rbo1")]

            @block.gpsimd
            def _(e):
                ch = Chain(e, S["s_split"])
                G = nc.gpsimd
                ch.link(G.tensor_copy(wup3[:, 0, :], wup[:, :]))
                ch.link(G.tensor_tensor(wup[:, :], wup[:, :], wup3[:, 0, :], ALU.subtract))
                ch.link(G.tensor_copy(wup3[:, 1, :], wup[:, :]))
                ch.link(G.tensor_tensor(wup[:, :], wup[:, :], wup3[:, 1, :], ALU.subtract))
                ch.link(G.tensor_copy(wup3[0:D, 2, :], wup[0:D, :]))
                ch.link(G.tensor_copy(wup3[D:P, 2, :], wup3[D:P, 0, :]))

            @block.tensor
            def _(e):
                T = nc.tensor

                def project(g):
                    cols = slice(g * 512, (g + 1) * 512)
                    if g:
                        e.wait_ge(S["s_proj"], 2 * g)
                        e.wait_ge(S["s_kb"], H1 * g)
                        e.wait_ge(S["s_vb"], g)
                    T.matmul(PS[0:D, 0:512], W65("Wq"), ZT[:, cols], start=True, stop=True).then_inc(S["s_q"], 1)
                    T.matmul(PS[0:D, 512:1024], W65("Wk"), ZT[:, cols], start=True, stop=True).then_inc(S["s_k"], 1)
                    for i in range(8):
                        for r in (0, 64):
                            ins = T.matmul(PS[r:r + 64, 1024 + i * D:1024 + (i + 1) * D],
                                           ZT[:, g * 512 + i * 64:g * 512 + (i + 1) * 64], W65("Wv"), start=True, stop=True)
                    ins.then_inc(S["s_vp"], 1)
                    e.wait_ge(S["s_proj"], 2 * g + 2)
                    for j in range(4):
                        n = 4 * g + j
                        if n:
                            e.wait_ge(S["s_rb"], n)
                        T.matmul(PS[:, 1536:1536 + H1 * NREL], QV[g % 2][:, j * P:(j + 1) * P],
                                 PB[:, :, :].rearrange("p h r -> p (h r)"), start=True, stop=True).then_inc(S["s_rp"], 1)

                def attend(g):
                    b = g % 2
                    e.wait_ge(S["s_kb"], H1 * (g + 1))
                    if g:
                        e.wait_ge(S["s_sx"], 4 * g)
                    for i in range(8):
                        o = PS[64 * (i % 2):64 * (i % 2) + 64, 2048 + (i // 2) * 256:2048 + (i // 2 + 1) * 256]
                        ins = T.matmul(o, QU[b][:, i * 64:(i + 1) * 64], KB[b][:, i, :, :].rearrange("p h s -> p (h s)"), start=True, stop=True)
                        if i % 4 == 3:
                            ins.then_inc(S["s_scp"], 1)
                    e.wait_ge(S["s_at"], g + 1)
                    if g:
                        e.wait_ge(S["s_op"], g)
                        e.wait_ge(S["s_h7"], g)
                    for t in range(8):
                        o = PS[:, 3072 + t * P:3072 + (t + 1) * P]
                        ins = T.transpose(o, SC[b][:, t * P:(t + 1) * P], ident)
                        if t % 4 == 3:
                            ins.then_inc(S["s_atp"], 1)
                    e.wait_ge(S["s_atc"], 2 * g + 2)
                    e.wait_ge(S["s_vb"], g + 1)
                    for i in range(8):
                        for hp in range(2):
                            at = AT[b][:, ((i // 2) * 2 + hp) * P + (i % 2) * 64:((i // 2) * 2 + hp) * P + (i % 2) * 64 + 64]
                            ins = T.matmul(PS[hp * 32:(hp + 1) * 32, 3072 + i * 64:3072 + (i + 1) * 64], VB[b][:, i, hp * 32:(hp + 1) * 32], at,
                                           start=True, stop=True)
                    ins.then_inc(S["s_cp"], 1)
                    e.wait_ge(S["s_ct"], g + 1)
                    for j in range(4):
                        ins = T.matmul(PS[:, 3584 + j * D:3584 + (j + 1) * D], CT[b][:, j * P:(j + 1) * P], W65("Wo"), start=True, stop=True)
                    ins.then_inc(S["s_op"], 1)
                e.wait_ge(S["s_one"], 2)
                project(0)
                for g in range(8):
                    if g < 7:
                        project(g + 1)
                    attend(g)

            @block.scalar
            def _(e):
                A = nc.scalar

                def project(g):
                    b = g % 2
                    if g >= 2:
                        e.wait_ge(S["s_scp"], 2 * (g - 1))
                    e.wait_ge(S["s_q"], g + 1)
                    if g >= 2:
                        e.wait_ge(S["s_rp"], 4 * (g - 1))
                    u = w65s[0:D, C65["u"][0]:C65["u"][1]]
                    v = w65s[0:D, C65["v"][0]:C65["v"][1]]
                    A.activation(QU[b], PS[0:D, 0:512], ACT.Identity, bias=u).then_inc(S["s_proj"], 1)
                    A.activation(QV[b], PS[0:D, 0:512], ACT.Identity, bias=v).then_inc(S["s_proj"], 1)
                    e.wait_ge(S["s_k"], g + 1)
                    for h in range(H1):
                        hc = consts[0:D, CCST["hcol"][0] + h:CCST["hcol"][0] + h + 1]
                        A.mul(KB[b][:, :, h, :], PS[0:D, 512:1024].rearrange("p (i s) -> p i s", i=8), hc).then_inc(S["s_kb"], 1)
                    for j in range(4):
                        n = 4 * g + j
                        e.wait_ge(S["s_rp"], n + 1)
                        if g >= 2:
                            e.wait_ge(s_rbo[b], 64 * (g // 2))
                        A.copy(RB[b][:, j, :], PS[:, 1536:1536 + H1 * NREL]).then_inc(S["s_rb"], 1)

                def attend(g):
                    b = g % 2
                    e.wait_ge(S["s_se"], g + 1)
                    A.activation(SC[b], SC[b], ACT.Exp, scale=HD1 ** -0.5).then_inc(S["s_skew"], 1)
                    for i in (0, 1):
                        e.wait_ge(S["s_atp"], 2 * g + i + 1)
                        if g >= 2:
                            e.wait_ge(S["s_cp"], g - 1)
                        A.copy(AT[b][:, i * 512:(i + 1) * 512], PS[:, 3072 + i * 512:3072 + (i + 1) * 512]).then_inc(S["s_atc"], 1)
                    e.wait_ge(S["s_cp"], g + 1)
                    if g >= 2:
                        e.wait_ge(S["s_op"], g - 1)
                    A.copy(CT[b][0:D, :], PS[0:D, 3072:3584]).then_inc(S["s_ct"], 1)
                project(0)
                for g in range(8):
                    if g < 7:
                        project(g + 1)
                    attend(g)

            @block.sync
            def _(e):
                for g in range(8):
                    b = g % 2
                    for j in range(4):
                        n = 4 * g + j
                        e.wait_ge(S["s_rb"], n + 1)
                        e.dma_start(skew_d[n * P * H1 * NREL:(n + 1) * P * H1 * NREL].rearrange("(p x) -> p x", p=P), RB[b][:, j, :]).then_inc(s_rbo[b], 16)
                    e.wait_ge(s_rbo[b], 64 * (g // 2 + 1))
                    if g >= 2:
                        e.wait_ge(S["s_sx"], 4 * (g - 1))
                    for i in range(8):
                        tok0 = g * 512 + i * 64
                        src = bass.AP(tensor=skew_d.tensor, offset=tok0 * H1 * NREL + NTOK - 1,
                                      ap=[[H1 * NREL - 1, 64], [NREL, H1], [1, 64]])
                        dst = PO[b][64 * (i % 2):64 * (i % 2) + 64, (i // 2) * 256:(i // 2 + 1) * 256].rearrange("p (h s) -> p h s", h=H1)
                        e.dma_start(dst, src).then_inc(s_pos[b], 16)

            @block.vector
            def _(e):
                ch = Chain(e, S["s_v7"])
                V = nc.vector
                for b in (0, 1):
                    V.memset(CT[b][D:D + 1, :], 1.0).then_inc(S["s_one"], 1)

                def values(g):
                    e.wait_ge(S["s_vp"], g + 1)
                    if g >= 2:
                        e.wait_ge(S["s_cp"], g - 1)
                    V.tensor_tensor(VB[g % 2], PS[:, 1024:1536].rearrange("p (i d) -> p i d", i=8),
                                    spread(CS("vmask"), 1, [P, 8, D]), ALU.mult).then_inc(S["s_vb"], 1)

                def attend(g):
                    b = g % 2
                    sc3 = SC[b].rearrange("p (r s) -> p r s", s=64)
                    R3 = [P, 16, 64]
                    e.wait_ge(s_pos[b], 128 * (g // 2 + 1))
                    e.wait_ge(S["s_scp"], 2 * g + 2)
                    if g >= 2:
                        e.wait_ge(S["s_atp"], 2 * (g - 1))
                    for i in (0, 1):
                        V.tensor_tensor(SC[b][:, i * 512:(i + 1) * 512], PS[:, 2048 + i * 512:2048 + (i + 1) * 512],
                                        PO[b][:, i * 512:(i + 1) * 512], ALU.add).then_inc(S["s_sx"], 2)
                    e.wait_ge(S["s_sx"], 4 * g + 4)
                    ch.link(V.reduce_max(mx[:, :], sc3, AX.X))
                    V.tensor_tensor(sc3, sc3, spread(mx[:, :], 2, R3), ALU.subtract).then_inc(S["s_se"], 1)
                    e.wait_ge(S["s_skew"], g + 1)
                    ch.link(V.reduce_sum(sm_[:, :], sc3, AX.X))
                    ch.link(V.reciprocal(sm_[:, :], sm_[:, :]))
                    V.tensor_tensor(sc3, sc3, spread(sm_[:, :], 2, R3), ALU.mult).then_inc(S["s_at"], 1)
                    e.wait_ge(S["s_op"], g + 1)
                    V.tensor_tensor(h3[:, 4 * g:4 * g + 4, :], h3[:, 4 * g:4 * g + 4, :],
                                    PS[:, 3584:3584 + 256].rearrange("p (t d) -> p t d", d=D), ALU.add).then_inc(S["s_h7"], 1)
                values(0)
                for g in range(8):
                    if g < 7:
                        values(g + 1)
                    attend(g)

        zA = zt_mem[:, 0:M // 2].bitcast(BF16)
        zB = zt_mem[:, M // 2:M].bitcast(BF16)
        z12 = R[:, 0:2048].bitcast(BF16).rearrange("p (t k) -> p t k", k=2 * D)
        z13 = R[:, 2048:4096].bitcast(BF16).rearrange("p (t k) -> p t k", k=2 * D)
        NB8 = 4
        hb = [R[:, 8192 + i * 512:8192 + (i + 1) * 512] for i in range(NB8)]
        hs = [R[:, 10240 + i * 512:10240 + (i + 1) * 512] for i in range(NB8)]
        yT = [R[:, 12288 + i * 512:12288 + (i + 1) * 512] for i in range(2)]
        gT = R[0:E1, 13312:13312 + M]
        g3 = R[:, 17408:17408 + NT * 3 * E1 // 2].bitcast(BF16).rearrange("p (t c e) -> p t c e", c=3, e=E1)
        g3T = R[0:3 * E1, 17792:17792 + 2048].bitcast(BF16)
        pick = R[0:3 * E1, 19840:19840 + E1 * P // 2].bitcast(BF16).rearrange("p (e m) -> p e m", e=E1)
        rest = [Zt[:, 0:256].rearrange("p (t e) -> p t e", e=E1), Zt[:, 256:512].rearrange("p (t e) -> p t e", e=E1)]
        identb = hid[0][:, 0:64].bitcast(BF16)
        oa = c3
        PSB = PS[:, :].bitcast(BF16)
        with ExitStack() as c8, nc.Block() as block:
            def sm(n):
                return c8.enter_context(nc.semaphore(n))
            s_v, s_z, s_bank, s_zT, s_x, s_e, s_lg, s_g3, s_gt, s_gtc, s_g3t, s_hp, s_hs, s_wb, s_sc, s_dn, s_yp, s_yc, s_op, s_fin, s_out = (
                sm("s_v8"), sm("s_z8"), sm("s_bank8"), sm("s_zT8"), sm("s_x8"), sm("s_e8"), sm("s_lg"), sm("s_g3"), sm("s_gt"),
                sm("s_gtc"), sm("s_g3t"), sm("s_hp8"), sm("s_hs8"), sm("s_wb"), sm("s_sc8"), sm("s_dn"), sm("s_yp8"), sm("s_yc"),
                sm("s_op8"), sm("s_fin"), sm("s_out"))
            s_z1, s_z1b, s_zB = sm("s_z1"), sm("s_z1b"), sm("s_zB")
            seq = [(g, x_) for g in range(8) for x_ in range(E1)]
            NS = len(seq)

            @block.tensor
            def _(e):
                T = nc.tensor
                passes = ((zA, 0), (zA, 1), (zB, 2))
                for st in (0, 1):
                    e.wait_ge(s_z, st + 1)
                    if st:
                        e.wait_ge(s_z1b, 1)
                    for t in range(NT):
                        ins = T.transpose(PSB[:, st * M + t * P:st * M + (t + 1) * P], (z12, z13)[st][:, t, :], identb)
                        if t % 8 == 7:
                            ins.then_inc(s_bank, 1)
                e.wait_ge(s_zT, 4)
                e.wait_ge(s_zB, 4)
                for t in range(NT):
                    for k, (zs, part) in enumerate(passes):
                        ins = T.matmul(PS[:, 3584 + t * E1:3584 + (t + 1) * E1], zs[:, t * P:(t + 1) * P], wup3[:, part, 0:E1],
                                       start=(k == 0), stop=(k == 2))
                ins.then_inc(s_lg, 1)
                w2 = W128("W2b").rearrange("p (e c d) -> p e c d", e=E1, c=FC1)

                def up(n):
                    g, x_ = seq[n]
                    for c in range(FC1):
                        q = 2 * n + c
                        if q >= 4:
                            e.wait_ge(s_hs, q - 3)
                        f = E1 + x_ * F1 + c * P
                        for k, (zs, part) in enumerate(passes):
                            ins = T.matmul(bank(q % 4), wup3[:, part, f:f + P], zs[:, g * 512:(g + 1) * 512], start=(k == 0), stop=(k == 2))
                        ins.then_inc(s_hp, 1)

                def spread_gate(n):
                    g, x_ = seq[n]
                    if n >= 2:
                        e.wait_ge(s_sc, 2 * n - 2)
                    T.matmul(bank(4 + n % 2), pick[:, x_, :], g3T[:, g * 512:(g + 1) * 512], start=True, stop=True).then_inc(s_wb, 1)

                def down(n):
                    g, x_ = seq[n]
                    e.wait_ge(s_sc, 2 * n + 2)
                    if x_ == 0 and g:
                        e.wait_ge(s_yc, g)
                    for c in range(FC1):
                        ins = T.matmul(PS[c * D:(c + 1) * D, 3072:3584], w2[:, x_, c, :], hs[(2 * n + c) % NB8], start=(x_ == 0),
                                       stop=(x_ == E1 - 1 and c == 1))
                    ins.then_inc(s_dn, 1)
                    if x_ == E1 - 1:
                        T.matmul(PS[0:D, 3072:3584], W65("b2b", E1), gT[:, g * 512:(g + 1) * 512], start=False, stop=True).then_inc(s_yp, 1)

                def finish(g):
                    e.wait_ge(s_yc, g + 1)
                    if g:
                        e.wait_ge(s_fin, g)
                    for j in range(4):
                        ins = T.matmul(PS[:, 3584 + j * D:3584 + (j + 1) * D], yT[g % 2][:, j * P:(j + 1) * P], CS("fold"), start=True, stop=True)
                    ins.then_inc(s_op, 1)
                up(0)
                up(1)
                e.wait_ge(s_g3, 2)
                for q in range(4):
                    if q:
                        e.wait_ge(s_gtc, q)
                    for t in range(8):
                        ins = T.transpose(PS[0:E1, 2048 + t * P:2048 + (t + 1) * P], gates[:, 8 * q + t, :], ident)
                    ins.then_inc(s_gt, 1)
                e.wait_ge(s_gtc, 4)
                for q in range(2):
                    if q:
                        e.wait_ge(s_gtc, 5)
                    for t in range(16):
                        ins = T.transpose(PSB[0:3 * E1, 4096 + t * P:4096 + (t + 1) * P],
                                          g3[:, 16 * q + t, :, :].rearrange("p c e -> p (c e)"), identb)
                    ins.then_inc(s_gt, 1)
                e.wait_ge(s_gtc, 6)
                spread_gate(0)
                for n in range(NS):
                    if n >= 1 and n + 1 < NS:
                        up(n + 1)
                    if n + 1 < NS:
                        spread_gate(n + 1)
                    down(n)
                    if seq[n][1] == 1 and seq[n][0]:
                        finish(seq[n][0] - 1)
                finish(7)

            @block.scalar
            def _(e):
                A = nc.scalar
                root(e, NT)
                e.wait_ge(s_z1, 1)
                A.copy(z13[:, :, 0:D], z12[:, :, 0:D]).then_inc(s_z1b, 1)
                for b in range(4):
                    e.wait_ge(s_bank, b + 1)
                    A.copy(zA[:, b * 1024:(b + 1) * 1024], PSB[:, b * 1024:(b + 1) * 1024]).then_inc(s_zT, 1)
                e.wait_ge(s_x, 1)
                A.activation(gates[:, :, :], gates[:, :, :], ACT.Exp).then_inc(s_e, 1)

                def gelu(n):
                    for c in range(FC1):
                        q = 2 * n + c
                        e.wait_ge(s_hp, q + 1)
                        if q >= NB8:
                            e.wait_ge(s_sc, q - NB8 + 1)
                        b1 = w128s[:, C128["b1b"][0] + FC1 * seq[n][1] + c:C128["b1b"][0] + FC1 * seq[n][1] + c + 1]
                        A.activation(hb[q % NB8], bank(q % 4), ACT.Gelu, bias=b1).then_inc(s_hs, 1)
                gelu(0)
                gelu(1)
                for q in range(4):
                    e.wait_ge(s_gt, q + 1)
                    A.copy(gT[:, q * 1024:(q + 1) * 1024], PS[0:E1, 2048:3072]).then_inc(s_gtc, 1)
                for q in range(2):
                    e.wait_ge(s_gt, 4 + q + 1)
                    A.copy(g3T[:, q * 2048:(q + 1) * 2048], PSB[0:3 * E1, 4096:6144]).then_inc(s_gtc, 1)
                for n in range(2, NS):
                    gelu(n)
                    g, x_ = seq[n]
                    if x_ == 0 and g:
                        e.wait_ge(s_yp, g)
                        if g >= 3:
                            e.wait_ge(s_op, g - 2)
                        A.copy(yT[(g - 1) % 2], bank(6)).then_inc(s_yc, 1)
                e.wait_ge(s_yp, 8)
                e.wait_ge(s_op, 6)
                A.copy(yT[1], bank(6)).then_inc(s_yc, 1)

            @block.vector
            def _(e):
                ch = Chain(e, s_v)
                V = nc.vector
                V.tensor_copy(identb, ident)
                layernorm(e, ch, h3, z3, NT, D)
                V.tensor_copy(z12[:, :, 0:D], z3).then_inc(s_z1, 1)
                e.wait_ge(s_z1, 1)
                ch.link(V.tensor_tensor(z3, z3, z12[:, :, 0:D], ALU.subtract))
                V.tensor_copy(z12[:, :, D:2 * D], z3).then_inc(s_z, 1)
                e.wait_ge(s_z, 1)
                V.tensor_tensor(z13[:, :, D:2 * D], z3, z12[:, :, D:2 * D], ALU.subtract).then_inc(s_z, 1)
                for b in range(4):
                    e.wait_ge(s_bank, 4 + b + 1)
                    V.tensor_copy(zB[:, b * 1024:(b + 1) * 1024], PSB[:, M + b * 1024:M + (b + 1) * 1024]).then_inc(s_zB, 1)
                V.tensor_copy(pick, spread(CS("pick", 3 * E1), 2, [3 * E1, E1, P])).then_inc(s_g3, 1)
                e.wait_ge(s_lg, 1)
                ch.link(V.tensor_tensor(gates[:, :, :], PS[:, 3584:3584 + NT * E1].rearrange("p (t e) -> p t e", e=E1),
                                        spread(RO("bg"), 1, [P, NT, E1]), ALU.add))
                gating(e, ch, gates[:, :, :], E1, CS("lowb"), s_x, s_e, 1)
                ch.link(V.tensor_copy(g3[:, :, 0, :], gates[:, :, :]))
                ch.link(V.tensor_tensor(rest[0], gates[:, :, :], g3[:, :, 0, :], ALU.subtract))
                ch.link(V.tensor_copy(g3[:, :, 1, :], rest[0]))
                ch.link(V.tensor_tensor(rest[1], rest[0], g3[:, :, 1, :], ALU.subtract))
                V.tensor_copy(g3[:, :, 2, :], rest[1]).then_inc(s_g3, 1)

                def add_out(g):
                    e.wait_ge(s_op, g + 1)
                    V.tensor_tensor(oa[:, 4 * g:4 * g + 4, :], h3[:, 4 * g:4 * g + 4, :],
                                    PS[:, 3584:3584 + 256].rearrange("p (t d) -> p t d", d=D), ALU.add).then_inc(s_fin, 1)
                for n, (g, x_) in enumerate(seq):
                    e.wait_ge(s_wb, n + 1)
                    for c in range(FC1):
                        q = 2 * n + c
                        e.wait_ge(s_hs, q + 1)
                        if q >= NB8:
                            e.wait_ge(s_dn, n - 1)
                        V.tensor_tensor(hs[q % NB8], hb[q % NB8], bank(4 + n % 2), ALU.mult).then_inc(s_sc, 1)
                    if x_ == 3 and g:
                        add_out(g - 1)
                add_out(7)

            @block.sync
            def _(e):
                for g in range(8):
                    e.wait_ge(s_fin, g + 1)
                    e.dma_start(out[g * 512:(g + 1) * 512, :].rearrange("(t p) d -> p t d", p=P), oa[:, 4 * g:4 * g + 4, :]).then_inc(s_out, 16)
                e.wait_ge(s_out, 128)


def kernel(**inputs):
    import numpy as np
    import concourse.bacc as bacc
    from concourse.bass_utils import run_bass_kernel_spmd

    a = {k: np.asarray(v) for k, v in inputs.items()}
    f = np.float32

    x = a["x"].reshape(NIMG, 3, 8, 16, 8, 16).transpose(1, 3, 5, 0, 2, 4).reshape(KC, P, M).transpose(1, 0, 2)

    def pad(m, n=D + 1):
        return np.concatenate([m, np.zeros((n - m.shape[0], m.shape[1]), f)], 0)

    def with_bias(w, b):
        return np.concatenate([w, b.reshape(1, -1)], 0)

    n = np.arange(NTOK)
    grid = np.stack([n // 8, n % 8]).astype(f) / f(7)
    grid = np.concatenate([np.concatenate([grid, np.ones((1, NTOK), f)], 0)] * 2, 1)
    rel = np.arange(61, dtype=f)[:, None] * np.exp(np.arange(0, D, 2, dtype=f) * f(-np.log(10000.0) / D))
    enc = np.stack([np.sin(rel), np.cos(rel)], -1).reshape(61, D).astype(f)
    enc = enc[np.clip(np.arange(-NTOK + 1, NTOK), -30, 30) + 30].T
    enc = np.concatenate([enc, np.ones((1, NREL), f)], 0)
    p = np.arange(P)
    heads = np.arange(D) // HD1
    c = {
        "ident": np.eye(P, dtype=f),
        "sign": np.stack([1 - 2 * ((p >> b) & 1) for b in range(7)], 1).astype(f),
        "iota": np.tile(np.arange(D, dtype=f), (P, 1)),
        "kvmask": pad(np.tile((np.arange(D)[:, None] // HC0 == np.arange(D) // HC0).astype(f) / f(NTOK), (1, 2)), P),
        "hcol": pad((heads[:, None] == np.arange(H1)).astype(f), P),
        "vmask": (heads[None, :] % 2 == (p[:, None] // 64)).astype(f),
        "lowa": np.tile(np.tril(np.ones((GE, GE), f), -1).reshape(1, -1), (P, 1)),
        "lowb": np.tile(np.tril(np.ones((E1, E1), f), -1).reshape(1, -1), (P, 1)),
    }
    c["pick"] = pad((np.arange(3 * E1)[:, None] % E1 == np.arange(E1)).astype(f), P)
    c["fold"] = np.concatenate([np.eye(D, dtype=f)] * 2, 0)
    c["lane"] = p[:, None].astype(f)
    c["hi4"] = (p[:, None] // GH).astype(f)
    c["head"] = (p[:, None] % GH == np.concatenate([np.arange(16) // GE, np.arange(GH)])).astype(f)
    g = a
    w65 = {
        "pos1": pad(np.concatenate([g["L0_tok_W1"], g["L0_tok_b1"][None], np.zeros((D - 3, D), f), g["L0_tok_bp"][None]], 0)),
        "pos2": with_bias(g["L0_tok_W2"], g["L0_tok_b2"]),
        "Wgat": pad(g["L0_ffn_W_gat"]),
        "W1a": with_bias(g["L0_ffn_W1"].transpose(1, 0, 2).reshape(D, -1), g["L0_ffn_b1"]),
        "Wq": with_bias(g["L1_attn_Wq"].T, g["L1_attn_bq"]),
        "Wk": with_bias(g["L1_attn_Wk"].T, g["L1_attn_bk"]),
        "Wv": with_bias(g["L1_attn_Wv"].T, g["L1_attn_bv"]),
        "Wpos": with_bias(g["L1_attn_Wpos"].T, g["L1_attn_bpos"]),
        "Wo": with_bias(g["L1_attn_Wo"].T, g["L1_attn_bo"]),
        "u": pad(g["L1_attn_u_bias"].reshape(D, 1)),
        "v": pad(g["L1_attn_v_bias"].reshape(D, 1)),
        "enc": enc,
        "grid": pad(grid),
        "b2b": pad(g["L1_ffn_b2"]),
    }
    w128 = {
        "Wp": g["L0_tok_Wp"].reshape(KC, P, D).transpose(1, 0, 2).reshape(P, -1),
        "W2a": g["L0_ffn_W2"].transpose(1, 0, 2).reshape(P, -1),
        "W2b": g["L1_ffn_W2"].reshape(E1, FC1, P, D).transpose(2, 0, 1, 3).reshape(P, -1),
        "b1b": g["L1_ffn_b1"].reshape(E1, FC1, P).transpose(2, 0, 1).reshape(P, -1),
    }
    wrow = {
        "kw": g["L0_attn_kln_weight"], "kb": g["L0_attn_kln_bias"],
        "vw": g["L0_attn_vln_weight"], "vb": g["L0_attn_vln_bias"],
        "asrc": g["L0_ffn_att_src"], "adst": g["L0_ffn_att_dst"], "bgat": g["L0_ffn_b_gat"],
        "lng": g["L0_ffn_ln_gamma"], "lnb": g["L0_ffn_ln_beta"], "g1": g["L1_attn_ln_gamma"], "be1": g["L1_attn_ln_beta"],
        "b2a": g["L0_ffn_b2"], "bg": g["L1_ffn_bg"],
    }

    def packed(parts, widths):
        for k, w in widths.items():
            assert parts[k].shape[1] == w, (k, parts[k].shape, w)
        return np.ascontiguousarray(np.concatenate([parts[k] for k in widths], 1))
    arrays = {
        "pixels": np.ascontiguousarray(x),
        "edge_list": np.ascontiguousarray(a["L0_ffn_edge_index"]),
        "w128": packed(w128, PK128), "w65": packed(w65, PK65),
        "wrow": packed({k: v.reshape(1, -1) for k, v in wrow.items()}, PROW),
        "w_up_1": np.ascontiguousarray(np.concatenate([g["L1_ffn_Wg"], g["L1_ffn_W1"].transpose(1, 0, 2).reshape(D, -1)], 1)),
        "consts": packed(c, CST),
    }
    nc = bacc.Bacc("TRN2", target_bir_lowering=False, num_devices=1)
    args = [nc.dram_tensor(k, v.shape, mybir.dt.from_np(v.dtype), kind="ExternalInput").ap() for k, v in arrays.items()]
    out = nc.dram_tensor("out", (M, D), F32, kind="ExternalOutput").ap()
    vit_tower(nc, *args, out)
    r = run_bass_kernel_spmd(nc, [arrays], core_ids=[0])
    return r.results[0]["out"].reshape(NIMG, NTOK, D)
```

```python
from contextlib import ExitStack

import concourse.bass as bass
from concourse import mybir

F32 = mybir.dt.float32
I32 = mybir.dt.int32
BF16 = mybir.dt.bfloat16
ALU = mybir.AluOpType
ACT = mybir.ActivationFunctionType
AX = mybir.AxisListType

P = 128
D = 64
NIMG = 64
NTOK = 64
M = NIMG * NTOK
NT = M // P
KP = 3 * 16 * 16
KC = KP // P
NE = 262144
EC = NE // P
H0, HC0 = 8, 8
GH, GE = 4, 4
F0 = 128
H1, HD1 = 4, 16
E1, F1 = 8, 256
FC1 = F1 // P
EPS = 1e-5
BIG = 1e30
PAD = float(1 << 24)
ROW = 2 * (GH * GE + GH)
HF = ROW // 2
NUP = E1 + E1 * F1
NREL = 2 * NTOK - 1
CUTS = ((32, 16), (128, 32), (EC, 256))
STEP = 512
LEAD = 3
SHORT = P * CUTS[-1][1] + LEAD * STEP
ZR = 4

PK128 = {"Wp": KC * D, "W2a": GE * D, "W2b": E1 * FC1 * D, "b1b": E1 * FC1}
PK65 = {"pos1": D, "pos2": D, "Wgat": GH * GE, "W1a": GE * F0, "Wq": D, "Wk": D, "Wv": D, "Wpos": D,
        "Wo": D, "u": 1, "v": 1, "enc": NREL, "grid": P, "b2b": D}
PROW = {"kw": D, "kb": D, "vw": D, "vb": D, "asrc": GH * GE, "adst": GH * GE, "bgat": GH * GE,
        "lng": GH * GE, "lnb": GH * GE, "g1": D, "be1": D, "b2a": GE * D, "bg": E1}
CST = {"ident": P, "sign": 7, "iota": P, "upto": P, "kvmask": P, "hcol": H1, "vmask": D, "lowa": GE * GE,
       "lowb": E1 * E1, "pick": E1, "fold": D, "lane": 1, "hi4": 1, "head": HF}


def columns(widths):
    at, out = 0, {}
    for name, w in widths.items():
        out[name] = (at, at + w)
        at += w
    return out, at


C128, N128 = columns(PK128)
C65, N65 = columns(PK65)
CROW, NROW = columns(PROW)
CCST, NCST = columns(CST)


def spread(ap, dim, shape):
    return ap.unsqueeze(dim).to_broadcast(shape)


def wait_reg(eng, sem, value):
    eng.wait_ge(sem, value)
    eng.nop(nofuse=True)


class Chain:

    def __init__(self, eng, sem):
        self.eng, self.sem, self.n = eng, sem, 0

    def link(self, ins):
        self.n += 1
        ins.then_inc(self.sem, 1)
        self.eng.wait_ge(self.sem, self.n)


def vit_tower(nc, x, edges, w128, w65, wrow, w1b, cst, out):
    ctx = ExitStack()
    with ctx:
        def sb(name, shape, dt=F32):
            return ctx.enter_context(nc.sbuf_tensor(name, shape, dt))

        def sem(name):
            return ctx.enter_context(nc.semaphore(name))

        Ht = sb("h_run", [P, NT * D])
        Zt = sb("z_norm", [P, NT * D])
        Ct = sb("centred", [P, NT * D])
        St = sb("squares", [P, NT * D])
        zt_mem = sb("z_T", [P, M])
        ZT = zt_mem[0:D + 1, :]
        R = sb("arena", [P, 20480])
        w128s = sb("w128s", [P, N128])
        w65s = sb("w65s", [D + 1, N65])
        wup = sb("w_up", [P, NUP])
        wup3 = sb("w_up3", [P, 3, NUP], BF16)
        rows = sb("rows_s", [P, NROW])
        consts = sb("consts_s", [P, NCST])
        mean = sb("mean", [P, NT * H0])
        var = sb("var", [P, NT * H0])
        ones = sb("ones", [P, P])
        cnt = sb("cnt", [P, NT])
        as_ = sb("a_src", [P, NT, GH])
        ad_ = sb("a_dst", [P, NT, GH])
        HG = sb("h_gat", [P, NT, GH * GE])
        ad3 = sb("a_dst3", [P, 3, NT, GH], BF16)
        zero_rows = sb("zero_rows", [P, ZR * ROW])
        node_at = sb("node_at", [P, NT], I32)
        gates = sb("gates", [P, NT, E1])
        nreal = sb("n_real", [1, 2], I32)
        PS = ctx.enter_context(nc.psum_tensor("psum", [P, 4096], F32))

        h3 = Ht[:, :].rearrange("p (t d) -> p t d", d=D)
        z3 = Zt[:, :].rearrange("p (t d) -> p t d", d=D)
        c3 = Ct[:, :].rearrange("p (t d) -> p t d", d=D)
        s3 = St[:, :].rearrange("p (t d) -> p t d", d=D)

        def bank(b):
            return PS[:, b * 512:(b + 1) * 512]

        def W128(n):
            return w128s[:, C128[n][0]:C128[n][1]]

        def W65(n, k=D + 1):
            return w65s[0:k, C65[n][0]:C65[n][1]]

        def RO(n):
            return rows[:, CROW[n][0]:CROW[n][1]]

        def CS(n, k=P):
            return consts[0:k, CCST[n][0]:CCST[n][1]]

        ident = CS("ident")

        ts_d = nc.dram_tensor("src_rows", [M, ROW], F32).ap()
        run_d = nc.dram_tensor("running_rows", [NE + LEAD * STEP, ROW], F32).ap()
        neg_d = nc.dram_tensor("restart_row", [NE + STEP], F32).ap()
        lo_row = nc.dram_tensor("dst_low_row", [NE + 2 * STEP], BF16).ap()
        hi_row = nc.dram_tensor("dst_high_row", [NE + 2 * STEP], BF16).ap()
        skew_d = nc.dram_tensor("skew", [M * H1 * NREL], F32).ap()

        keyA = R[:, 0:2048]
        keyB = R[:, 2048:4096]
        s_ln = sem("s_ln")
        s_std = sem("s_std")
        n_ln = [0]

        def either(e, short, full):
            dense_ = e.value_load(nreal[0:1, 1:2], min_val=0, max_val=P)
            with e.If(dense_ < 1):
                short()
            with e.If(dense_ > 0):
                full()

        def clear(e, first, last):
            dst = run_d[first:last, :].rearrange("(p n z) r -> p n (z r)", p=P, z=ZR)
            return e.dma_start(dst, spread(zero_rows[:, :], 1, [P, (last - first) // P // ZR, ZR * ROW]))

        def layernorm(e, ch, xin, z, groups, width, unbiased=False):
            m, v = mean[:, 0:groups], var[:, 0:groups]
            cg = Ct[:, :].rearrange("p (g d) -> p g d", d=width)
            sg = St[:, :].rearrange("p (g d) -> p g d", d=width)
            ch.link(nc.vector.reduce_sum(m, xin, AX.X))
            ch.link(nc.vector.tensor_scalar(m, m, -1.0 / width, None, ALU.mult))
            ch.link(nc.vector.tensor_tensor(cg, xin, spread(m, 2, [P, groups, width]), ALU.add))
            ch.link(nc.vector.tensor_tensor(sg, cg, cg, ALU.mult))
            ch.link(nc.vector.reduce_sum(v, sg, AX.X))
            n_ln[0] += 1
            if unbiased:
                nc.vector.tensor_scalar(v, v, 1.0 / (width - 1), None, ALU.mult).then_inc(s_ln, 1)
            else:
                nc.vector.tensor_scalar(v, v, 1.0 / width, EPS, ALU.mult, ALU.add).then_inc(s_ln, 1)
            e.wait_ge(s_std, n_ln[0])
            if unbiased:
                ch.link(nc.vector.tensor_scalar(v, v, EPS, None, ALU.add))
            ch.link(nc.vector.reciprocal(v, v))
            ch.link(nc.vector.tensor_tensor(z, cg, spread(v, 2, [P, groups, width]), ALU.mult))

        n_root = [0]

        def root(e, groups):
            n_root[0] += 1
            e.wait_ge(s_ln, n_root[0])
            nc.scalar.sqrt(var[:, 0:groups], var[:, 0:groups]).then_inc(s_std, 1)

        def gating(e, ch, sc, n, low, s_x, s_e, k):
            A = R[:, 0:NT * n * n].rearrange("p (t i j) -> p t i j", i=n, j=n)
            B = R[:, 2048:2048 + NT * n * n].rearrange("p (t i j) -> p t i j", i=n, j=n)
            rank = R[:, 4096:4096 + NT * n].rearrange("p (t i) -> p t i", i=n)
            top = R[:, 4608:4608 + NT]
            full = [P, NT, n, n]
            xj, xi = spread(sc, 2, full), spread(sc, 3, full)
            nc.vector.tensor_tensor(A, xj, xi, ALU.is_gt).then_inc(ch.sem, 1)
            ch.n += 1
            ch.link(nc.vector.tensor_tensor(B, xj, xi, ALU.is_equal))
            lo = spread(low, 1, [P, NT, n * n]).rearrange("p t (i j) -> p t i j", i=n)
            ch.link(nc.vector.tensor_tensor(B, B, lo, ALU.mult))
            ch.link(nc.vector.tensor_tensor(A, A, B, ALU.add))
            ch.link(nc.vector.reduce_sum(rank, A, AX.X))
            ch.link(nc.vector.tensor_scalar(rank, rank, 1.5, None, ALU.is_lt))
            ch.link(nc.vector.reduce_max(top, sc, AX.X))
            nc.vector.tensor_tensor(sc, sc, spread(top, 2, [P, NT, n]), ALU.subtract).then_inc(s_x, 1)
            e.wait_ge(s_e, k)
            ch.link(nc.vector.tensor_tensor(sc, sc, rank, ALU.mult))
            ch.link(nc.vector.reduce_sum(top, sc, AX.X))
            ch.link(nc.vector.reciprocal(top, top))
            ch.link(nc.vector.tensor_tensor(sc, sc, spread(top, 2, [P, NT, n]), ALU.mult))

        def transpose_z(e, s_z, s_bank, s_free, z_count):
            e.wait_ge(s_z, z_count)
            for t in range(NT):
                ins = nc.tensor.transpose(PS[0:D, t * P:(t + 1) * P], z3[:, t, :], ident)
                if t % 4 == 3:
                    ins.then_inc(s_bank, 1)

        def copy_zT(e, s_bank, base, s_zT):
            for b in range(8):
                e.wait_ge(s_bank, base + b + 1)
                nc.scalar.copy(ZT[0:D, b * 512:(b + 1) * 512], PS[0:D, b * 512:(b + 1) * 512]).then_inc(s_zT, 1)

        xbuf = [R[:, 10240 + i * 3072:10240 + (i + 1) * 3072].rearrange("p (c t) -> p c t", c=KC) for i in (0, 1)]
        e_src = R[:, 4096:6144].bitcast(I32)
        e_dst = R[:, 6144:8192].bitcast(I32)
        lo_d = R[:, 8192:9216].bitcast(BF16)
        hi_d = R[:, 9216:10240].bitcast(BF16)
        one_lo = [Zt[:, :].bitcast(BF16).rearrange("p (l k) -> p l k", k=64),
                  Ct[:, :].bitcast(BF16).rearrange("p (l k) -> p l k", k=64)]
        one_hi = [St[:, :].bitcast(BF16).rearrange("p (l k) -> p l k", k=64),
                  R[:, 18432:20480].bitcast(BF16).rearrange("p (l k) -> p l k", k=64)]
        iota_lk = keyB.bitcast(BF16).rearrange("p (l k) -> p l k", k=64)
        pos_l = sb("pos_l", [D + 2, P])
        pos_r = sb("pos_r", [D + 2, D])
        rc = sb("real_count", [P, 2])
        blocks = sb("block_counts", [P, EC // CUTS[0][0]])
        dense = sb("dense", [P, 3])
        zeros = sb("zeros", [P, P], BF16)
        EARLY, LATE = 24, 8
        HB = EC // (EARLY + LATE)

        def hots(b, cols, ready):
            nc.vector.tensor_tensor(one_lo[b], spread(lo_d[:, cols], 1, [P, 64, HB]), iota_lk, ALU.is_equal)
            nc.vector.tensor_tensor(one_hi[b], spread(hi_d[:, cols], 1, [P, 64, HB]), iota_lk,
                                    ALU.is_equal).then_inc(ready, 1)
        with ExitStack() as c1, nc.Block() as block:
            def sm(n):
                return c1.enter_context(nc.semaphore(n))
            s_pack, s_edge = sm("s_pack"), sm("s_edge")
            s_x = [sm("s_x0"), sm("s_x1")]
            s_xused, s_hid, s_posl, s_posones, s_ones = sm("s_xused"), sm("s_hid"), sm("s_posl"), sm("s_posones"), sm("s_ones")
            s_tok, s_v, s_hot, s_hotused, s_cnt, s_cntc, s_rc, s_rsum = (sm("s_tok"), sm("s_v1"), sm("s_hot"), sm("s_hotused"),
                                                                  sm("s_cnt"), sm("s_cntc"), sm("s_rc"), sm("s_rsum"))
            s_h = sm("s_h")
            NG = M // 512

            @block.sync
            def _(e):
                e.dma_start(e_src, edges[0, :].rearrange("(p c) -> p c", p=P)).then_inc(s_edge, 16)
                e.dma_start(e_dst, edges[1, :].rearrange("(p c) -> p c", p=P)).then_inc(s_edge, 16)
                for g in range(NG):
                    if g >= 2:
                        e.wait_ge(s_xused, g - 1)
                    e.dma_start(xbuf[g % 2], x[:, :, g * 512:(g + 1) * 512]).then_inc(s_x[g % 2], 16)

            @block.scalar
            def _(e):
                e.dma_start(consts[:, :], cst).then_inc(s_pack, 16)
                e.dma_start(w65s[:, :], w65).then_inc(s_pack, 16)
                e.dma_start(w128s[:, :], w128).then_inc(s_pack, 16)
                e.dma_start(rows[:, :], wrow.to_broadcast([P, NROW])).then_inc(s_pack, 16)
                e.dma_start(pos_r[0:D + 1, :], w65[:, C65["pos2"][0]:C65["pos2"][1]]).then_inc(s_pack, 16)
                e.dma_start(pos_r[D + 1:D + 2, :], w65[D:D + 1, C65["pos1"][0]:C65["pos1"][1]]).then_inc(s_pack, 16)
                for half in (0, 1):
                    e.dma_start(wup[half * D:(half + 1) * D, :], w1b).then_inc(s_pack, 16)
                e.wait_ge(s_hid, 1)
                nc.scalar.activation(pos_l[0:D, :], PS[0:D, 7 * 512:7 * 512 + P], ACT.Relu).then_inc(s_posl, 1)
                for b in range(4):
                    e.wait_ge(s_tok, b + 1)
                    nc.scalar.copy(Ht[:, b * 512:(b + 1) * 512], bank(b)).then_inc(s_h, 1)

            @block.tensor
            def _(e):
                e.wait_ge(s_pack, 128)
                nc.tensor.matmul(PS[0:D, 7 * 512:7 * 512 + P], W65("pos1", 3), W65("grid", 3),
                                 start=True, stop=True).then_inc(s_hid, 1)
                acc = PS[0:64, 4 * 512:4 * 512 + 64]
                wp = W128("Wp").rearrange("p (c d) -> p c d", c=KC)
                e.wait_ge(s_posl, 1)
                e.wait_ge(s_posones, 1)
                nc.tensor.matmul(acc, zeros[:, 0:D], zeros[:, 0:D], start=True, stop=False)
                with e.Fori(0, NG // 2) as i:
                    for j in range(8):
                        if j % 4 == 0:
                            wait_reg(e, s_x[j // 4], i * 16 + 16)
                        o = PS[:, bass.ds(i * 512 + j * D, D)]
                        for c in range(KC):
                            ins = nc.tensor.matmul(o, xbuf[j // 4][:, c, (j % 4) * P:(j % 4 + 1) * P], wp[:, c, :],
                                                   start=(c == 0), stop=False)
                        if j % 4 == 3:
                            ins.then_inc(s_xused, 1)
                        ins = nc.tensor.matmul(o, pos_l[:, :], pos_r[:, :], start=False, stop=True)
                        if j == 7:
                            ins.then_inc(s_tok, 1)
                        if j >= EARLY // 4:
                            continue
                        wait_reg(e, s_hot, i * (EARLY // 4) + (j + 1))
                        for k in range(HB):
                            ins = nc.tensor.matmul(acc, one_lo[j % 2][:, :, k], one_hi[j % 2][:, :, k], start=False, stop=False)
                        ins.then_inc(s_hotused, 1)
                nc.tensor.matmul(acc, zeros[:, 0:D], zeros[:, 0:D], start=False, stop=True).then_inc(s_cnt, 1)
                e.wait_ge(s_rc, 1)
                e.wait_ge(s_ones, 1)
                nc.tensor.matmul(PS[0:1, 6 * 512:6 * 512 + 2], ones[:, 0:1], rc[:, :], start=True, stop=True).then_inc(s_rsum, 1)

            @block.vector
            def _(e):
                ch = Chain(e, s_v)
                nc.vector.memset(zeros[:, :], 0.0)
                nc.vector.memset(pos_l[D:D + 2, :], 1.0).then_inc(s_posones, 1)
                nc.vector.memset(ones[:, :], 1.0).then_inc(s_ones, 1)
                nc.vector.memset(ZT[D:D + 1, :], 1.0)
                e.wait_ge(s_edge, 32)
                srcf, dstf = Zt[:, :], Ct[:, :]
                ch.link(nc.vector.tensor_copy(srcf, e_src))
                ch.link(nc.vector.tensor_copy(dstf, e_dst))
                ch.link(nc.vector.scalar_tensor_tensor(keyA, dstf, float(M), srcf, ALU.mult, ALU.add))
                ch.link(nc.vector.tensor_scalar(keyB, srcf, float(M - 1), PAD, ALU.is_ge, ALU.mult))
                ch.link(nc.vector.tensor_tensor(keyA, keyA, keyB, ALU.add))
                ch.link(nc.vector.tensor_scalar(keyA, keyA, PAD, None, ALU.min))
                ch.link(nc.vector.tensor_scalar(keyB, keyA, PAD, None, ALU.is_lt))
                ch.link(nc.vector.reduce_sum(rc[:, 0:1], keyB, AX.X))
                for i, (blk, keep) in enumerate(CUTS):
                    nb = EC // blk
                    ch.link(nc.vector.reduce_sum(blocks[:, 0:nb], keyB.rearrange("p (n b) -> p n b", b=blk), AX.X))
                    ch.link(nc.vector.reduce_max(dense[:, i:i + 1], blocks[:, 0:nb], AX.X))
                    ch.link(nc.vector.tensor_scalar(dense[:, i:i + 1], dense[:, i:i + 1], float(keep), None, ALU.is_gt))
                nc.vector.reduce_max(rc[:, 1:2], dense[:, :], AX.X).then_inc(s_rc, 1)
                lo_i, hi_i = St[:, :].bitcast(I32), R[:, 18432:20480].bitcast(I32)
                ch.link(nc.vector.tensor_scalar(lo_i, e_dst, 63, None, ALU.bitwise_and))
                ch.link(nc.vector.tensor_copy(lo_d, lo_i))
                ch.link(nc.vector.tensor_scalar(hi_i, e_dst, 6, None, ALU.arith_shift_right))
                ch.link(nc.vector.tensor_scalar(dstf, hi_i, 64.0, None, ALU.min))
                ch.link(nc.vector.tensor_scalar(srcf, srcf, float(M - 1), 64.0, ALU.is_lt, ALU.mult))
                ch.link(nc.vector.tensor_tensor(hi_d, dstf, srcf, ALU.add))
                e.wait_ge(s_pack, 128)
                ch.link(nc.vector.tensor_copy(iota_lk, spread(CS("iota")[:, 0:64], 2, [P, 64, 64])))

                hots(0, slice(0, HB), s_hot)
                hots(1, slice(HB, 2 * HB), s_hot)
                with e.Fori(0, (EARLY - 2) // 2) as i:
                    for j in (0, 1):
                        wait_reg(e, s_hotused, i * 2 + 1 + j)
                        hots(j, bass.ds((i * 2 + 2 + j) * HB, HB), s_hot)
                e.wait_ge(s_cnt, 1)
                acc = PS[0:64, 4 * 512:4 * 512 + 64].rearrange("l (t b) -> l t b", b=2)
                nc.vector.tensor_copy(cnt[0:64, :], acc[:, :, 0])
                nc.vector.tensor_copy(cnt[64:128, :], acc[:, :, 1])
                e.wait_ge(s_rsum, 1)
                nc.vector.tensor_copy(nreal[:, :], PS[0:1, 6 * 512:6 * 512 + 2])

        kt = R[:, 10240:12288].rearrange("p (t d) -> p t d", d=D)
        vblk = R[:, 12288:16384].rearrange("p (t i d) -> p t i d", i=2, d=D)
        KV = R[0:D, 4096:8192].rearrange("p (t n) -> p t n", n=P)
        TS = R[:, 10240:10240 + NT * ROW].rearrange("p (t r) -> p t r", r=ROW)
        PT = [P, NT, D]
        with ExitStack() as c2, nc.Block() as block:
            def sm(n):
                return c2.enter_context(nc.semaphore(n))
            s_v, s_z, s_bank, s_zT, s_kv, s_kvp, s_kvc, s_o, s_hg, s_tab, s_out, s_zTf = (
                sm("s_v2"), sm("s_z"), sm("s_bank"), sm("s_zT"), sm("s_kv"), sm("s_kvp"), sm("s_kvc"), sm("s_o"),
                sm("s_hg"), sm("s_tab"), sm("s_tabout"), sm("s_zTf"))

            @block.vector
            def _(e):
                ch = Chain(e, s_v)
                nc.vector.memset(zero_rows[:, :], 0.0)
                nc.vector.memset(R[:, 12288:16384], 0.0).then_inc(s_v, 1)
                ch.n += 1
                layernorm(e, ch, h3, z3, NT, D)
                nc.vector.tensor_tensor(Ht[:, :], Ht[:, :], Zt[:, :], ALU.add).then_inc(s_z, 1)
                zg = Zt[:, :].rearrange("p (g d) -> p g d", d=HC0)
                layernorm(e, ch, zg, Ct[:, :].rearrange("p (g d) -> p g d", d=HC0), NT * H0, HC0, unbiased=True)
                ch.link(nc.vector.tensor_tensor(kt, c3, spread(RO("kw"), 1, PT), ALU.mult))
                ch.link(nc.vector.tensor_tensor(kt, kt, spread(RO("kb"), 1, PT), ALU.add))
                ch.link(nc.vector.tensor_tensor(s3, c3, spread(RO("vw"), 1, PT), ALU.mult))
                for i in (0, 1):
                    r = slice(64 * i, 64 * i + 64)
                    ins = nc.vector.tensor_tensor(vblk[r, :, i, :], s3[r, :, :],
                                                  spread(rows[r, CROW["vb"][0]:CROW["vb"][1]], 1, [64, NT, D]), ALU.add)
                ins.then_inc(s_kv, 1)
                for b in range(8):
                    e.wait_ge(s_kvp, b + 1)
                    nc.vector.tensor_tensor(KV[:, 4 * b:4 * b + 4, :], PS[0:D, b * 512:(b + 1) * 512].rearrange("p (t n) -> p t n", n=P),
                                            spread(CS("kvmask", D), 1, [D, 4, P]), ALU.mult).then_inc(s_kvc, 1)
                for b in range(8):
                    e.wait_ge(s_o, b + 1)
                    for i in (0, 1):
                        r = slice(64 * i, 64 * i + 64)
                        o = PS[r, b * 512:(b + 1) * 512].rearrange("p (t i d) -> p t i d", i=2, d=D)[:, :, i, :]
                        ins = nc.vector.tensor_tensor(h3[r, 4 * b:4 * b + 4, :], h3[r, 4 * b:4 * b + 4, :], o, ALU.add)
                        if (b, i) != (7, 1):
                            ins.then_inc(s_v, 1)
                            ch.n += 1
                ch.link(ins)
                layernorm(e, ch, h3, z3, NT, D)
                e.sem_inc(s_z, 1)
                e.wait_ge(s_hg, 1)
                ch.link(nc.vector.tensor_copy(HG[:, :, :], bank(0).rearrange("p (t f) -> p t f", f=GH * GE)))
                G4 = [P, NT, GH, GE]
                for name, a, scratch in (("asrc", as_, s3), ("adst", ad_, c3)):
                    pr = scratch[:, :, 0:GH * GE]
                    ch.link(nc.vector.tensor_tensor(pr, HG[:, :, :], spread(RO(name), 1, [P, NT, GH * GE]), ALU.mult))
                    ch.link(nc.vector.reduce_sum(a[:, :, :], pr.rearrange("p t (h e) -> p t h e", h=GH), AX.X))
                nc.vector.tensor_copy(TS[:, :, 0:16].rearrange("p t (h e) -> p t h e", h=GH), spread(as_[:, :, :], 3, G4))
                nc.vector.tensor_copy(TS[:, :, 16:20], as_[:, :, :])
                low = s3[:, :, 0:GH]
                ch.link(nc.vector.tensor_copy(ad3[:, 0, :, :], ad_[:, :, :]))
                ch.link(nc.vector.tensor_tensor(low, ad_[:, :, :], ad3[:, 0, :, :], ALU.subtract))
                ch.link(nc.vector.tensor_copy(ad3[:, 1, :, :], low))
                ch.link(nc.vector.tensor_tensor(low, low, ad3[:, 1, :, :], ALU.subtract))
                ch.link(nc.vector.tensor_copy(ad3[:, 2, :, :], low))
                nc.vector.tensor_copy(TS[:, :, 20:36], HG[:, :, :])
                nc.vector.memset(TS[:, :, 36:40], 1.0).then_inc(s_tab, 1)

            @block.scalar
            def _(e):
                root(e, NT)
                root(e, NT * H0)
                copy_zT(e, s_bank, 0, s_zT)
                root(e, NT)
                copy_zT(e, s_bank, 8, s_zT)

            @block.tensor
            def _(e):
                transpose_z(e, s_z, s_bank, None, 1)
                e.wait_ge(s_kv, 1)
                for t in range(NT):
                    if t % 4 == 0:
                        e.wait_ge(s_zT, t // 4 + 1)
                    ins = nc.tensor.matmul(PS[0:D, t * P:(t + 1) * P], kt[:, t, :],
                                           vblk[:, t, :, :].rearrange("p i d -> p (i d)"), start=True, stop=True)
                    if t % 4 == 3:
                        ins.then_inc(s_kvp, 1)
                for t in range(NT):
                    if t % 4 == 0:
                        e.wait_ge(s_kvc, t // 4 + 1)
                    ins = nc.tensor.matmul(PS[:, t * P:(t + 1) * P], ZT[0:D, t * P:(t + 1) * P], KV[:, t, :], start=True, stop=True)
                    if t % 4 == 3:
                        ins.then_inc(s_o, 1)
                transpose_z(e, s_z, s_bank, None, 2)
                e.wait_ge(s_zT, 16)
                for t in range(NT):
                    ins = nc.tensor.matmul(PS[:, t * 16:(t + 1) * 16], ZT[0:D, t * P:(t + 1) * P], W65("Wgat", D), start=True, stop=True)
                ins.then_inc(s_hg, 1)

            @block.sync
            def _(e):
                e.wait_ge(s_kv, 1)
                clear(e, 0, SHORT).then_inc(s_out, 16)
                e.wait_ge(s_tab, 1)
                e.dma_start(ts_d.rearrange("(t p) r -> p t r", p=P), TS).then_inc(s_out, 16)
                e.wait_ge(s_out, 32)

        Y = [R[:, 10240 + i * 2048:10240 + (i + 1) * 2048].rearrange("p (t d) -> p t d", d=D) for i in range(GE)]
        hid = [sb(f"hid{i}", [P, 512]) for i in range(2)]
        keys = [keyA, keyB]

        def merges(bits, first, last, w):
            return [("swap", j, k if k < bits else None, w) for k in range(first, last + 1) for j in range(k - 1, -1, -1)]

        def across(bits, w):
            plan = [("sign", 0, w)] + [("swap", j, None, w) for j in range(bits - 1, -1, -1)] + [("sign", 0, w)]
            for k in range(bits + 1, bits + 8):
                b = k - bits if k < bits + 7 else None
                plan += [("turn", None, w)] + [("swap", j, b, w) for j in range(k - bits - 1, -1, -1)] + [("turn", b, w)]
                plan += [("swap", j, None, w) for j in range(bits - 1, -1, -1)]
                if b is not None:
                    plan += [("sign", b, w)]
            return plan
        full_plan = merges(11, 1, 10, EC) + across(11, EC)
        short_plan = (merges(11, 1, 5, 2048) + [("pack", 32, 16, 2048)]
                      + merges(11, 5, 6, 1024) + [("pack", 64, 32, 1024)]
                      + merges(9, 6, 9, 512) + across(8, 256))

        def walk(plan):
            cur = n = turned = signed = 0
            for it in plan:
                yield it, cur, n, turned, signed
                if it[0] == "swap":
                    n += 4 if it[2] is not None else 2
                    cur ^= 1
                elif it[0] == "pack":
                    n += 2
                    cur ^= 1
                elif it[0] == "sign":
                    signed += 1
                else:
                    turned += max(1, it[2] // 512)
                    cur ^= 1
            yield None, cur, n, turned, signed

        idxS = R[:, 4096:4096 + 2056].bitcast(I32)
        srcI = R[:, 6144:6144 + 2048].bitcast(I32)
        DF, SF = Zt, Ct
        prevc = sb("prev_col", [P, 1])
        HC = 32
        iota3 = Zt[:, :].bitcast(BF16).rearrange("p (l k) -> p l k", k=HC)
        hot_hi = [R[:, 6160 + i * 512:6672 + i * 512].bitcast(BF16).rearrange("p (l k) -> p l k", k=HC) for i in (0, 1)]
        ncnt, tot, pos, zero_c = (sb("node_edges", [P, NT]), sb("tile_edges", [P, NT]), sb("last_edge", [P, NT]), sb("zero_c", [P, NT]))
        tail_b = sb("tail_b", [1, 2 * STEP], BF16)
        tail_f = sb("tail_f", [1, STEP])
        same_t = R[:, 18432:20480]
        with ExitStack() as c3_, nc.Block() as block:
            def sm(n):
                return c3_.enter_context(nc.semaphore(n))
            s_swap, s_turn, s_back, s_sign = sm("s_swap"), sm("s_turn"), sm("s_back"), sm("s_sign")
            s_hp, s_hs, s_yp, s_y = sm("s_hp"), sm("s_hs"), sm("s_yp"), sm("s_y")
            s_v, s_d, s_shift, s_neg, s_rows, s_srcf, s_t, s_i, s_tail = (sm("s_v4"), sm("s_d"), sm("s_shift"), sm("s_neg"), sm("s_rows"),
                                                                  sm("s_srcf"), sm("s_t"), sm("s_i"), sm("s_tail"))
            s_hot3, s_used3, s_cnt3, s_ncnt, s_pref = sm("s_hot3"), sm("s_used3"), sm("s_cnt3"), sm("s_ncnt"), sm("s_pref")

            def sort_vector(e, plan):
                for it, cur, n, turned, signed in walk(plan):
                    if it is None:
                        e.wait_ge(s_swap, n)
                        return cur, n
                    src, dst = keys[cur][:, 0:it[-1]], keys[cur ^ 1][:, 0:it[-1]]
                    if it[0] == "swap":
                        _, j, k, w = it
                        if n:
                            e.wait_ge(s_swap, n)
                        if k is None:
                            pat, kw = "p (g two s) -> p g two s", dict(two=2, s=1 << j)
                            jobs = [(src.rearrange(pat, **kw), dst.rearrange(pat, **kw), ALU.min, ALU.max)]
                        else:
                            pat = "p (n up g two s) -> p n up g two s"
                            kw = dict(up=2, g=1 << (k - 1 - j), two=2, s=1 << j)
                            a, d = src.rearrange(pat, **kw), dst.rearrange(pat, **kw)
                            jobs = [(a[:, :, 0], d[:, :, 0], ALU.min, ALU.max), (a[:, :, 1], d[:, :, 1], ALU.max, ALU.min)]
                        for a, d, first, second in jobs:
                            ix = (slice(None),) * (len(a.shape) - 2)
                            lo, hi = a[ix + (0,)], a[ix + (1,)]
                            nc.vector.tensor_tensor(d[ix + (0,)], lo, hi, first).then_inc(s_swap, 1)
                            nc.vector.tensor_tensor(d[ix + (1,)], lo, hi, second).then_inc(s_swap, 1)
                    elif it[0] == "pack":
                        _, blk, keep, w = it
                        e.wait_ge(s_swap, n)
                        a = src.rearrange("p (n up b) -> p n up b", up=2, b=blk)
                        d = dst[:, 0:w * keep // blk].rearrange("p (n up b) -> p n up b", up=2, b=keep)
                        nc.vector.tensor_copy(d[:, :, 0], a[:, :, 0, 0:keep]).then_inc(s_swap, 1)
                        nc.vector.tensor_copy(d[:, :, 1], a[:, :, 1, blk - keep:]).then_inc(s_swap, 1)
                    elif it[0] == "sign":
                        e.wait_ge(s_sign, signed + 1)
                    else:
                        e.wait_ge(s_back, turned + max(1, it[2] // 512))

            NR3, TURNS = 8 * GE, 14
            AHEAD = NR3 - TURNS

            def between(step):
                def after(k):
                    step(AHEAD + k)
                    if k == TURNS - 1:
                        step(NR3)
                return after

            def expert_scalar(e):
                def step(i):
                    if i < NR3:
                        e.wait_ge(s_hp, i + 1)
                        if i >= 2:
                            e.wait_ge(s_yp, i - 1)
                        nc.scalar.activation(hid[i % 2][:, :], bank(4 + i % 2), ACT.Gelu).then_inc(s_hs, 1)
                    if i:
                        g, x_ = divmod(i - 1, GE)
                        e.wait_ge(s_yp, i)
                        nc.scalar.copy(Y[x_][:, 4 * g:4 * g + 4, :],
                                       PS[:, (6 + (i - 1) % 2) * 512:(6 + (i - 1) % 2) * 512 + 256].rearrange("p (t d) -> p t d", d=D)).then_inc(s_y, 1)
                return step

            def expert_tensor(e):
                w1 = W65("W1a").rearrange("p (e f) -> p e f", e=GE)
                w2 = W128("W2a").rearrange("p (e d) -> p e d", e=GE)

                def step(i):
                    if i < NR3:
                        g, x_ = divmod(i, GE)
                        if i >= 2:
                            e.wait_ge(s_hs, i - 1)
                        nc.tensor.matmul(bank(4 + i % 2), w1[:, x_, :], ZT[:, g * 512:(g + 1) * 512], start=True, stop=True).then_inc(s_hp, 1)
                    if i:
                        r = i - 1
                        x_ = r % GE
                        e.wait_ge(s_hs, i)
                        if r >= 2:
                            e.wait_ge(s_y, r - 1)
                        b2 = rows[0:1, CROW["b2a"][0] + x_ * D:CROW["b2a"][0] + (x_ + 1) * D]
                        o = PS[:, (6 + r % 2) * 512:(6 + r % 2) * 512 + 4 * D].rearrange("p (t d) -> p t d", d=D)
                        nc.tensor.matmul(o, ones[0:1, :], spread(b2, 1, [1, 4, D]), start=True, stop=False)
                        for j in range(4):
                            ins = nc.tensor.matmul(o[:, j, :], hid[r % 2][:, j * P:(j + 1) * P], w2[:, x_, :], start=False, stop=(j == 3))
                        ins.then_inc(s_yp, 1)
                return step

            def sort_scalar(e, plan, after):
                k = 0
                for it, cur, n, turned, signed in walk(plan):
                    if it is None:
                        return
                    if it[0] in ("sign", "turn") and it[1] is not None:
                        s = consts[:, CCST["sign"][0] + it[1]:CCST["sign"][0] + it[1] + 1]
                    if it[0] == "sign":
                        w = it[2]
                        e.wait_ge(s_swap, n)
                        nc.scalar.mul(keys[cur][:, 0:w], keys[cur][:, 0:w], s).then_inc(s_sign, 1)
                    elif it[0] == "turn":
                        w = min(it[2], 512)
                        for c in range(it[2] // w):
                            e.wait_ge(s_turn, turned + c + 1)
                            o, i_ = keys[cur ^ 1][:, c * w:(c + 1) * w], PS[:, c * w:(c + 1) * w]
                            if it[1] is None:
                                nc.scalar.copy(o, i_).then_inc(s_back, 1)
                            else:
                                nc.scalar.mul(o, i_, s).then_inc(s_back, 1)
                        after(k)
                        k += 1

            def sort_tensor(e, plan, after):
                k = 0
                for it, cur, n, turned, signed in walk(plan):
                    if it is None:
                        return
                    if it[0] == "turn":
                        w = it[2]
                        e.wait_ge(s_swap, n)
                        if signed:
                            e.wait_ge(s_sign, signed)
                        if turned:
                            e.wait_ge(s_back, turned)
                        per = min(w, 512) // P
                        for c in range(w // P):
                            ins = nc.tensor.transpose(PS[:, c * P:(c + 1) * P], keys[cur][:, c * P:(c + 1) * P], ident)
                            if c % per == per - 1:
                                ins.then_inc(s_turn, 1)
                        after(k)
                        k += 1

            def columns_vector(e, w, cur, n):
                ch = Chain(e, s_v)
                K, other = keys[cur][:, 0:w], keys[cur ^ 1][:, 0:w]
                ki, di, si = other.bitcast(I32), idxS[:, 0:w], srcI[:, 0:w]
                d, sf, same = DF[:, 0:w], SF[:, 0:w], same_t[:, 0:w]
                nc.vector.memset(tail_b[:, :], 0.0)
                nc.vector.memset(tail_f[:, :], 0.0).then_inc(s_tail, 1)
                ch.link(nc.vector.tensor_copy(ki, K))
                ch.link(nc.vector.tensor_scalar(di, ki, 12, None, ALU.arith_shift_right))
                nc.vector.memset(prevc[:, :], -1.0)
                nc.vector.tensor_copy(d, di).then_inc(s_d, 1)
                ch.link(nc.vector.tensor_scalar(si, ki, M - 1, None, ALU.bitwise_and))
                nc.vector.tensor_copy(sf, si).then_inc(s_srcf, 1)
                lo_b, hi_b = K.bitcast(BF16)[:, 0:w], K.bitcast(BF16)[:, w:2 * w]
                ch.link(nc.vector.tensor_scalar(ki, di, P - 1, None, ALU.bitwise_and))
                ch.link(nc.vector.tensor_copy(lo_b, ki))
                ch.link(nc.vector.tensor_scalar(ki, di, 7, None, ALU.arith_shift_right))
                nc.vector.tensor_copy(hi_b, ki).then_inc(s_neg, 1)
                e.wait_ge(s_d, 1)
                ch.link(nc.vector.tensor_tensor(same[:, 1:], d[:, 1:], d[:, :-1], ALU.is_equal))
                e.wait_ge(s_shift, 16)
                ch.link(nc.vector.tensor_tensor(same[:, 0:1], d[:, 0:1], prevc[:, :], ALU.is_equal))
                nc.vector.tensor_scalar(same, same, 1.0, BIG, ALU.subtract, ALU.mult).then_inc(s_neg, 1)
                e.wait_ge(s_neg, 2)
                ch.link(nc.vector.tensor_copy(iota3, spread(CS("iota"), 2, [P, P, HC])))
                hot_lo = [St[:, :].bitcast(BF16).rearrange("p (l k) -> p l k", k=HC),
                          keys[cur ^ 1][:, :].bitcast(BF16).rearrange("p (l k) -> p l k", k=HC)]

                def hots(b, cols):
                    nc.vector.tensor_tensor(hot_lo[b], spread(lo_b[:, cols], 1, [P, P, HC]), iota3, ALU.is_equal)
                    nc.vector.tensor_tensor(hot_hi[b], spread(hi_b[:, cols], 1, [P, NT, HC]), iota3[:, 0:NT, :],
                                            ALU.is_equal).then_inc(s_hot3, 1)
                e.wait_ge(s_srcf, 1)
                hots(0, slice(0, HC))
                hots(1, slice(HC, 2 * HC))
                with e.Fori(0, (w // HC - 2) // 2) as i:
                    for j in (0, 1):
                        wait_reg(e, s_used3, i * 2 + 1 + j)
                        hots(j, bass.ds((i * 2 + 2 + j) * HC, HC))
                e.wait_ge(s_cnt3, 1)
                nc.vector.memset(zero_c[:, :], 0.0)
                nc.vector.tensor_copy(ncnt[:, :], bank(5)[:, 0:NT]).then_inc(s_ncnt, 1)
                e.wait_ge(s_pref, 1)
                ch.link(nc.vector.tensor_copy(tot[:, :], bank(6)[:, NT:2 * NT]))
                ch.link(nc.vector.tensor_tensor_scan(pos[:, :], tot[:, :], zero_c[:, :], zero_c[:, 0:1], ALU.add, ALU.add))
                ch.link(nc.vector.tensor_tensor(pos[:, :], pos[:, :], tot[:, :], ALU.subtract))
                ch.link(nc.vector.tensor_tensor(pos[:, :], pos[:, :], bank(6)[:, 0:NT], ALU.add))
                ch.link(nc.vector.tensor_scalar(tot[:, :], ncnt[:, :], 0.5, float(4 * NE), ALU.is_lt, ALU.mult))
                ch.link(nc.vector.tensor_tensor(pos[:, :], pos[:, :], tot[:, :], ALU.add))
                ch.link(nc.vector.tensor_scalar(pos[:, :], pos[:, :], float(LEAD * STEP - 1), None, ALU.add))
                nc.vector.tensor_copy(node_at[:, :], pos[:, :])
                e.wait_ge(s_t, 1)
                e.wait_ge(s_i, max(1, w // 512))
                nc.vector.memset(idxS[:, w:w + 8], 0)

            def columns_sync(e, w, cur):
                e.wait_ge(s_d, 1)
                with nc.allow_non_contiguous_dma(reason="one column, moved by a partition"):
                    e.dma_start(prevc[1:P, :], DF[0:P - 1, w - 1:w]).then_inc(s_shift, 16)
                e.wait_ge(s_neg, 2)
                e.wait_ge(s_tail, 1)
                K = keys[cur][:, 0:w].bitcast(BF16)
                for row, a, tail in ((lo_row, K[:, 0:w], tail_b), (hi_row, K[:, w:2 * w], tail_b), (neg_d, same_t[:, 0:w], tail_f)):
                    e.dma_start(row[0:P * w].rearrange("(p c) -> p c", p=P), a).then_inc(s_rows, 16)
                    e.dma_start(row[P * w:P * w + tail.shape[1]].unsqueeze(0), tail[:, :]).then_inc(s_rows, 16)
                if w == EC:
                    clear(e, SHORT, NE + LEAD * STEP).then_inc(s_rows, 16)
                    e.wait_ge(s_rows, 112)
                else:
                    e.wait_ge(s_rows, 96)

            def columns_tensor(e, w, cur):
                e.wait_ge(s_srcf, 1)
                for c in range(w // P):
                    ins = nc.tensor.transpose(PS[:, c * P:(c + 1) * P], SF[:, c * P:(c + 1) * P], ident)
                ins.then_inc(s_t, 1)
                acc = bank(5)[:, 0:NT]
                hot_lo = [St[:, :].bitcast(BF16).rearrange("p (l k) -> p l k", k=HC),
                          keys[cur ^ 1][:, :].bitcast(BF16).rearrange("p (l k) -> p l k", k=HC)]
                nc.tensor.matmul(acc, zeros[:, :], zeros[:, 0:NT], start=True, stop=False)
                with e.Fori(0, w // HC // 2) as i:
                    for j in (0, 1):
                        wait_reg(e, s_hot3, i * 2 + (j + 1))
                        for k in range(HC):
                            ins = nc.tensor.matmul(acc, hot_lo[j][:, :, k], hot_hi[j][:, :, k], start=False, stop=False)
                        ins.then_inc(s_used3, 1)
                nc.tensor.matmul(acc, zeros[:, :], zeros[:, 0:NT], start=False, stop=True).then_inc(s_cnt3, 1)
                e.wait_ge(s_ncnt, 1)
                nc.tensor.matmul(bank(6)[:, 0:NT], CS("upto"), ncnt[:, :], start=True, stop=True)
                nc.tensor.matmul(bank(6)[:, NT:2 * NT], ones[:, :], ncnt[:, :], start=True, stop=True).then_inc(s_pref, 1)

            def columns_scalar(e, w):
                nb = max(1, w // 512)
                e.wait_ge(s_t, 1)
                e.wait_ge(s_neg, 2)
                o = idxS[:, 0:w].rearrange("q (p c) -> q c p", c=w // P)
                for c in range(nb):
                    k = (w // P) // nb
                    nc.scalar.copy(o[:, c * k:(c + 1) * k, :],
                                   PS[:, c * 512:c * 512 + k * P].rearrange("q (c p) -> q c p", c=k)).then_inc(s_i, 1)

            @block.vector
            def _(e):
                def path(plan, w):
                    cur, n = sort_vector(e, plan)
                    columns_vector(e, w, cur, n)
                either(e, lambda: path(short_plan, 256), lambda: path(full_plan, EC))

            @block.sync
            def _(e):
                def path(plan, w):
                    for it, cur, n, turned, signed in walk(plan):
                        pass
                    columns_sync(e, w, cur)
                either(e, lambda: path(short_plan, 256), lambda: path(full_plan, EC))

            @block.scalar
            def _(e):
                step = expert_scalar(e)
                for i in range(AHEAD):
                    step(i)

                def path(plan, w):
                    sort_scalar(e, plan, between(step))
                    columns_scalar(e, w)
                either(e, lambda: path(short_plan, 256), lambda: path(full_plan, EC))

            @block.tensor
            def _(e):
                step = expert_tensor(e)
                for i in range(AHEAD):
                    step(i)

                def path(plan, w):
                    sort_tensor(e, plan, between(step))
                    e.wait_ge(s_y, NR3)
                    for it, cur, n, turned, signed in walk(plan):
                        pass
                    columns_tensor(e, w, cur)
                either(e, lambda: path(short_plan, 256), lambda: path(full_plan, EC))

        curS = sb("cur_src", [P, 2, 4], I32)
        warm = sb("warm", [P, 1])

        def two(t, at, n=512, k=HF):
            return t[0:k, at:at + 2 * n].rearrange("p (b n) -> p b n", b=2)
        Gs = R[:, 0:320].rearrange("p (b c r) -> p b c r", b=2, c=4)
        ends = R[:, 480:800].rearrange("p (b c r) -> p b c r", b=2, c=4)
        leak, ev, acc, dec, wt = two(Zt, 0), two(Zt, 1024), two(Ct, 0), two(Ct, 1024), two(St, 0)
        run = two(R, 1024, 513)
        negr = two(St, 1024)
        mk = two(R, 2052, 512, P)
        lo_s = two(R[:, 3076:3588].bitcast(BF16), 0, 512, P)
        hi_s = two(R[:, 18432:18944].bitcast(BF16), 0, 512, P)
        oh = two(R[:, 18944:19456].bitcast(BF16), 0, 512, P)
        LEVELS = (4, 4, 4, 4)
        with ExitStack() as c5, nc.Block() as block:
            def sm(n):
                return c5.enter_context(nc.semaphore(n))
            s_row, s_leak, s_ch, s_sub, s_exp, s_acc, s_tr, s_ends, s_oh, s_t1, s_msk, s_cp, s_ini = (
                sm("s_row"), sm("s_leak"), sm("s_ch5"), sm("s_sub"), sm("s_exp"), sm("s_acc"), sm("s_tr"), sm("s_ends"),
                sm("s_oh"), sm("s_t1"), sm("s_msk"), sm("s_cp"), sm("s_ini"))
            s_mul = sm("s_mul")
            s_gat, s_sc = [sm("s_gat0"), sm("s_gat1")], [sm("s_sc0"), sm("s_sc1")]
            s_lh, s_ng = [sm("s_lh0"), sm("s_lh1")], [sm("s_ng0"), sm("s_ng1")]

            def rounds(e, n, body):
                def level(base, todo, counts):
                    todo //= counts[0]
                    with e.Fori(0, counts[0]) as k:
                        g = base + k * todo if todo > 1 else base + k
                        with e.If(n > g * (2 * STEP)):
                            if len(counts) > 1:
                                level(g, todo, counts[1:])
                            else:
                                body(g)
                level(0, NE // STEP // 2, LEVELS)

            def streamed(e):
                return e.value_load(nreal[0:1, 0:1], min_val=0, max_val=NE)

            def rows_out(e, b, block_):
                e.dma_start(run_d[bass.ds(block_ * STEP, STEP), :].rearrange("(c p) f -> p c f", p=P), ends[:, b, :, :]).then_inc(s_sc[b], 16)

            @block.sync
            def _(e):
                def digits(i, b):
                    for row, t in ((lo_row, lo_s), (hi_row, hi_s)):
                        e.dma_start(t[:, b, :], row[bass.ds(i * STEP, STEP)].unsqueeze(0).to_broadcast([P, STEP])).then_inc(s_lh[b], 16)

                def restarts(i, b):
                    e.dma_start(negr[:, b, :], neg_d[bass.ds(i * STEP, STEP)].unsqueeze(0).to_broadcast([HF, STEP])).then_inc(s_ng[b], 16)
                n = streamed(e)
                digits(0, 0)
                digits(1, 1)
                restarts(0, 0)
                e.wait_ge(s_ini, 1)
                rows_out(e, 0, 0)
                rows_out(e, 1, 1)

                def body(g):
                    for b in (0, 1):
                        i = 2 * g + b
                        wait_reg(e, s_msk, i + 2)
                        digits(i + 2, b)
                        wait_reg(e, s_acc, i + 2)
                        restarts(i + 1, b ^ 1)
                        wait_reg(e, s_ends, i + 3)
                        rows_out(e, b ^ 1, i + (LEAD - 1))
                rounds(e, n, body)
                last = (n + (2 * STEP - 1)) // (2 * STEP)
                wait_reg(e, s_ends, 2 * last + 3)
                rows_out(e, 1, 2 * last + (LEAD - 1))
                wait_reg(e, s_sc[0], 16 * last + 16)
                wait_reg(e, s_sc[1], 16 * last + 32)
                wait_reg(e, s_ng[0], 16 * last + 16)

            @block.gpsimd
            def _(e):
                n = streamed(e)

                def gather(i, b, made):
                    e.tensor_copy(curS[:, b, :], idxS[:, bass.ds(i * 4, 4)] if not isinstance(i, int) else idxS[:, i * 4:i * 4 + 4]).then_inc(s_cp, 1)
                    if isinstance(made, int):
                        e.wait_ge(s_cp, made)
                    else:
                        wait_reg(e, s_cp, made)
                    for c in range(4):
                        e.indirect_dma_start(Gs[:, b, c, :], None, ts_d,
                                             bass.IndirectOffsetOnAxis(curS[:, b, c:c + 1], axis=0)).then_inc(s_gat[b], 16)

                gather(0, 0, 1)
                gather(1, 1, 2)

                def body(g):
                    for b in (0, 1):
                        i = 2 * g + b
                        wait_reg(e, s_row, i + 1)
                        gather(i + 2, b, i + 3)
                rounds(e, n, body)
                last = (n + (2 * STEP - 1)) // (2 * STEP)
                wait_reg(e, s_gat[0], 64 * last + 64)
                wait_reg(e, s_gat[1], 64 * last + 64)

            @block.tensor
            def _(e):
                T = nc.tensor

                def lookup(b):
                    for k in range(3):
                        ins = T.matmul(bank(b), ad3[:, k, :, :].rearrange("p t h -> p (t h)"), oh[:, b, :], start=(k == 0), stop=(k == 2))
                    ins.then_inc(s_t1, 1)

                def turn_in(b):
                    o = PS[0:HF, (2 + b) * 512:(3 + b) * 512]
                    T.matmul(o, CS("head"), mk[:, b, :], start=True, stop=False)
                    for c in range(4):
                        T.matmul(o[:, c * P:(c + 1) * P], Gs[:, b, c, 0:HF], ident, start=False, stop=(c == 3))
                    for c in range(4):
                        ins = T.transpose(PS[0:HF, (4 + b) * 512 + c * P:(4 + b) * 512 + (c + 1) * P], Gs[:, b, c, HF:ROW], ident)
                    ins.then_inc(s_row, 1)

                def turn_out(b):
                    for c in range(4):
                        o = (6 + b) * 512 + c * ROW
                        T.transpose(PS[:, o:o + HF], acc[:, b, c * P:(c + 1) * P], CS("ident", HF)[:, 0:HF])
                        ins = T.transpose(PS[:, o + HF:o + ROW], run[:, b, 1 + c * P:1 + (c + 1) * P], CS("ident", HF)[:, 0:HF])
                    ins.then_inc(s_tr, 1)
                n = streamed(e)
                for b in (0, 1):
                    e.wait_ge(s_oh, b + 1)
                    lookup(b)
                e.wait_ge(s_msk, 2)
                e.wait_ge(s_gat[0], 64)
                turn_in(0)

                def body(g):
                    for b in (0, 1):
                        i = 2 * g + b
                        wait_reg(e, s_msk, i + 3)
                        wait_reg(e, s_gat[b ^ 1], 64 * (g + 1 + b))
                        turn_in(b ^ 1)
                        wait_reg(e, s_acc, i + 2)
                        wait_reg(e, s_ends, i + 1)
                        turn_out(b ^ 1)
                        wait_reg(e, s_oh, i + 3)
                        lookup(b)
                rounds(e, n, body)
                last = (n + (2 * STEP - 1)) // (2 * STEP)
                wait_reg(e, s_acc, 2 * last + 2)
                wait_reg(e, s_ends, 2 * last + 1)
                turn_out(1)

            @block.scalar
            def _(e):
                n = streamed(e)

                def lay_out(b):
                    nc.scalar.copy(ends[:, b, :, :], PS[:, (6 + b) * 512:(6 + b) * 512 + 4 * ROW].rearrange("p (c f) -> p c f", c=4)).then_inc(s_ends, 1)
                e.wait_ge(s_row, 1)
                nc.scalar.mul(leak[:, 0, :], PS[0:HF, 1024:1536], 0.2).then_inc(s_leak, 1)

                def body(g):
                    nc.scalar.activation(warm[:, :], zero_c[:, 0:1], ACT.Exp)
                    for b in (0, 1):
                        i = 2 * g + b
                        wait_reg(e, s_sub, 4 * g + 2 * b + 1)
                        nc.scalar.activation(wt[:, b, :], wt[:, b, :], ACT.Exp).then_inc(s_exp, 1)
                        wait_reg(e, s_sub, 4 * g + 2 * b + 2)
                        nc.scalar.activation(dec[:, b, :], dec[:, b, :], ACT.Exp).then_inc(s_exp, 1)
                        wait_reg(e, s_row, i + 2)
                        nc.scalar.mul(leak[:, b ^ 1, :], PS[0:HF, (2 + (b ^ 1)) * 512:(3 + (b ^ 1)) * 512], 0.2).then_inc(s_leak, 1)
                        wait_reg(e, s_tr, i + 2)
                        wait_reg(e, s_sc[b ^ 1], 16 * g + 16)
                        lay_out(b ^ 1)
                rounds(e, n, body)
                last = (n + (2 * STEP - 1)) // (2 * STEP)
                wait_reg(e, s_tr, 2 * last + 2)
                wait_reg(e, s_sc[1], 16 * last + 16)
                lay_out(1)

            @block.vector
            def _(e):
                V = nc.vector
                LINKS = 4
                n = streamed(e)
                V.memset(ends[:, :, :, :], 0.0).then_inc(s_ini, 1)
                V.memset(run[:, 1, :], 0.0).then_inc(s_ch, 1)
                V.memset(acc[:, 1, :], 0.0).then_inc(s_ch, 1)
                e.wait_ge(s_ch, 2)
                for s_, k in ((s_acc, 2), (s_tr, 1), (s_ends, 2), (s_msk, 1)):
                    e.sem_inc(s_, k)

                def onehot(b):
                    V.tensor_scalar(oh[:, b, :], lo_s[:, b, :], CS("lane"), None, ALU.is_equal).then_inc(s_oh, 1)

                def mask(b):
                    V.scalar_tensor_tensor(mk[:, b, :], hi_s[:, b, :], CS("hi4"), bank(b), ALU.is_equal, ALU.mult).then_inc(s_msk, 1)
                for b in (0, 1):
                    e.wait_ge(s_lh[b], 32)
                    onehot(b)
                e.wait_ge(s_t1, 1)
                mask(0)

                def body(g):
                    for b in (0, 1):
                        i = 2 * g + b
                        made = [2 * LINKS * g + LINKS * b + 2]

                        def link(ins):
                            made[0] = made[0] + 1
                            ins.then_inc(s_ch, 1)
                            wait_reg(e, s_ch, made[0])
                        wait_reg(e, s_t1, i + 2)
                        mask(b ^ 1)
                        wait_reg(e, s_leak, i + 1)
                        wait_reg(e, s_tr, i + 1)
                        V.tensor_copy(run[:, b, 0:1], run[:, b ^ 1, 512:513]).then_inc(s_ch, 1)
                        made[0] = made[0] + 1
                        link(V.tensor_tensor(ev[:, b, :], PS[0:HF, (2 + b) * 512:(3 + b) * 512], leak[:, b, :], ALU.max))
                        wait_reg(e, s_ng[b], 16 * g + 16)
                        link(V.tensor_tensor_scan(run[:, b, 1:513], negr[:, b, :], ev[:, b, :], run[:, b, 0:1], ALU.add, ALU.max))
                        V.tensor_tensor(wt[:, b, :], ev[:, b, :], run[:, b, 1:513], ALU.subtract).then_inc(s_sub, 1)
                        link(V.tensor_tensor(dec[:, b, :], negr[:, b, :], run[:, b, 0:512], ALU.add))
                        V.tensor_tensor(dec[:, b, :], dec[:, b, :], run[:, b, 1:513], ALU.subtract).then_inc(s_sub, 1)
                        wait_reg(e, s_lh[b], 32 * g + 64)
                        onehot(b)
                        wait_reg(e, s_exp, 4 * g + 2 * b + 2)
                        V.tensor_tensor(wt[:, b, :], wt[:, b, :], PS[0:HF, (4 + b) * 512:(5 + b) * 512], ALU.mult).then_inc(s_mul, 1)
                        wait_reg(e, s_mul, i + 1)
                        V.tensor_tensor_scan(acc[:, b, :], dec[:, b, :], wt[:, b, :], acc[:, b ^ 1, 511:512], ALU.mult, ALU.add).then_inc(s_acc, 1)
                        wait_reg(e, s_acc, i + 3)
                rounds(e, n, body)

        NR = R[:, 6144:6144 + NT * ROW].rearrange("p (t r) -> p t r", r=ROW)
        c4r = sb("row_4095", [P, ROW])
        sm4 = [R[:, 7424 + i * 128:7424 + (i + 1) * 128].rearrange("p (t h) -> p t h", h=GH) for i in range(6)]
        AG = R[:, 0:512].rearrange("p (t f) -> p t f", f=GH * GE)
        A2 = R[:, 512:1024].rearrange("p (t f) -> p t f", f=GH * GE)
        PB = sb("pos_blk", [D, H1, NREL])
        with ExitStack() as c6, nc.Block() as block:
            def sm(n):
                return c6.enter_context(nc.semaphore(n))
            s_ld, s_v, s_x, s_e, s_z, s_bank, s_zT, s_pp, s_pb = (sm("s_ld"), sm("s_v6"), sm("s_x6"), sm("s_e6"), sm("s_z6"), sm("s_bank6"),
                                                             sm("s_zT6"), sm("s_pp"), sm("s_pb"))
            s_nr, s_got, s_hot6, s_used6, s_cnt6 = sm("s_nr"), sm("s_got"), sm("s_hot6"), sm("s_used6"), sm("s_cnt6")
            es, ec, er, ss, cn, tm = sm4
            G4 = [P, NT, GH]
            G16 = [P, NT, GH, GE]

            @block.sync
            def _(e):
                e.dma_start(c4r[:, :], ts_d[M - 1:M, :].to_broadcast([P, ROW])).then_inc(s_ld, 16)

            @block.gpsimd
            def _(e):
                e.wait_ge(s_nr, 2)

                def collect(rows_):
                    for t in range(NT):
                        e.indirect_dma_start(NR[:, t, :], None, run_d[0:rows_, :], bass.IndirectOffsetOnAxis(node_at[:, t:t + 1], axis=0),
                                             bounds_check=rows_ - 1, oob_is_err=False).then_inc(s_got, 16)
                either(e, lambda: collect(SHORT), lambda: collect(NE + LEAD * STEP))

            @block.scalar
            def _(e):
                for i in (0, 1, 2):
                    e.wait_ge(s_x, i + 1)
                    t = (es, ec, er)[i]
                    nc.scalar.activation(t[:, :, :], t[:, :, :], ACT.Exp).then_inc(s_e, 1)
                root(e, NT)
                e.wait_ge(s_x, 4)
                nc.scalar.activation(sm4[3][:, :, :], sm4[3][:, :, :], ACT.Exp).then_inc(s_e, 1)
                e.wait_ge(s_pp, 1)
                for h in range(H1):
                    hc = consts[0:D, CCST["hcol"][0] + h:CCST["hcol"][0] + h + 1]
                    nc.scalar.mul(PB[:, h, :], PS[0:D, 0:NREL], hc).then_inc(s_pb, 1)
                root(e, NT)
                root(e, NT)
                copy_zT(e, s_bank, 0, s_zT)

            @block.tensor
            def _(e):
                nc.tensor.matmul(PS[0:D, 0:NREL], W65("Wpos"), W65("enc"), start=True, stop=True).then_inc(s_pp, 1)
                acc = PS[0:64, 4 * 512:4 * 512 + 64]
                nc.tensor.matmul(acc, zeros[:, 0:D], zeros[:, 0:D], start=True, stop=False)
                with e.Fori(0, LATE // 2) as i:
                    for j in (0, 1):
                        wait_reg(e, s_hot6, i * 2 + (j + 1))
                        for k in range(HB):
                            ins = nc.tensor.matmul(acc, one_lo[j][:, :, k], one_hi[j][:, :, k], start=False, stop=False)
                        ins.then_inc(s_used6, 1)
                nc.tensor.matmul(acc, zeros[:, 0:D], zeros[:, 0:D], start=False, stop=True).then_inc(s_cnt6, 1)
                e.wait_ge(s_pb, H1)
                transpose_z(e, s_z, s_bank, None, 1)

            @block.vector
            def _(e):
                ch = Chain(e, s_v)
                V = nc.vector
                V.memset(NR[:, :, 0:HF], 0.0).then_inc(s_nr, 1)
                V.memset(NR[:, :, HF:ROW], -BIG).then_inc(s_nr, 1)
                ch.link(V.tensor_copy(iota_lk, spread(CS("iota")[:, 0:64], 2, [P, 64, 64])))
                hots(0, slice(EARLY * HB, (EARLY + 1) * HB), s_hot6)
                hots(1, slice((EARLY + 1) * HB, (EARLY + 2) * HB), s_hot6)
                with e.Fori(0, (LATE - 2) // 2) as i:
                    for j in (0, 1):
                        wait_reg(e, s_used6, i * 2 + 1 + j)
                        hots(j, bass.ds((i * 2 + (EARLY + 2 + j)) * HB, HB), s_hot6)
                e.wait_ge(s_cnt6, 1)
                for i in (0, 1):
                    part = PS[0:64, 4 * 512:4 * 512 + 64].rearrange("l (t b) -> l t b", b=2)[:, :, i]
                    half = cnt[64 * i:64 * i + 64, :]
                    ch.link(V.tensor_tensor(half, half, part, ALU.add))
                e.wait_ge(s_ld, 16)
                ch.link(V.tensor_tensor(es[:, :, :], as_[:, :, :], ad_[:, :, :], ALU.add))
                ch.link(V.tensor_tensor(ec[:, :, :], ad_[:, :, :], spread(c4r[:, 16:20], 1, G4), ALU.add))
                for t in (es, ec):
                    ch.link(V.tensor_scalar(tm[:, :, :], t[:, :, :], 0.2, None, ALU.mult))
                    ch.link(V.tensor_tensor(t[:, :, :], t[:, :, :], tm[:, :, :], ALU.max))
                ch.link(V.tensor_scalar(cn[:, :, 0], cnt[:, :], 0.5, 1.0, ALU.is_ge, ALU.subtract))
                ch.link(V.tensor_scalar(cn[:, :, 0], cn[:, :, 0], BIG, None, ALU.mult))
                ch.link(V.tensor_tensor(ec[:, :, :], ec[:, :, :], cn[:, :, 0:1].to_broadcast(G4), ALU.add))
                RM = NR[:, :, HF + 16:HF + 20]
                ch.link(V.tensor_tensor(tm[:, :, :], es[:, :, :], ec[:, :, :], ALU.max))
                e.wait_ge(s_got, 16 * NT)
                ch.link(V.tensor_tensor(tm[:, :, :], tm[:, :, :], RM, ALU.max))
                V.tensor_tensor(es[:, :, :], es[:, :, :], tm[:, :, :], ALU.subtract).then_inc(s_x, 1)
                V.tensor_tensor(ec[:, :, :], ec[:, :, :], tm[:, :, :], ALU.subtract).then_inc(s_x, 1)
                V.tensor_tensor(er[:, :, :], RM, tm[:, :, :], ALU.subtract).then_inc(s_x, 1)
                e.wait_ge(s_e, 3)
                ch.link(V.tensor_tensor(ec[:, :, :], ec[:, :, :], spread(cnt[:, :], 2, G4), ALU.mult))
                ch.link(V.tensor_tensor(ss[:, :, :], es[:, :, :], ec[:, :, :], ALU.add))
                ch.link(V.tensor_tensor(tm[:, :, :], er[:, :, :], NR[:, :, 16:20], ALU.mult))
                ch.link(V.tensor_tensor(ss[:, :, :], ss[:, :, :], tm[:, :, :], ALU.add))
                ch.link(V.tensor_scalar(ss[:, :, :], ss[:, :, :], 1e-16, None, ALU.add))
                ch.link(V.reciprocal(ss[:, :, :], ss[:, :, :]))
                ag = AG[:, :, :].rearrange("p t (h e) -> p t h e", h=GH)
                a2 = A2[:, :, :].rearrange("p t (h e) -> p t h e", h=GH)
                ch.link(V.tensor_tensor(ag, HG[:, :, :].rearrange("p t (h e) -> p t h e", h=GH), spread(es[:, :, :], 3, G16), ALU.mult))
                c16 = spread(c4r[:, HF:HF + 16], 1, [P, NT, 16]).rearrange("p t (h e) -> p t h e", h=GH)
                ch.link(V.tensor_tensor(a2, c16, spread(ec[:, :, :], 3, G16), ALU.mult))
                ch.link(V.tensor_tensor(AG[:, :, :], AG[:, :, :], A2[:, :, :], ALU.add))
                ch.link(V.tensor_tensor(a2, NR[:, :, 0:16].rearrange("p t (h e) -> p t h e", h=GH), spread(er[:, :, :], 3, G16), ALU.mult))
                ch.link(V.tensor_tensor(AG[:, :, :], AG[:, :, :], A2[:, :, :], ALU.add))
                ch.link(V.tensor_tensor(ag, ag, spread(ss[:, :, :], 3, G16), ALU.mult))
                ch.link(V.tensor_tensor(AG[:, :, :], AG[:, :, :], spread(RO("bgat"), 1, [P, NT, 16]), ALU.add))
                m, v = mean[:, 0:NT], var[:, 0:NT]
                ch.link(V.reduce_sum(m, AG[:, :, :], AX.X))
                ch.link(V.tensor_scalar(m, m, -1.0 / 16, None, ALU.mult))
                ch.link(V.tensor_tensor(AG[:, :, :], AG[:, :, :], spread(m, 2, [P, NT, 16]), ALU.add))
                ch.link(V.tensor_tensor(A2[:, :, :], AG[:, :, :], AG[:, :, :], ALU.mult))
                ch.link(V.reduce_sum(v, A2[:, :, :], AX.X))
                n_ln[0] += 1
                V.tensor_scalar(v, v, 1.0 / 16, EPS, ALU.mult, ALU.add).then_inc(s_ln, 1)
                e.wait_ge(s_std, n_ln[0])
                ch.link(V.reciprocal(v, v))
                ch.link(V.tensor_tensor(AG[:, :, :], AG[:, :, :], spread(v, 2, [P, NT, 16]), ALU.mult))
                ch.link(V.tensor_tensor(AG[:, :, :], AG[:, :, :], spread(RO("lng"), 1, [P, NT, 16]), ALU.mult))
                ch.link(V.tensor_tensor(AG[:, :, :], AG[:, :, :], spread(RO("lnb"), 1, [P, NT, 16]), ALU.add))
                sc = sm4[3][:, :, :]
                ch.link(V.reduce_sum(sc, AG[:, :, :].rearrange("p t (h e) -> p t e h", h=GH), AX.X))
                ch.link(V.tensor_scalar(sc, sc, 1.0 / GH, None, ALU.mult))
                gating(e, ch, sc, GE, CS("lowa"), s_x, s_e, 4)
                for i in range(GE):
                    ch.link(V.tensor_tensor(s3, Y[i], sc[:, :, i:i + 1].to_broadcast(PT), ALU.mult))
                    ch.link(V.tensor_tensor(Ht[:, :], Ht[:, :], St[:, :], ALU.add))
                layernorm(e, ch, h3, z3, NT, D)
                layernorm(e, ch, z3, z3, NT, D)
                ch.link(V.tensor_tensor(z3, z3, spread(RO("g1"), 1, PT), ALU.mult))
                V.tensor_tensor(z3, z3, spread(RO("be1"), 1, PT), ALU.add).then_inc(s_z, 1)

        base = 0

        def take(n):
            nonlocal base
            base += n
            return R[:, base - n:base]
        QU = [take(512)[0:D, :] for _ in (0, 1)]
        QV = [take(512)[0:D, :] for _ in (0, 1)]
        KB = [take(2048)[0:D, :].rearrange("p (i h s) -> p i h s", i=8, h=H1) for _ in (0, 1)]
        VB = [take(512).rearrange("p (i d) -> p i d", i=8) for _ in (0, 1)]
        RB = [take(4 * H1 * NREL).rearrange("p (t x) -> p t x", t=4) for _ in (0, 1)]
        PO = [take(1024) for _ in (0, 1)]
        SC = [take(1024) for _ in (0, 1)]
        AT = [take(1024) for _ in (0, 1)]
        CT = [take(512)[0:D + 1, :] for _ in (0, 1)]
        b2s = sb("b2_parts", [3 * E1, 3, D], BF16)
        mx, sm_ = sb("row_max", [P, 16]), sb("row_sum", [P, 16])
        RPB = (1536, 512)
        assert base <= 20480
        with ExitStack() as c7, nc.Block() as block:
            def sm(n):
                return c7.enter_context(nc.semaphore(n))
            names = ["s_q", "s_k", "s_vp", "s_rp", "s_proj", "s_kb", "s_vb", "s_rb", "s_ex", "s_scp", "s_sx", "s_se", "s_at", "s_atp",
                     "s_atc", "s_cp", "s_ct", "s_op", "s_h7", "s_v7", "s_one", "s_split"]
            S = {n: sm(n) for n in names}
            s_pos = [sm("s_pos0"), sm("s_pos1")]
            s_rbo = [sm("s_rbo0"), sm("s_rbo1")]

            @block.gpsimd
            def _(e):
                ch = Chain(e, S["s_split"])
                G = nc.gpsimd
                ch.link(G.tensor_copy(wup3[:, 0, :], wup[:, :]))
                ch.link(G.tensor_tensor(wup[:, :], wup[:, :], wup3[:, 0, :], ALU.subtract))
                ch.link(G.tensor_copy(wup3[:, 1, :], wup[:, :]))
                ch.link(G.tensor_tensor(wup[:, :], wup[:, :], wup3[:, 1, :], ALU.subtract))
                ch.link(G.tensor_copy(wup3[0:D, 2, :], wup[0:D, :]))
                ch.link(G.tensor_copy(wup3[D:P, 2, :], wup3[D:P, 0, :]))
                b2 = W65("b2b", 3 * E1)
                for k in range(3):
                    ch.link(G.tensor_copy(b2s[:, k, :], b2))
                    if k < 2:
                        ch.link(G.tensor_tensor(b2, b2, b2s[:, k, :], ALU.subtract))

            @block.tensor
            def _(e):
                T = nc.tensor

                def project(g):
                    cols = slice(g * 512, (g + 1) * 512)
                    if g:
                        e.wait_ge(S["s_proj"], 2 * g)
                        e.wait_ge(S["s_kb"], H1 * g)
                        e.wait_ge(S["s_rb"], 4 * g)
                        e.wait_ge(S["s_vb"], g)
                    T.matmul(PS[0:D, 0:512], W65("Wq"), ZT[:, cols], start=True, stop=True).then_inc(S["s_q"], 1)
                    T.matmul(PS[0:D, 512:1024], W65("Wk"), ZT[:, cols], start=True, stop=True).then_inc(S["s_k"], 1)
                    for i in range(8):
                        for r in (0, 64):
                            ins = T.matmul(PS[r:r + 64, 1024 + i * D:1024 + (i + 1) * D],
                                           ZT[:, g * 512 + i * 64:g * 512 + (i + 1) * 64], W65("Wv"), start=True, stop=True)
                    ins.then_inc(S["s_vp"], 1)
                    e.wait_ge(S["s_proj"], 2 * g + 2)
                    for j in range(4):
                        n = 4 * g + j
                        if n >= 2:
                            e.wait_ge(S["s_rb"], n - 1)
                        if j == 1:
                            e.wait_ge(S["s_kb"], H1 * (g + 1))
                        T.matmul(PS[:, RPB[j % 2]:RPB[j % 2] + H1 * NREL], QV[g % 2][:, j * P:(j + 1) * P],
                                 PB[:, :, :].rearrange("p h r -> p (h r)"), start=True, stop=True).then_inc(S["s_rp"], 1)

                def score(g):
                    b = g % 2
                    e.wait_ge(S["s_kb"], H1 * (g + 1))
                    if g:
                        e.wait_ge(S["s_sx"], 4 * g)
                    for i in range(8):
                        o = PS[64 * (i % 2):64 * (i % 2) + 64, 2048 + (i // 2) * 256:2048 + (i // 2 + 1) * 256]
                        ins = T.matmul(o, QU[b][:, i * 64:(i + 1) * 64], KB[b][:, i, :, :].rearrange("p h s -> p (h s)"), start=True, stop=True)
                        if i % 4 == 3:
                            ins.then_inc(S["s_scp"], 1)

                def attend(g):
                    b = g % 2
                    e.wait_ge(S["s_at"], g + 1)
                    if g:
                        e.wait_ge(S["s_op"], g)
                        e.wait_ge(S["s_h7"], g)
                    for t in range(8):
                        o = PS[:, 3072 + t * P:3072 + (t + 1) * P]
                        ins = T.transpose(o, SC[b][:, t * P:(t + 1) * P], ident)
                        if t % 4 == 3:
                            ins.then_inc(S["s_atp"], 1)
                    e.wait_ge(S["s_atc"], 2 * g + 2)
                    e.wait_ge(S["s_vb"], g + 1)
                    for i in range(8):
                        for hp in range(2):
                            at = AT[b][:, ((i // 2) * 2 + hp) * P + (i % 2) * 64:((i // 2) * 2 + hp) * P + (i % 2) * 64 + 64]
                            ins = T.matmul(PS[hp * 32:(hp + 1) * 32, 3072 + i * 64:3072 + (i + 1) * 64], VB[b][:, i, hp * 32:(hp + 1) * 32], at,
                                           start=True, stop=True)
                    ins.then_inc(S["s_cp"], 1)
                    e.wait_ge(S["s_ct"], g + 1)
                    for j in range(4):
                        ins = T.matmul(PS[:, 3584 + j * D:3584 + (j + 1) * D], CT[b][:, j * P:(j + 1) * P], W65("Wo"), start=True, stop=True)
                    ins.then_inc(S["s_op"], 1)
                e.wait_ge(S["s_one"], 2)
                project(0)
                score(0)
                for g in range(8):
                    if g < 7:
                        project(g + 1)
                        score(g + 1)
                    attend(g)

            @block.scalar
            def _(e):
                A = nc.scalar

                def project(g):
                    b = g % 2
                    if g >= 2:
                        e.wait_ge(S["s_scp"], 2 * (g - 1))
                    e.wait_ge(S["s_q"], g + 1)
                    if g >= 2:
                        e.wait_ge(S["s_rp"], 4 * (g - 1))
                    u = w65s[0:D, C65["u"][0]:C65["u"][1]]
                    v = w65s[0:D, C65["v"][0]:C65["v"][1]]
                    A.activation(QU[b], PS[0:D, 0:512], ACT.Identity, bias=u).then_inc(S["s_proj"], 1)
                    A.activation(QV[b], PS[0:D, 0:512], ACT.Identity, bias=v).then_inc(S["s_proj"], 1)
                    e.wait_ge(S["s_k"], g + 1)
                    for h in range(H1):
                        hc = consts[0:D, CCST["hcol"][0] + h:CCST["hcol"][0] + h + 1]
                        A.mul(KB[b][:, :, h, :], PS[0:D, 512:1024].rearrange("p (i s) -> p i s", i=8), hc).then_inc(S["s_kb"], 1)
                    for j in range(4):
                        n = 4 * g + j
                        e.wait_ge(S["s_rp"], n + 1)
                        if g >= 2:
                            e.wait_ge(s_rbo[b], 64 * (g // 2))
                        A.copy(RB[b][:, j, :], PS[:, RPB[j % 2]:RPB[j % 2] + H1 * NREL]).then_inc(S["s_rb"], 1)

                def exps(g):
                    e.wait_ge(S["s_se"], g + 1)
                    A.activation(SC[g % 2], SC[g % 2], ACT.Exp, scale=HD1 ** -0.5).then_inc(S["s_ex"], 1)

                def attend(g):
                    b = g % 2
                    for i in (0, 1):
                        e.wait_ge(S["s_atp"], 2 * g + i + 1)
                        if g >= 2:
                            e.wait_ge(S["s_cp"], g - 1)
                        A.copy(AT[b][:, i * 512:(i + 1) * 512], PS[:, 3072 + i * 512:3072 + (i + 1) * 512]).then_inc(S["s_atc"], 1)
                    e.wait_ge(S["s_cp"], g + 1)
                    if g >= 2:
                        e.wait_ge(S["s_op"], g - 1)
                    A.copy(CT[b][0:D, :], PS[0:D, 3072:3584]).then_inc(S["s_ct"], 1)
                project(0)
                for g in range(8):
                    if g < 7:
                        project(g + 1)
                    if g == 0:
                        exps(0)
                    attend(g)
                    if g < 7:
                        exps(g + 1)

            @block.sync
            def _(e):
                for g in range(8):
                    b = g % 2
                    for j in range(4):
                        n = 4 * g + j
                        e.wait_ge(S["s_rb"], n + 1)
                        e.dma_start(skew_d[n * P * H1 * NREL:(n + 1) * P * H1 * NREL].rearrange("(p x) -> p x", p=P), RB[b][:, j, :]).then_inc(s_rbo[b], 16)
                    e.wait_ge(s_rbo[b], 64 * (g // 2 + 1))
                    if g >= 2:
                        e.wait_ge(S["s_sx"], 4 * (g - 1))
                    for i in range(8):
                        tok0 = g * 512 + i * 64
                        src = bass.AP(tensor=skew_d.tensor, offset=tok0 * H1 * NREL + NTOK - 1,
                                      ap=[[H1 * NREL - 1, 64], [NREL, H1], [1, 64]])
                        dst = PO[b][64 * (i % 2):64 * (i % 2) + 64, (i // 2) * 256:(i // 2 + 1) * 256].rearrange("p (h s) -> p h s", h=H1)
                        e.dma_start(dst, src).then_inc(s_pos[b], 16)

            @block.vector
            def _(e):
                ch = Chain(e, S["s_v7"])
                V = nc.vector
                for b in (0, 1):
                    V.memset(CT[b][D:D + 1, :], 1.0).then_inc(S["s_one"], 1)

                def values(g):
                    e.wait_ge(S["s_vp"], g + 1)
                    if g >= 2:
                        e.wait_ge(S["s_cp"], g - 1)
                    V.tensor_tensor(VB[g % 2], PS[:, 1024:1536].rearrange("p (i d) -> p i d", i=8),
                                    spread(CS("vmask"), 1, [P, 8, D]), ALU.mult).then_inc(S["s_vb"], 1)

                def soften(g):
                    b = g % 2
                    sc3 = SC[b].rearrange("p (r s) -> p r s", s=64)
                    R3 = [P, 16, 64]
                    e.wait_ge(s_pos[b], 128 * (g // 2 + 1))
                    e.wait_ge(S["s_scp"], 2 * g + 2)
                    if g >= 2:
                        e.wait_ge(S["s_atp"], 2 * (g - 1))
                    for i in (0, 1):
                        V.tensor_tensor(SC[b][:, i * 512:(i + 1) * 512], PS[:, 2048 + i * 512:2048 + (i + 1) * 512],
                                        PO[b][:, i * 512:(i + 1) * 512], ALU.add).then_inc(S["s_sx"], 2)
                    e.wait_ge(S["s_sx"], 4 * g + 4)
                    ch.link(V.reduce_max(mx[:, :], sc3, AX.X))
                    V.tensor_tensor(sc3, sc3, spread(mx[:, :], 2, R3), ALU.subtract).then_inc(S["s_se"], 1)
                    e.wait_ge(S["s_ex"], g + 1)
                    ch.link(V.reduce_sum(sm_[:, :], sc3, AX.X))
                    ch.link(V.reciprocal(sm_[:, :], sm_[:, :]))
                    V.tensor_tensor(sc3, sc3, spread(sm_[:, :], 2, R3), ALU.mult).then_inc(S["s_at"], 1)

                def add(g):
                    e.wait_ge(S["s_op"], g + 1)
                    V.tensor_tensor(h3[:, 4 * g:4 * g + 4, :], h3[:, 4 * g:4 * g + 4, :],
                                    PS[:, 3584:3584 + 256].rearrange("p (t d) -> p t d", d=D), ALU.add).then_inc(S["s_h7"], 1)
                    e.wait_ge(S["s_h7"], g + 1)
                    ts = slice(4 * g, 4 * g + 4)
                    m, v = mean[:, ts], var[:, ts]
                    ch.link(V.reduce_sum(m, h3[:, ts, :], AX.X))
                    ch.link(V.tensor_scalar(m, m, -1.0 / D, None, ALU.mult))
                    ch.link(V.tensor_tensor(c3[:, ts, :], h3[:, ts, :], spread(m, 2, [P, 4, D]), ALU.add))
                    ch.link(V.tensor_tensor(s3[:, ts, :], c3[:, ts, :], c3[:, ts, :], ALU.mult))
                    ch.link(V.reduce_sum(v, s3[:, ts, :], AX.X))
                    ch.link(V.tensor_scalar(v, v, 1.0 / D, EPS, ALU.mult, ALU.add))
                values(0)
                soften(0)
                for g in range(8):
                    if g < 7:
                        values(g + 1)
                        soften(g + 1)
                    add(g)

        zA = zt_mem[:, 0:M // 2].bitcast(BF16)
        zB = zt_mem[:, M // 2:M].bitcast(BF16)
        z12 = R[:, 0:2048].bitcast(BF16).rearrange("p (t k) -> p t k", k=2 * D)
        z13 = R[:, 2048:4096].bitcast(BF16).rearrange("p (t k) -> p t k", k=2 * D)
        NB8 = 4
        hb = [R[:, 8192 + i * 512:8192 + (i + 1) * 512] for i in range(NB8)]
        hs = [R[:, 10240 + i * 512:10240 + (i + 1) * 512] for i in range(NB8)]
        yT = [R[:, 12288 + i * 512:12288 + (i + 1) * 512] for i in range(2)]
        g3 = R[:, 17408:17408 + NT * 3 * E1 // 2].bitcast(BF16).rearrange("p (t c e) -> p t c e", c=3, e=E1)
        g3T = R[0:3 * E1, 17792:17792 + 2048].bitcast(BF16)
        pick = R[0:3 * E1, 19840:19840 + E1 * P // 2].bitcast(BF16).rearrange("p (e m) -> p e m", e=E1)
        rest = [Zt[:, 0:256].rearrange("p (t e) -> p t e", e=E1), Zt[:, 256:512].rearrange("p (t e) -> p t e", e=E1)]
        identb = hid[0][:, 0:64].bitcast(BF16)
        oa = c3
        PSB = PS[:, :].bitcast(BF16)
        with ExitStack() as c8, nc.Block() as block:
            def sm(n):
                return c8.enter_context(nc.semaphore(n))
            s_v, s_z, s_bank, s_zT, s_x, s_e, s_lg, s_g3, s_gt, s_gtc, s_g3t, s_hp, s_hs, s_wb, s_sc, s_dn, s_yp, s_yc, s_op, s_fin, s_out = (
                sm("s_v8"), sm("s_z8"), sm("s_bank8"), sm("s_zT8"), sm("s_x8"), sm("s_e8"), sm("s_lg"), sm("s_g3"), sm("s_gt"),
                sm("s_gtc"), sm("s_g3t"), sm("s_hp8"), sm("s_hs8"), sm("s_wb"), sm("s_sc8"), sm("s_dn"), sm("s_yp8"), sm("s_yc"),
                sm("s_op8"), sm("s_fin"), sm("s_out"))
            s_z1, s_z1b, s_zB = sm("s_z1"), sm("s_z1b"), sm("s_zB")
            s_gtv = sm("s_gtv")
            seq = [(g, x_) for g in range(8) for x_ in range(E1)]
            NS = len(seq)

            @block.tensor
            def _(e):
                T = nc.tensor
                passes = ((zA, 0), (zA, 1), (zB, 2))
                for st in (0, 1):
                    e.wait_ge(s_z, st + 1)
                    if st:
                        e.wait_ge(s_z1b, 1)
                    for t in range(NT):
                        ins = T.transpose(PSB[:, st * M + t * P:st * M + (t + 1) * P], (z12, z13)[st][:, t, :], identb)
                        if t % 8 == 7:
                            ins.then_inc(s_bank, 1)
                e.wait_ge(s_zT, 4)
                e.wait_ge(s_zB, 4)
                for t in range(NT):
                    for k, (zs, part) in enumerate(passes):
                        ins = T.matmul(PS[:, 3584 + t * E1:3584 + (t + 1) * E1], zs[:, t * P:(t + 1) * P], wup3[:, part, 0:E1],
                                       start=(k == 0), stop=(k == 2))
                ins.then_inc(s_lg, 1)
                w2 = W128("W2b").rearrange("p (e c d) -> p e c d", e=E1, c=FC1)

                def up(n):
                    g, x_ = seq[n]
                    for c in range(FC1):
                        q = 2 * n + c
                        if q >= 4:
                            e.wait_ge(s_hs, q - 3)
                        f = E1 + x_ * F1 + c * P
                        for k, (zs, part) in enumerate(passes):
                            ins = T.matmul(bank(q % 4), wup3[:, part, f:f + P], zs[:, g * 512:(g + 1) * 512], start=(k == 0), stop=(k == 2))
                        ins.then_inc(s_hp, 1)

                def spread_gate(n):
                    g, x_ = seq[n]
                    if n >= 2:
                        e.wait_ge(s_sc, 2 * n - 2)
                    T.matmul(bank(4 + n % 2), pick[:, x_, :], g3T[:, g * 512:(g + 1) * 512], start=True, stop=True).then_inc(s_wb, 1)

                def down(n):
                    g, x_ = seq[n]
                    e.wait_ge(s_sc, 2 * n + 2)
                    if x_ == 0 and g:
                        e.wait_ge(s_yc, g)
                    for c in range(FC1):
                        ins = T.matmul(PS[c * D:(c + 1) * D, 3072:3584], w2[:, x_, c, :], hs[(2 * n + c) % NB8], start=(x_ == 0),
                                       stop=(x_ == E1 - 1 and c == 1))
                    ins.then_inc(s_dn, 1)
                    if x_ == E1 - 1:
                        for k in range(3):
                            ins = T.matmul(PS[0:D, 3072:3584], b2s[:, k, :], g3T[:, g * 512:(g + 1) * 512], start=False, stop=(k == 2))
                        ins.then_inc(s_yp, 1)

                def finish(g):
                    e.wait_ge(s_yc, g + 1)
                    if g:
                        e.wait_ge(s_fin, g)
                    for j in range(4):
                        ins = T.matmul(PS[:, 3584 + j * D:3584 + (j + 1) * D], yT[g % 2][:, j * P:(j + 1) * P], CS("fold"), start=True, stop=True)
                    ins.then_inc(s_op, 1)
                up(0)
                up(1)
                e.wait_ge(s_g3, 2)
                for q in range(4):
                    if q == 2:
                        e.wait_ge(s_gtc, 1)
                    if q == 3:
                        e.wait_ge(s_gtv, 1)
                    for t in range(8):
                        ins = T.transpose(PSB[0:3 * E1, 4096 + (q % 2) * 1024 + t * P:4096 + (q % 2) * 1024 + (t + 1) * P],
                                          g3[:, 8 * q + t, :, :].rearrange("p c e -> p (c e)"), identb)
                    ins.then_inc(s_gt, 1)
                e.wait_ge(s_gtc, 2)
                e.wait_ge(s_gtv, 2)
                spread_gate(0)
                for n in range(NS):
                    if n >= 1 and n + 1 < NS:
                        up(n + 1)
                    if n + 1 < NS:
                        spread_gate(n + 1)
                    down(n)
                    if seq[n][1] == 1 and seq[n][0]:
                        finish(seq[n][0] - 1)
                finish(7)

            @block.scalar
            def _(e):
                A = nc.scalar
                root(e, NT)
                e.wait_ge(s_z1, 1)
                A.copy(z13[:, :, 0:D], z12[:, :, 0:D]).then_inc(s_z1b, 1)
                for b in range(4):
                    e.wait_ge(s_bank, b + 1)
                    A.copy(zA[:, b * 1024:(b + 1) * 1024], PSB[:, b * 1024:(b + 1) * 1024]).then_inc(s_zT, 1)
                e.wait_ge(s_x, 1)
                A.activation(gates[:, :, :], gates[:, :, :], ACT.Exp).then_inc(s_e, 1)

                def gelu(n):
                    for c in range(FC1):
                        q = 2 * n + c
                        e.wait_ge(s_hp, q + 1)
                        if q >= NB8:
                            e.wait_ge(s_sc, q - NB8 + 1)
                        b1 = w128s[:, C128["b1b"][0] + FC1 * seq[n][1] + c:C128["b1b"][0] + FC1 * seq[n][1] + c + 1]
                        A.activation(hb[q % NB8], bank(q % 4), ACT.Gelu, bias=b1).then_inc(s_hs, 1)
                gelu(0)
                gelu(1)
                for q in (0, 2):
                    e.wait_ge(s_gt, q + 1)
                    A.copy(g3T[:, q * 1024:(q + 1) * 1024], PSB[0:3 * E1, 4096:5120]).then_inc(s_gtc, 1)
                for n in range(2, NS):
                    gelu(n)
                    g, x_ = seq[n]
                    if x_ == 0 and g:
                        e.wait_ge(s_yp, g)
                        if g >= 3:
                            e.wait_ge(s_op, g - 2)
                        A.copy(yT[(g - 1) % 2], bank(6)).then_inc(s_yc, 1)
                e.wait_ge(s_yp, 8)
                e.wait_ge(s_op, 6)
                A.copy(yT[1], bank(6)).then_inc(s_yc, 1)

            @block.vector
            def _(e):
                ch = Chain(e, s_v)
                V = nc.vector
                n_ln[0] += 1
                V.tensor_copy(identb, ident).then_inc(s_ln, 1)
                e.wait_ge(s_std, n_ln[0])
                ch.link(V.reciprocal(var[:, 0:NT], var[:, 0:NT]))
                ch.link(V.tensor_tensor(z3, c3, spread(var[:, 0:NT], 2, PT), ALU.mult))
                V.tensor_copy(z12[:, :, 0:D], z3).then_inc(s_z1, 1)
                e.wait_ge(s_z1, 1)
                ch.link(V.tensor_tensor(z3, z3, z12[:, :, 0:D], ALU.subtract))
                V.tensor_copy(z12[:, :, D:2 * D], z3).then_inc(s_z, 1)
                e.wait_ge(s_z, 1)
                V.tensor_tensor(z13[:, :, D:2 * D], z3, z12[:, :, D:2 * D], ALU.subtract).then_inc(s_z, 1)
                for b in range(4):
                    e.wait_ge(s_bank, 4 + b + 1)
                    V.tensor_copy(zB[:, b * 1024:(b + 1) * 1024], PSB[:, M + b * 1024:M + (b + 1) * 1024]).then_inc(s_zB, 1)
                V.tensor_copy(pick, spread(CS("pick", 3 * E1), 2, [3 * E1, E1, P])).then_inc(s_g3, 1)
                e.wait_ge(s_lg, 1)
                ch.link(V.tensor_tensor(gates[:, :, :], PS[:, 3584:3584 + NT * E1].rearrange("p (t e) -> p t e", e=E1),
                                        spread(RO("bg"), 1, [P, NT, E1]), ALU.add))
                gating(e, ch, gates[:, :, :], E1, CS("lowb"), s_x, s_e, 1)
                ch.link(V.tensor_copy(g3[:, :, 0, :], gates[:, :, :]))
                ch.link(V.tensor_tensor(rest[0], gates[:, :, :], g3[:, :, 0, :], ALU.subtract))
                ch.link(V.tensor_copy(g3[:, :, 1, :], rest[0]))
                ch.link(V.tensor_tensor(rest[1], rest[0], g3[:, :, 1, :], ALU.subtract))
                V.tensor_copy(g3[:, :, 2, :], rest[1]).then_inc(s_g3, 1)
                for q in (1, 3):
                    e.wait_ge(s_gt, q + 1)
                    V.tensor_copy(g3T[:, q * 1024:(q + 1) * 1024], PSB[0:3 * E1, 5120:6144]).then_inc(s_gtv, 1)

                def add_out(g):
                    e.wait_ge(s_op, g + 1)
                    V.tensor_tensor(oa[:, 4 * g:4 * g + 4, :], h3[:, 4 * g:4 * g + 4, :],
                                    PS[:, 3584:3584 + 256].rearrange("p (t d) -> p t d", d=D), ALU.add).then_inc(s_fin, 1)
                for n, (g, x_) in enumerate(seq):
                    e.wait_ge(s_wb, n + 1)
                    for c in range(FC1):
                        q = 2 * n + c
                        e.wait_ge(s_hs, q + 1)
                        if q >= NB8:
                            e.wait_ge(s_dn, n - 1)
                        V.tensor_tensor(hs[q % NB8], hb[q % NB8], bank(4 + n % 2), ALU.mult).then_inc(s_sc, 1)
                    if x_ == 3 and g:
                        add_out(g - 1)
                add_out(7)

            @block.sync
            def _(e):
                for g in range(8):
                    e.wait_ge(s_fin, g + 1)
                    e.dma_start(out[g * 512:(g + 1) * 512, :].rearrange("(t p) d -> p t d", p=P), oa[:, 4 * g:4 * g + 4, :]).then_inc(s_out, 16)
                e.wait_ge(s_out, 128)


def kernel(**inputs):
    import numpy as np
    import concourse.bacc as bacc
    from concourse.bass_utils import run_bass_kernel_spmd

    a = {k: np.asarray(v) for k, v in inputs.items()}
    f = np.float32

    x = a["x"].reshape(NIMG, 3, 8, 16, 8, 16).transpose(1, 3, 5, 0, 2, 4).reshape(KC, P, M).transpose(1, 0, 2)

    def pad(m, n=D + 1):
        return np.concatenate([m, np.zeros((n - m.shape[0], m.shape[1]), f)], 0)

    def with_bias(w, b):
        return np.concatenate([w, b.reshape(1, -1)], 0)

    n = np.arange(NTOK)
    grid = np.stack([n // 8, n % 8]).astype(f) / f(7)
    grid = np.concatenate([np.concatenate([grid, np.ones((1, NTOK), f)], 0)] * 2, 1)
    rel = np.arange(61, dtype=f)[:, None] * np.exp(np.arange(0, D, 2, dtype=f) * f(-np.log(10000.0) / D))
    enc = np.stack([np.sin(rel), np.cos(rel)], -1).reshape(61, D).astype(f)
    enc = enc[np.clip(np.arange(-NTOK + 1, NTOK), -30, 30) + 30].T
    enc = np.concatenate([enc, np.ones((1, NREL), f)], 0)
    p = np.arange(P)
    heads = np.arange(D) // HD1
    c = {
        "ident": np.eye(P, dtype=f),
        "sign": np.stack([1 - 2 * ((p >> b) & 1) for b in range(7)], 1).astype(f),
        "iota": np.tile(np.arange(P, dtype=f), (P, 1)),
        "upto": np.triu(np.ones((P, P), f)),
        "kvmask": pad(np.tile((np.arange(D)[:, None] // HC0 == np.arange(D) // HC0).astype(f) / f(NTOK), (1, 2)), P),
        "hcol": pad((heads[:, None] == np.arange(H1)).astype(f), P),
        "vmask": (heads[None, :] % 2 == (p[:, None] // 64)).astype(f),
        "lowa": np.tile(np.tril(np.ones((GE, GE), f), -1).reshape(1, -1), (P, 1)),
        "lowb": np.tile(np.tril(np.ones((E1, E1), f), -1).reshape(1, -1), (P, 1)),
    }
    c["pick"] = pad((np.arange(3 * E1)[:, None] % E1 == np.arange(E1)).astype(f), P)
    c["fold"] = np.concatenate([np.eye(D, dtype=f)] * 2, 0)
    c["lane"] = p[:, None].astype(f)
    c["hi4"] = (p[:, None] // GH).astype(f)
    c["head"] = (p[:, None] % GH == np.concatenate([np.arange(16) // GE, np.arange(GH)])).astype(f)
    g = a
    w65 = {
        "pos1": pad(np.concatenate([g["L0_tok_W1"], g["L0_tok_b1"][None], np.zeros((D - 3, D), f), g["L0_tok_bp"][None]], 0)),
        "pos2": with_bias(g["L0_tok_W2"], g["L0_tok_b2"]),
        "Wgat": pad(g["L0_ffn_W_gat"]),
        "W1a": with_bias(g["L0_ffn_W1"].transpose(1, 0, 2).reshape(D, -1), g["L0_ffn_b1"]),
        "Wq": with_bias(g["L1_attn_Wq"].T, g["L1_attn_bq"]),
        "Wk": with_bias(g["L1_attn_Wk"].T, g["L1_attn_bk"]),
        "Wv": with_bias(g["L1_attn_Wv"].T, g["L1_attn_bv"]),
        "Wpos": with_bias(g["L1_attn_Wpos"].T, g["L1_attn_bpos"]),
        "Wo": with_bias(g["L1_attn_Wo"].T, g["L1_attn_bo"]),
        "u": pad(g["L1_attn_u_bias"].reshape(D, 1)),
        "v": pad(g["L1_attn_v_bias"].reshape(D, 1)),
        "enc": enc,
        "grid": pad(grid),
        "b2b": pad(np.concatenate([g["L1_ffn_b2"]] * 3, 0)),
    }
    w128 = {
        "Wp": g["L0_tok_Wp"].reshape(KC, P, D).transpose(1, 0, 2).reshape(P, -1),
        "W2a": g["L0_ffn_W2"].transpose(1, 0, 2).reshape(P, -1),
        "W2b": g["L1_ffn_W2"].reshape(E1, FC1, P, D).transpose(2, 0, 1, 3).reshape(P, -1),
        "b1b": g["L1_ffn_b1"].reshape(E1, FC1, P).transpose(2, 0, 1).reshape(P, -1),
    }
    wrow = {
        "kw": g["L0_attn_kln_weight"], "kb": g["L0_attn_kln_bias"],
        "vw": g["L0_attn_vln_weight"], "vb": g["L0_attn_vln_bias"],
        "asrc": g["L0_ffn_att_src"], "adst": g["L0_ffn_att_dst"], "bgat": g["L0_ffn_b_gat"],
        "lng": g["L0_ffn_ln_gamma"], "lnb": g["L0_ffn_ln_beta"], "g1": g["L1_attn_ln_gamma"], "be1": g["L1_attn_ln_beta"],
        "b2a": g["L0_ffn_b2"], "bg": g["L1_ffn_bg"],
    }

    def packed(parts, widths):
        for k, w in widths.items():
            assert parts[k].shape[1] == w, (k, parts[k].shape, w)
        return np.ascontiguousarray(np.concatenate([parts[k] for k in widths], 1))
    arrays = {
        "pixels": np.ascontiguousarray(x),
        "edge_list": np.ascontiguousarray(a["L0_ffn_edge_index"]),
        "w128": packed(w128, PK128), "w65": packed(w65, PK65),
        "wrow": packed({k: v.reshape(1, -1) for k, v in wrow.items()}, PROW),
        "w_up_1": np.ascontiguousarray(np.concatenate([g["L1_ffn_Wg"], g["L1_ffn_W1"].transpose(1, 0, 2).reshape(D, -1)], 1)),
        "consts": packed(c, CST),
    }
    nc = bacc.Bacc("TRN2", target_bir_lowering=False, num_devices=1)
    args = [nc.dram_tensor(k, v.shape, mybir.dt.from_np(v.dtype), kind="ExternalInput").ap() for k, v in arrays.items()]
    out = nc.dram_tensor("out", (M, D), F32, kind="ExternalOutput").ap()
    vit_tower(nc, *args, out)
    r = run_bass_kernel_spmd(nc, [arrays], core_ids=[0])
    return r.results[0]["out"].reshape(NIMG, NTOK, D)
```
